# Optimizing a Trainium2 kernel written in Bass

```python
import numpy as np
import jax
import jax.numpy as jnp

def _softmax(x, axis=-1):
    return jax.nn.softmax(x, axis=axis)

def _gelu(x):
    return jax.nn.gelu(x, approximate=True)

def _silu(x):
    return jax.nn.silu(x)

def _sigmoid(x):
    return jax.nn.sigmoid(x)

def _layernorm(x, axis=-1, eps=1e-05):
    m = jnp.mean(x, axis=axis, keepdims=True)
    v = jnp.var(x, axis=axis, keepdims=True)
    return (x - m) / jnp.sqrt(v + eps)

def _scatter_add(tgt, idx, src, axis=0):
    return tgt.at[idx].add(src)

def _segment_sum(src, seg, n):
    return jax.ops.segment_sum(src, seg, n)
kernel_name = 'mk_sandwich_d1_jaxref_r8_6e29a8'

def setup_inputs(seed: int=0):
    np.random.seed(seed)
    _w = jnp.asarray

    def _L0_attn_setup():
        import jax, jax.numpy as jnp
        import numpy as np
        D_MODEL, D_STATE, D_CONV, EXPAND = (128, 16, 4, 2)
        D_INNER = EXPAND * D_MODEL
        BATCH, SEQ = (2, 256)

        def _depthwise_causal_conv(x, w, b):
            K = w.shape[1]
            L = x.shape[1]
            xp = jnp.pad(x, ((0, 0), (K - 1, 0), (0, 0)))
            out = b
            for k in range(K):
                out = out + xp[:, k:k + L, :] * w[:, k]
            return out

        def _selective_scan(x, delta, Bm, Cm, A, Dv):

            def step(state, inp):
                x_t, d_t, B_t, C_t = inp
                decay = jnp.exp(d_t[..., None] * A)
                state = decay * state + B_t[:, None, :] * x_t[..., None]
                y_t = jnp.einsum('bds,bs->bd', state, C_t) + x_t * Dv
                return (state, y_t)
            init = jnp.zeros((x.shape[0], x.shape[2], A.shape[1]), x.dtype)
            xs = tuple((jnp.swapaxes(a, 0, 1) for a in (x, delta, Bm, Cm)))
            _, ys = jax.lax.scan(step, init, xs)
            return jnp.swapaxes(ys, 0, 1)
        key = jax.random.key(seed)
        ks = jax.random.split(key, 10)
        s = lambda fan_in: 1.0 / np.sqrt(fan_in)
        return {'x': jax.random.normal(ks[0], (BATCH, SEQ, D_MODEL), jnp.float32), 'W_in': jax.random.normal(ks[1], (2 * D_INNER, D_MODEL), jnp.float32) * s(D_MODEL), 'w_conv': jax.random.normal(ks[2], (D_INNER, D_CONV), jnp.float32) * s(D_CONV), 'b_conv': jax.random.normal(ks[3], (D_INNER,), jnp.float32) * 0.02, 'W_x': jax.random.normal(ks[4], (D_INNER + 2 * D_STATE, D_INNER), jnp.float32) * s(D_INNER), 'W_dt': jax.random.normal(ks[5], (D_INNER, D_INNER), jnp.float32) * s(D_INNER), 'b_dt': jax.random.normal(ks[6], (D_INNER,), jnp.float32) * 0.02, 'A_log': jnp.log(jax.random.uniform(ks[7], (D_INNER, D_STATE), jnp.float32, 0.0001, 1.0)), 'D': jnp.ones((D_INNER,), jnp.float32), 'W_out': jax.random.normal(ks[8], (D_MODEL, D_INNER), jnp.float32) * s(D_INNER)}
    _L0_attn_in = _L0_attn_setup()

    def _L0_ffn_setup():
        import jax, jax.numpy as jnp
        import numpy as np
        TOPK = 4
        key = jax.random.key(seed)
        ks = jax.random.split(key, 9)
        B, T, D = (4, 256, 128)
        E, H = (32, 128)
        HS = H * TOPK
        s = lambda k, shape, fan: jax.random.normal(k, shape, dtype=jnp.float32) / np.sqrt(fan)
        return {'x': jax.random.normal(ks[0], (B, T, D), dtype=jnp.float32), 'router_w': s(ks[1], (E, D), D), 'router_bias': jnp.zeros((E,), dtype=jnp.float32), 'gate_w': s(ks[2], (E, H, D), D), 'up_w': s(ks[3], (E, H, D), D), 'down_w': s(ks[4], (E, D, H), H), 'sgate_w': s(ks[5], (HS, D), D), 'sup_w': s(ks[6], (HS, D), D), 'sdown_w': s(ks[7], (D, HS), HS)}
    _L0_ffn_in = _L0_ffn_setup()
    _d = {'L0_attn_x': _L0_attn_in['x'], 'L0_attn_W_in': _L0_attn_in['W_in'], 'L0_attn_w_conv': _L0_attn_in['w_conv'], 'L0_attn_b_conv': _L0_attn_in['b_conv'], 'L0_attn_W_x': _L0_attn_in['W_x'], 'L0_attn_W_dt': _L0_attn_in['W_dt'], 'L0_attn_b_dt': _L0_attn_in['b_dt'], 'L0_attn_A_log': _L0_attn_in['A_log'], 'L0_attn_D': _L0_attn_in['D'], 'L0_attn_W_out': _L0_attn_in['W_out'], 'L0_ffn_router_w': _L0_ffn_in['router_w'], 'L0_ffn_router_bias': _L0_ffn_in['router_bias'], 'L0_ffn_gate_w': _L0_ffn_in['gate_w'], 'L0_ffn_up_w': _L0_ffn_in['up_w'], 'L0_ffn_down_w': _L0_ffn_in['down_w'], 'L0_ffn_sgate_w': _L0_ffn_in['sgate_w'], 'L0_ffn_sup_w': _L0_ffn_in['sup_w'], 'L0_ffn_sdown_w': _L0_ffn_in['sdown_w']}
    _x0 = _d['L0_attn_x']
    _d['L0_attn_x'] = jax.random.normal(jax.random.fold_in(jax.random.key(seed), 1), (32, 256, 128), dtype=_x0.dtype)
    del _x0
    return _d

def reference(L0_attn_x, L0_attn_W_in, L0_attn_w_conv, L0_attn_b_conv, L0_attn_W_x, L0_attn_W_dt, L0_attn_b_dt, L0_attn_A_log, L0_attn_D, L0_attn_W_out, L0_ffn_router_w, L0_ffn_router_bias, L0_ffn_gate_w, L0_ffn_up_w, L0_ffn_down_w, L0_ffn_sgate_w, L0_ffn_sup_w, L0_ffn_sdown_w):

    def _L0_attn_ref(x, W_in, w_conv, b_conv, W_x, W_dt, b_dt, A_log, D, W_out):
        import jax, jax.numpy as jnp
        import numpy as np
        D_MODEL, D_STATE, D_CONV, EXPAND = (128, 16, 4, 2)
        D_INNER = EXPAND * D_MODEL
        BATCH, SEQ = (2, 256)

        def _depthwise_causal_conv(x, w, b):
            K = w.shape[1]
            L = x.shape[1]
            xp = jnp.pad(x, ((0, 0), (K - 1, 0), (0, 0)))
            out = b
            for k in range(K):
                out = out + xp[:, k:k + L, :] * w[:, k]
            return out

        def _selective_scan(x, delta, Bm, Cm, A, Dv):

            def step(state, inp):
                x_t, d_t, B_t, C_t = inp
                decay = jnp.exp(d_t[..., None] * A)
                state = decay * state + B_t[:, None, :] * x_t[..., None]
                y_t = jnp.einsum('bds,bs->bd', state, C_t) + x_t * Dv
                return (state, y_t)
            init = jnp.zeros((x.shape[0], x.shape[2], A.shape[1]), x.dtype)
            xs = tuple((jnp.swapaxes(a, 0, 1) for a in (x, delta, Bm, Cm)))
            _, ys = jax.lax.scan(step, init, xs)
            return jnp.swapaxes(ys, 0, 1)
        silu = jax.nn.silu
        xz = x @ W_in.T
        x_inner, z = jnp.split(xz, 2, axis=-1)
        x_conv = silu(_depthwise_causal_conv(x_inner, w_conv, b_conv))
        x_dbl = x_conv @ W_x.T
        delta, Bm, Cm = jnp.split(x_dbl, [D_INNER, D_INNER + D_STATE], axis=-1)
        delta = jax.nn.softplus(delta @ W_dt.T + b_dt)
        A = -jnp.exp(A_log.astype(jnp.float32))
        y = _selective_scan(x_conv, delta, Bm, Cm, A, D)
        y = y * silu(z)
        return y @ W_out.T

    def _L0_ffn_ref(x, router_w, router_bias, gate_w, up_w, down_w, sgate_w, sup_w, sdown_w):
        import jax, jax.numpy as jnp
        import numpy as np
        TOPK = 4
        B, T, D = x.shape
        flat = x.reshape(B * T, D)
        logits = flat.astype(jnp.float32) @ router_w.T + router_bias
        scores = jax.nn.softmax(logits, axis=-1)
        topk_scores, topk_idx = jax.lax.top_k(scores, TOPK)
        topk_scores = topk_scores / jnp.clip(topk_scores.sum(axis=-1, keepdims=True), 1e-12, None)
        h = jax.nn.silu(jnp.einsum('nd,ehd->neh', flat, gate_w)) * jnp.einsum('nd,ehd->neh', flat, up_w)
        expert_out = jnp.einsum('neh,edh->ned', h, down_w)
        sel = jnp.take_along_axis(expert_out, topk_idx[:, :, None], axis=1)
        out = (sel * topk_scores.astype(flat.dtype)[:, :, None]).sum(axis=1)
        out = out + jax.nn.silu(flat @ sgate_w.T) * (flat @ sup_w.T) @ sdown_w.T
        return out.reshape(B, T, D)
    x = L0_attn_x
    x = x + _layernorm(_L0_attn_ref(_layernorm(x, axis=-1), L0_attn_W_in, L0_attn_w_conv, L0_attn_b_conv, L0_attn_W_x, L0_attn_W_dt, L0_attn_b_dt, L0_attn_A_log, L0_attn_D, L0_attn_W_out), axis=-1)
    x = x + _layernorm(_L0_ffn_ref(_layernorm(x, axis=-1), L0_ffn_router_w, L0_ffn_router_bias, L0_ffn_gate_w, L0_ffn_up_w, L0_ffn_down_w, L0_ffn_sgate_w, L0_ffn_sup_w, L0_ffn_sdown_w), axis=-1)
    return x

_drawn_inputs = setup_inputs


def setup_inputs(seed=0):
    import zlib

    import numpy as np

    out = dict(_drawn_inputs(seed))
    spreads = {'L0_attn_D': (1.0, 0.2), 'L0_ffn_router_bias': (0.0, 0.1)}
    factors = {'L0_attn_b_dt': 3.492}
    for name, (base, spread) in spreads.items():
        noise = np.random.default_rng([zlib.crc32(name.encode()), seed]).standard_normal(out[name].shape)
        drawn = base * np.exp(spread * noise) if base else spread * noise
        out[name] = jnp.asarray(drawn.astype(out[name].dtype))
    for name, factor in factors.items():
        out[name] = (out[name] * factor).astype(out[name].dtype)
    return out
```

```python
import numpy as np
import concourse.bass as bass
from concourse import mybir
from contextlib import ExitStack

F32 = mybir.dt.float32
BF16 = mybir.dt.bfloat16
U32 = mybir.dt.uint32
I32 = mybir.dt.int32
ALU = mybir.AluOpType
ACT = mybir.ActivationFunctionType
AX = mybir.AxisListType

P = 128
BATCH, SEQ = 32, 256
DM = 128
DI = 256
NS = 16
KC = 4
NH = DI // P
TOK = BATCH * SEQ
UB = 2
UT = UB * SEQ
UNITS = TOK // UT
TPU = UT // P
TILES = TOK // P
SG = 4
NSG = NS // SG
NCH = NSG * NH
NE, TOPK = 32, 4
HS = P * TOPK
HST = HS // P
SLOT_TILES = TOK * TOPK // P + NE
SLOTS = SLOT_TILES * P
GT = 4
GROUPS = SLOT_TILES // GT
EPS = 1e-5
EXP_LN = "natural_log_exp_and_others"
A_RING, H_RING = 2, 4
ARENA_COLS = (A_RING + H_RING + 4) * SG * UT
POOL_CMUL = (3, 7)


def at(u, n):
    return isinstance(u, int) and u == n


def pause(eng, scratch, place):
    eng.tensor_tensor(scratch[:, place:place + 1], scratch[:, 0:1], scratch[:, 0:1], ALU.mult)


def mamba_moe_kernel(nc, x, W_inT, w_convT, b_conv, W_x, W_xT, W_dtT, b_dt, A_log, Dv, W_outT,
                     routerT, router_bias, gate_upT, downT, sgateT, supT, sdownT,
                     sel, ident, upper, out):
    xs_dram = nc.dram_tensor("xs_scratch", (SLOTS, DM), F32, kind="Internal").ap()
    ys_dram = nc.dram_tensor("ys_scratch", (SLOTS, DM), F32, kind="Internal").ap()
    xn2_dram = nc.dram_tensor("xn2_scratch", (TOK, DM), F32, kind="Internal").ap()
    xn2T_dram = nc.dram_tensor("xn2T_scratch", (UNITS * P, UT), F32, kind="Internal").ap()

    def unit_rows(dram, u):
        return dram[bass.ds(u * UT, UT), :].rearrange("(j p) d -> p j d", p=P)

    with ExitStack() as ctx:
        def sb(name, shape, dt=F32):
            return ctx.enter_context(nc.sbuf_tensor(name, shape, dt))

        def sem(name):
            return ctx.enter_context(nc.semaphore(name))

        X2 = sb("X2", [P, TILES, DM])
        LG = sb("LG", [P, TILES, NE])
        V8 = sb("V8", [P, TILES, 8])
        I8 = sb("I8", [P, TILES, 8], U32)
        IDX = sb("IDX", [P, TILES * TOPK], U32)
        WT = sb("WT", [P, TILES, TOPK])

        idf = sb("idf", [P, P])
        eps = sb("eps", [P, 1])
        s_eps = sem("s_eps")
        scratch = sb("scratch", [P, 16])
        ARENA = sb("ARENA", [P, ARENA_COLS])

        with ExitStack() as m:
            def msb(name, shape, dt=F32):
                return m.enter_context(nc.sbuf_tensor(name, shape, dt))

            def msem(name):
                return m.enter_context(nc.semaphore(name))

            CW = SG * UT

            def ring(base, n):
                return [ARENA[:, base + i * CW:base + (i + 1) * CW].rearrange("p (s t) -> p s t", s=SG)
                        for i in range(n)]

            decay = ring(0, A_RING)
            state = ring(A_RING * CW, H_RING)
            Bbc = ring((A_RING + H_RING) * CW, 2)
            Cbc = ring((A_RING + H_RING + 2) * CW, 2)
            setup = ARENA[:, (A_RING + H_RING) * CW:(A_RING + H_RING + 4) * CW]
            self32 = setup[0:3 * 2 * NS, 0:2 * NS * P]
            o = 2 * NS * P
            winx = setup[:, o:o + DI]
            wcv = setup[:, o + DI:o + DI + KC * DI]
            o += DI + KC * DI
            wxd = setup[:, o:o + NH * DI].rearrange("p (h c) -> p h c", h=NH)
            o += NH * DI
            wdt = setup[:, o:o + NH * DI].rearrange("p (h c) -> p h c", h=NH)
            winz = msb("winz", [P, DI])
            wcomb = msb("wcomb", [P, KC, DI])
            bcv = msb("bcv", [P, NH])
            bdt = msb("bdt", [P, NH])
            wbc = msb("wbc", [P, NH, 3, 2 * NS])
            wdelta = msb("wdelta", [P, NH, DI])
            Apos = msb("Apos", [P, NH, NS])
            Aneg = msb("Aneg", [P, NH, NS])
            Dsb = msb("Dsb", [P, NH])
            wout = msb("wout", [P, NH, DM])
            wr = msb("wr", [P, NE])
            rbias = msb("rbias", [P, NE])
            selb = msb("selb", [3 * 2 * NS, 2 * NS, P], BF16)
            zrow = msb("zrow", [P, 1024])

            xst = msb("xst", [P, TPU, 6])
            xmv = msb("xmv", [P, TPU, 2])
            xln = msb("xln", [P, TPU])
            xrs = msb("xrs", [P, TPU])
            xn = msb("xn", [P, TPU, DM])
            xnT = msb("xnT", [P, UB, KC - 1 + SEQ])
            xc = msb("xc", [P, 2, NH, UT])
            sz = msb("sz", [P, 2, NH, UT])
            dl = msb("dl", [P, 2, NH, UB, SEQ])
            dtmp = msb("dtmp", [P, NH, UT])
            bcs = msb("bcs", [96, 2, UT], BF16)
            r1 = msb("r1", [96, UT])
            r2 = msb("r2", [96, UT])
            yg = msb("yg", [P, NH, UT])
            mst = msb("mst", [P, TPU, 6])
            mmv = msb("mmv", [P, TPU, 2])
            mln = msb("mln", [P, TPU])
            mrs = msb("mrs", [P, TPU])
            mo = msb("mo", [P, TPU, DM])
            nst = msb("nst", [P, TPU, 6])
            nmv = msb("nmv", [P, TPU, 2])
            nln = msb("nln", [P, TPU])
            nrs = msb("nrs", [P, TPU])
            xn2 = msb("xn2", [P, TPU, DM])
            xn2T = msb("xn2T", [P, UT])
            lgs = msb("lgs", [P, TPU, NE])
            v8s = msb("v8s", [P, TPU, 8])
            i8s = msb("i8s", [P, TPU, 8], U32)

            Y = [m.enter_context(nc.psum_tensor(f"Y{h}", [P, UT], F32)) for h in range(NH)]
            BCP = [m.enter_context(nc.psum_tensor(f"BCP{i}", [P, 2, UT], F32)) for i in range(2)]
            PJ = [m.enter_context(nc.psum_tensor(f"PJ{i}", [P, UT], F32)) for i in range(2)]

            s_w = msem("s_w")
            s_x0, s_x1, s_xr = msem("s_x0"), msem("s_x1"), msem("s_xr")
            s_set = msem("s_set")
            s_wc = msem("s_wc")
            s_wdm, s_wdc = msem("s_wdm"), msem("s_wdc")
            s_ap, s_an = msem("s_ap"), msem("s_an")
            s_zero = msem("s_zero")
            s_xst, s_xmv, s_xln, s_xrs, s_xn = (msem(n) for n in ("s_xst", "s_xmv", "s_xln", "s_xrs", "s_xn"))
            s_T, s_xnT = msem("s_T"), msem("s_xnT")
            s_pc = [msem(f"s_pc{h}") for h in range(NH)]
            s_xc = [msem(f"s_xc{h}") for h in range(NH)]
            s_pz = [msem(f"s_pz{h}") for h in range(NH)]
            s_sz = [msem(f"s_sz{h}") for h in range(NH)]
            s_pbc, s_hi, s_r1 = msem("s_pbc"), msem("s_hi"), msem("s_r1")
            s_mid, s_r2, s_bcs = msem("s_mid"), msem("s_r2"), msem("s_bcs")
            s_pd = [msem(f"s_pd{h}") for h in range(NH)]
            s_dm = [msem(f"s_dm{h}") for h in range(NH)]
            s_de = [msem(f"s_de{h}") for h in range(NH)]
            s_dn = [msem(f"s_dn{h}") for h in range(NH)]
            s_dl = [msem(f"s_dl{h}") for h in range(NH)]
            s_bp, s_bcp = msem("s_bp"), msem("s_bcp")
            s_exp, s_bx, s_scan = msem("s_exp"), msem("s_bx"), msem("s_scan")
            s_cmv, s_cmp = msem("s_cmv"), msem("s_cmp")
            s_sum = msem("s_sum")
            s_yd, s_yg, s_po = msem("s_yd"), msem("s_yg"), msem("s_po")
            s_mst, s_mmv, s_mln, s_mrs, s_mo = (msem(n) for n in ("s_mst", "s_mmv", "s_mln", "s_mrs", "s_mo"))
            s_res, s_nst, s_nmv, s_nln, s_nrs = (msem(n) for n in ("s_res", "s_nst", "s_nmv", "s_nln", "s_nrs"))
            s_xn2, s_T2, s_xn2T = msem("s_xn2"), msem("s_T2"), msem("s_xn2T")
            s_pl, s_lg, s_v8, s_i8, s_keep = (msem(n) for n in ("s_pl", "s_lg", "s_v8", "s_i8", "s_keep"))
            s_stx, s_stT = msem("s_stx"), msem("s_stT")

            NWD = 20

            def nvec(u, c):
                p = sum(k < c for k in POOL_CMUL)
                return u * (NCH - len(POOL_CMUL)) + c - p

            def npool(u, c):
                return u * len(POOL_CMUL) + sum(k < c for k in POOL_CMUL)

            block = m.enter_context(nc.Block())

            @block.sync
            def _(sp):
                sp.dma_start(X2[:, 0:TPU, :], unit_rows(x, 0)).then_inc(s_x0, 16)
                loads = [
                    (winx, W_inT[:, 0:DI]), (winz[:], W_inT[:, DI:2 * DI]),
                    (wcv, w_convT.rearrange("k c -> (k c)").partition_broadcast(P)),
                    (bcv[:], b_conv),
                    (bdt[:], b_dt),
                    (wxd, W_x[0:DI, :].rearrange("(h p) c -> p h c", p=P)),
                    (wdt, W_dtT.rearrange("(h p) c -> p h c", p=P)),
                    (Apos[:], A_log.rearrange("(h p) s -> p h s", p=P)),
                    (Dsb[:], Dv),
                    (wout[:], W_outT.rearrange("(h p) c -> p h c", p=P)),
                    (wr[:], routerT), (rbias[:], router_bias.partition_broadcast(P)),
                    (self32, sel), (idf[:], ident),
                ] + [(wbc[:, h, r, :], W_xT[h * P:(h + 1) * P, DI:DI + 2 * NS]) for h in range(NH) for r in range(3)]
                assert len(loads) == NWD
                for dst, src in loads:
                    sp.dma_start(dst, src).then_inc(s_w, 16)
                sp.dma_start(X2[:, TPU:2 * TPU, :], unit_rows(x, 1)).then_inc(s_x1, 16)
                sp.dma_start(X2[:, 2 * TPU:TILES, :],
                             x[2 * UT:TOK, :].rearrange("(j p) d -> p j d", p=P)).then_inc(s_xr, 16)
                sp.wait_ge(s_set, 1)
                for z in range(SLOT_TILES // 8):
                    sp.dma_start(xs_dram[z * 8 * P:(z + 1) * 8 * P, :].rearrange("(p r) d -> p (r d)", p=P),
                                 zrow[:]).then_inc(s_zero, 16)

                def store(u):
                    sp.wait_ge(s_xn2, u + 1)
                    sp.dma_start(unit_rows(xn2_dram, u), xn2[:]).then_inc(s_stx, 16)
                    sp.wait_ge(s_xn2T, u + 1)
                    sp.dma_start(xn2T_dram[bass.ds(u * P, P), :], xn2T[:]).then_inc(s_stT, 16)
                with sp.Fori(0, UNITS) as u:
                    store(u)
                sp.wait_ge(s_stx, 16 * UNITS)
                sp.wait_ge(s_stT, 16 * UNITS)
                sp.wait_ge(s_zero, 16 * (SLOT_TILES // 8))

            @block.tensor
            def _(pe):
                pe.wait_ge(s_w, 16 * NWD)
                for kc in range(NH):
                    for mm in range(NH):
                        last = pe.matmul(PJ[kc][:, 0:DI], wxd[:, mm, kc * P:(kc + 1) * P], wdt[:, mm, :],
                                         start=mm == 0, stop=mm == NH - 1)
                    last.then_inc(s_wdm, 1)

                def transposed(f):
                    pe.wait_ge(s_xn, f + 1)
                    if at(f, 0):
                        pe.wait_ge(s_wdc, NH)
                    else:
                        pe.wait_ge(s_dl[0], f)
                        if not (at(f, 1) or at(f, 2)):
                            pe.wait_ge(s_lg, f - 2)
                    for j in range(TPU):
                        t = pe.transpose(PJ[1][:, j * P:(j + 1) * P], xn[:, j, :], idf[:])
                    t.then_inc(s_T, 1)

                def project(f):
                    pe.wait_ge(s_xnT, f + 1)
                    if at(f, 0):
                        pe.wait_ge(s_wc, KC)
                    else:
                        pe.wait_ge(s_dl[1], f)
                        if not (at(f, 1) or at(f, 2)):
                            pe.wait_ge(s_xn2T, f - 2)
                    for h in range(NH):
                        for k in range(KC):
                            t = pe.matmul(PJ[h][:].rearrange("p (b t) -> p b t", b=UB),
                                          wcomb[:, k, h * P:(h + 1) * P],
                                          xnT[:, :, k:k + SEQ], start=k == 0, stop=k == KC - 1)
                        t.then_inc(s_pc[h], 1)
                    for h in range(NH):
                        pe.wait_ge(s_xc[h], f + 1)
                        pe.matmul(PJ[h][:].rearrange("p (b t) -> p b t", b=UB), winz[:, h * P:(h + 1) * P],
                                  xnT[:, :, KC - 1:KC - 1 + SEQ], start=True, stop=True).then_inc(s_pz[h], 1)

                def project_bc(f, par):
                    pe.wait_ge(s_sz[0], f + 1)
                    for h in range(NH):
                        t = pe.matmul(PJ[0][0:96, :], wbc[:, h, :, :].rearrange("p r n -> p (r n)"),
                                      xc[:, par, h, :], start=h == 0, stop=h == NH - 1)
                    t.then_inc(s_pbc, 1)

                def project_delta(f, par, b):
                    for o in range(NH):
                        if o == 0:
                            pe.wait_ge(s_sz[1], f + 1)
                            if b is not None:
                                pe.wait_ge(s_mo, b + 1)
                        else:
                            pe.wait_ge(s_r1, f + 1)
                        for h in range(NH):
                            t = pe.matmul(PJ[1 - o][:], wdelta[:, h, o * P:(o + 1) * P], xc[:, par, h, :],
                                          start=h == 0, stop=h == NH - 1)
                        t.then_inc(s_pd[o], 1)

                def broadcast(u, par, sg, which):
                    if which == 0 and sg == 0:
                        pe.wait_ge(s_bcs, u + 1)
                    for i in range(2):
                        k = sg * 4 + which * 2 + i
                        if not (at(u, 0) and k < 2):
                            pe.wait_ge(s_bcp, u * (NSG * 4) + k - 1)
                        for q in range(2):
                            s = which * NS + sg * SG + i * 2 + q
                            t = pe.matmul(BCP[k % 2][:, q, :], selb[:, s, :], bcs[:, par, :], start=True, stop=True)
                        t.then_inc(s_bp, 1)

                def sum_states(u, c):
                    sg, h = c // NH, c % NH
                    if c in POOL_CMUL:
                        pe.wait_ge(s_cmp, npool(u, c) + 1)
                    else:
                        pe.wait_ge(s_cmv, nvec(u, c) + 1)
                    if sg == 0 and not at(u, 0):
                        pe.wait_ge(s_yd, u * NH)
                    for s in range(SG):
                        t = pe.matmul(Y[h][:], idf[:], state[c % H_RING][:, s, :],
                                      start=sg == 0 and s == 0, stop=sg == NSG - 1 and s == SG - 1)
                    t.then_inc(s_sum, 1)

                def out_proj(b, front):
                    pe.wait_ge(s_yg, b + 1)
                    if front:
                        pe.wait_ge(s_sz[1], b + 3)
                    else:
                        pe.wait_ge(s_lg, b)
                    for j in range(TPU):
                        for h in range(NH):
                            t = pe.matmul(PJ[1][:, j * P:(j + 1) * P], yg[:, h, j * P:(j + 1) * P], wout[:, h, :],
                                          start=h == 0, stop=h == NH - 1)
                    t.then_inc(s_po, 1)

                def transposed2(b, front):
                    pe.wait_ge(s_xn2, b + 1)
                    if front:
                        pe.wait_ge(s_dl[1], b + 3)
                    for j in range(TPU):
                        t = pe.transpose(PJ[0][:, j * P:(j + 1) * P], xn2[:, j, :], idf[:])
                    t.then_inc(s_T2, 1)

                def logits(b, front):
                    pe.wait_ge(s_xn2T, b + 1)
                    if front:
                        pe.wait_ge(s_dl[0], b + 3)
                    for j in range(TPU):
                        t = pe.matmul(PJ[1][:, j * NE:(j + 1) * NE], xn2T[:, j * P:(j + 1) * P], wr[:],
                                      start=True, stop=True)
                    t.then_inc(s_pl, 1)

                def body(u, par, front, back):
                    for c in range(NCH):
                        if c == 2 and front:
                            transposed(u + 1)
                        if c == 3 and front:
                            project(u + 1)
                        if c == 4 and back:
                            out_proj(u - 1, front)
                        if c == 5 and front:
                            project_bc(u + 1, 1 - par)
                            project_delta(u + 1, 1 - par, u - 1 if back else None)
                        if c < NCH - 2:
                            broadcast(u, par, c // 2 + 1, c % 2)
                        elif front:
                            broadcast(u + 1, 1 - par, 0, c % 2)
                        if c >= 2:
                            sum_states(u, c - 2)
                        elif back:
                            sum_states(u - 1, NCH - 2 + c)
                        if c == 7 and back:
                            transposed2(u - 1, front)
                            logits(u - 1, front)

                transposed(0)
                project(0)
                project_bc(0, 0)
                project_delta(0, 0, None)
                broadcast(0, 0, 0, 0)
                broadcast(0, 0, 0, 1)
                body(0, 0, True, False)
                body(1, 1, True, True)
                body(2, 0, True, True)
                with pe.Fori(1, UNITS // 2 - 1) as pair:
                    u = pair * 2 + 1
                    body(u, 1, True, True)
                    body(u + 1, 0, True, True)
                body(UNITS - 1, 1, False, True)
                sum_states(UNITS - 1, NCH - 2)
                sum_states(UNITS - 1, NCH - 1)
                out_proj(UNITS - 1, False)
                transposed2(UNITS - 1, False)
                logits(UNITS - 1, False)

            @block.scalar
            def _(act):
                act.wait_ge(s_eps, 2)
                act.wait_ge(s_set, 4)
                act.wait_ge(s_w, 16 * NWD)
                act.activation(Apos[:], Apos[:], ACT.Exp).then_inc(s_ap, 1)
                act.activation(selb[:], self32.rearrange("p (s m) -> p s m", s=2 * NS), ACT.Copy).then_inc(s_ap, 1)
                for kc in range(NH):
                    act.wait_ge(s_wdm, kc + 1)
                    act.activation(wdelta[:, kc, :], PJ[kc][:, 0:DI], ACT.Copy).then_inc(s_wdc, 1)

                def rstd(var, ln, rs, s_mv, s_ln, s_rs, u):
                    act.wait_ge(s_mv, u + 1)
                    act.activation(ln[:], var[:, :, 1], ACT.Ln, bias=eps[:]).then_inc(s_ln, 1)
                    act.wait_ge(s_ln, u + 1)
                    act.activation(rs[:], ln[:], ACT.Exp, scale=-0.5).then_inc(s_rs, 1)

                def copy_xnT(f):
                    act.wait_ge(s_T, f + 1)
                    act.activation(xnT[:, :, KC - 1:KC - 1 + SEQ], PJ[1][:].rearrange("p (b t) -> p b t", b=UB),
                                   ACT.Copy).then_inc(s_xnT, 1)

                def silus(f, par, back):
                    if back:
                        act.wait_ge(s_yg, f - 1)
                    for h in range(NH):
                        act.wait_ge(s_pc[h], f + 1)
                        act.activation(xc[:, par, h, :], PJ[h][:], ACT.Silu, bias=bcv[:, h:h + 1]).then_inc(s_xc[h], 1)
                    for h in range(NH):
                        act.wait_ge(s_pz[h], f + 1)
                        act.activation(sz[:, par, h, :], PJ[h][:], ACT.Silu).then_inc(s_sz[h], 1)
                    act.preload_act_table_set(EXP_LN)

                def softplus(f):
                    for h in range(NH):
                        act.wait_ge(s_dm[h], f + 1)
                        act.activation(dtmp[:, h, :], dtmp[:, h, :], ACT.Exp).then_inc(s_de[h], 1)
                    for h in range(NH):
                        act.wait_ge(s_de[h], f + 1)
                        act.activation(dtmp[:, h, :], dtmp[:, h, :], ACT.Ln, bias=1.0).then_inc(s_dn[h], 1)

                def copies(u, sg, which):
                    dst = (Bbc, Cbc)[which][sg % 2]
                    for i in range(2):
                        k = sg * 4 + which * 2 + i
                        act.wait_ge(s_bp, u * (NSG * 4) + k + 1)
                        if i == 0 and not (at(u, 0) and sg < 2):
                            v, c = (u, (sg - 1) * NH) if sg else (u - 1, NCH - NH)
                            if which == 0:
                                act.wait_ge(s_bx, v * NCH + c)
                            else:
                                act.wait_ge(s_cmv, nvec(v, c))
                                act.wait_ge(s_cmp, npool(v, c))
                        act.activation(dst[:, 2 * i:2 * i + 2, :], BCP[k % 2][:], ACT.Copy).then_inc(s_bcp, 1)

                def decays(u, par, c):
                    sg, h = c // NH, c % NH
                    if sg == 0:
                        act.wait_ge(s_dl[h], u + 1)
                    if not (at(u, 0) and c < A_RING):
                        act.wait_ge(s_scan, u * NCH + c - A_RING + 1)
                    a = decay[c % A_RING].rearrange("p s (b t) -> p s b t", b=UB)
                    for s in range(SG):
                        t = act.activation(a[:, s, :, 1:SEQ], dl[:, par, h, :, 1:SEQ], ACT.Exp,
                                           scale=Aneg[:, h, sg * SG + s:sg * SG + s + 1])
                    t.then_inc(s_exp, 1)

                def copy_xn2T(b):
                    act.wait_ge(s_T2, b + 1)
                    if not at(b, 0):
                        act.wait_ge(s_stT, 16 * b)
                        act.wait_ge(s_pl, b)
                    act.activation(xn2T[:], PJ[0][:], ACT.Copy).then_inc(s_xn2T, 1)

                def body(u, par, front, back):
                    for c in range(NCH):
                        if c == 1 and front:
                            rstd(xmv, xln, xrs, s_xmv, s_xln, s_xrs, u + 1)
                        if c == 3 and front:
                            copy_xnT(u + 1)
                            silus(u + 1, 1 - par, back)
                        if c == 5 and back:
                            rstd(mmv, mln, mrs, s_mmv, s_mln, s_mrs, u - 1)
                        if c == 6 and front:
                            softplus(u + 1)
                        if c == 6 and back:
                            rstd(nmv, nln, nrs, s_nmv, s_nln, s_nrs, u - 1)
                        decays(u, par, c)
                        if c < NCH - 2:
                            copies(u, c // 2 + 1, c % 2)
                        elif front:
                            copies(u + 1, 0, c % 2)
                    if back:
                        copy_xn2T(u - 1)

                act.wait_ge(s_an, 1)
                act.preload_act_table_set(EXP_LN)
                rstd(xmv, xln, xrs, s_xmv, s_xln, s_xrs, 0)
                copy_xnT(0)
                silus(0, 0, False)
                softplus(0)
                act.wait_ge(s_ap, 2)
                copies(0, 0, 0)
                copies(0, 0, 1)
                body(0, 0, True, False)
                body(1, 1, True, True)
                body(2, 0, True, True)
                with act.Fori(1, UNITS // 2 - 1) as pair:
                    u = pair * 2 + 1
                    act.preload_act_table_set(EXP_LN)
                    body(u, 1, True, True)
                    body(u + 1, 0, True, True)
                body(UNITS - 1, 1, False, True)
                rstd(mmv, mln, mrs, s_mmv, s_mln, s_mrs, UNITS - 1)
                rstd(nmv, nln, nrs, s_nmv, s_nln, s_nrs, UNITS - 1)
                copy_xn2T(UNITS - 1)

            @block.gpsimd
            def _(pool):
                zero = scratch[:, 0:1].to_broadcast([P, UT])

                def parts(f, par, bx, cm):
                    pool.wait_ge(s_bx, bx)
                    pool.wait_ge(s_cmp, cm)
                    pool.wait_ge(s_r1, f + 1)
                    pool.tensor_tensor(bcs[32:64, par, :], r1[32:64, :], zero[32:64], ALU.add).then_inc(s_mid, 1)
                    pool.wait_ge(s_mid, 2 * f + 1)
                    pool.tensor_tensor(bcs[64:96, par, :], r1[64:96, :], zero[64:96], ALU.add).then_inc(s_mid, 1)
                    pool.wait_ge(s_mid, 2 * f + 2)
                    pool.tensor_tensor(r2[64:96, :], r1[64:96, :], bcs[64:96, par, :], ALU.subtract).then_inc(s_r2, 1)
                    pool.wait_ge(s_r2, f + 1)
                    pool.tensor_tensor(bcs[64:96, par, :], r2[64:96, :], zero[64:96], ALU.add).then_inc(s_bcs, 1)

                def times_b(u, par, c):
                    sg, h = c // NH, c % NH
                    n = u * NCH + c
                    if sg == 0:
                        pool.wait_ge(s_xc[h], u + 1)
                    pool.wait_ge(s_bcp, u * (NSG * 4) + sg * 4 + 2)
                    if not (at(u, 0) and c < H_RING):
                        pool.wait_ge(s_sum, n - H_RING + 1)
                    pool.tensor_tensor(state[c % H_RING], Bbc[sg % 2],
                                       xc[:, par, h, :].unsqueeze(1).to_broadcast([P, SG, UT]),
                                       ALU.mult).then_inc(s_bx, 1)

                def times_c(u, c):
                    sg = c // NH
                    pool.wait_ge(s_scan, u * NCH + c + 1)
                    pool.wait_ge(s_bcp, u * (NSG * 4) + sg * 4 + 4)
                    pool.tensor_tensor(state[c % H_RING], state[c % H_RING], Cbc[sg % 2], ALU.mult).then_inc(s_cmp, 1)

                def body(u, par, front, back):
                    for c in range(NCH):
                        times_b(u, par, c)
                        if c == 6 and front:
                            parts(u + 1, 1 - par, u * NCH + c + 1, npool(u, c - 1))
                            pool.wait_ge(s_bcs, u + 2)
                        if c - 1 in POOL_CMUL:
                            times_c(u, c - 1)
                        if c == 0 and back and NCH - 1 in POOL_CMUL:
                            times_c(u - 1, NCH - 1)

                parts(0, 0, 0, 0)
                pool.wait_ge(s_bcs, 1)
                body(0, 0, True, False)
                body(1, 1, True, True)
                body(2, 0, True, True)
                with pool.Fori(1, UNITS // 2 - 1) as pair:
                    u = pair * 2 + 1
                    body(u, 1, True, True)
                    body(u + 1, 0, True, True)
                body(UNITS - 1, 1, False, True)
                if NCH - 1 in POOL_CMUL:
                    times_c(UNITS - 1, NCH - 1)

            @block.vector
            def _(dve):
                dve.memset(eps[:], EPS).then_inc(s_eps, 1)
                dve.memset(scratch[:], 0.0).then_inc(s_eps, 1)
                dve.memset(zrow[:], 0.0).then_inc(s_set, 1)
                dve.memset(xnT[:], 0.0).then_inc(s_set, 1)
                for a in decay:
                    dve.memset(a, 0.0).then_inc(s_set, 1)
                dve.wait_ge(s_w, 16 * NWD)
                for k in range(KC):
                    dve.tensor_tensor(wcomb[:, k, :], winx, wcv[:, k * DI:(k + 1) * DI], ALU.mult).then_inc(s_wc, 1)
                dve.wait_ge(s_ap, 1)
                dve.tensor_scalar(Aneg[:], Apos[:], -1.0, None, ALU.mult).then_inc(s_an, 1)

                def x2_tile(u, j):
                    return X2[:, bass.ds(u * TPU + j, 1), :].rearrange("p j d -> p (j d)")

                def moments(src, st, mv, s_st, s_mv, u):
                    for j in range(TPU):
                        t = dve.bn_stats(st[:, j, :], src(j))
                    t.then_inc(s_st, 1)
                    dve.wait_ge(s_st, u + 1)
                    pause(dve, scratch, 1)
                    for j in range(TPU):
                        t = dve.bn_aggr(mv[:, j, :], st[:, j, :])
                    t.then_inc(s_mv, 1)

                def normalise(dst, src, mv, rs, s_rs, s_done, u):
                    dve.wait_ge(s_rs, u + 1)
                    for j in range(TPU):
                        t = dve.tensor_scalar(dst(j), src(j), mv[:, j, 0:1], rs[:, j:j + 1], ALU.subtract, ALU.mult)
                    t.then_inc(s_done, 1)

                def x_moments(f):
                    if at(f, 0):
                        dve.wait_ge(s_x0, 16)
                    elif at(f, 1):
                        dve.wait_ge(s_x1, 16)
                    else:
                        dve.wait_ge(s_xr, 16)
                    moments(lambda j: x2_tile(f, j), xst, xmv, s_xst, s_xmv, f)

                def x_norm(f):
                    if not at(f, 0):
                        dve.wait_ge(s_T, f)
                    normalise(lambda j: xn[:, j, :], lambda j: x2_tile(f, j), xmv, xrs, s_xrs, s_xn, f)

                def high_parts(f, par):
                    dve.wait_ge(s_pbc, f + 1)
                    dve.tensor_copy(bcs[:, par, :], PJ[0][0:96, :]).then_inc(s_hi, 1)
                    dve.wait_ge(s_hi, f + 1)
                    dve.tensor_tensor(r1[:], PJ[0][0:96, :], bcs[:, par, :], ALU.subtract).then_inc(s_r1, 1)

                def delta_min(f):
                    for h in range(NH):
                        dve.wait_ge(s_pd[h], f + 1)
                        dve.tensor_scalar(dtmp[:, h, :], PJ[1 - h][:], bdt[:, h:h + 1], 40.0,
                                          ALU.add, ALU.min).then_inc(s_dm[h], 1)

                def delta_max(f, par):
                    for h in range(NH):
                        dve.wait_ge(s_dn[h], f + 1)
                        dve.scalar_tensor_tensor(out=dl[:, par, h, :, :].rearrange("p b t -> p (b t)"),
                                                 in0=PJ[1 - h][:], scalar=bdt[:, h:h + 1], in1=dtmp[:, h, :],
                                                 op0=ALU.add, op1=ALU.max).then_inc(s_dl[h], 1)

                def scan(u, c):
                    n = u * NCH + c
                    dve.wait_ge(s_bx, n + 1)
                    dve.wait_ge(s_exp, n + 1)
                    st = state[c % H_RING].rearrange("p s t -> p (s t)")
                    dve.tensor_tensor_scan(st, decay[c % A_RING].rearrange("p s t -> p (s t)"), st,
                                           0.0, ALU.mult, ALU.add).then_inc(s_scan, 1)

                def times_c(u, c):
                    sg = c // NH
                    dve.wait_ge(s_scan, u * NCH + c + 1)
                    dve.wait_ge(s_bcp, u * (NSG * 4) + sg * 4 + 4)
                    dve.tensor_tensor(state[c % H_RING], state[c % H_RING], Cbc[sg % 2], ALU.mult).then_inc(s_cmv, 1)

                def gate(b, par):
                    dve.wait_ge(s_sum, (b + 1) * NCH)
                    if not at(b, 0):
                        dve.wait_ge(s_po, b)
                    for h in range(NH):
                        dve.scalar_tensor_tensor(out=yg[:, h, :], in0=xc[:, par, h, :], scalar=Dsb[:, h:h + 1],
                                                 in1=Y[h][:], op0=ALU.mult, op1=ALU.add).then_inc(s_yd, 1)
                    dve.wait_ge(s_yd, (b + 1) * NH)
                    dve.tensor_tensor(yg[:], yg[:], sz[:, par, :, :], ALU.mult).then_inc(s_yg, 1)

                def out_moments(b):
                    dve.wait_ge(s_po, b + 1)
                    pause(dve, scratch, 2)
                    moments(lambda j: PJ[1][:, j * P:(j + 1) * P], mst, mmv, s_mst, s_mmv, b)

                def residual(b):
                    normalise(lambda j: mo[:, j, :], lambda j: PJ[1][:, j * P:(j + 1) * P], mmv, mrs, s_mrs, s_mo, b)
                    dve.wait_ge(s_mo, b + 1)
                    rows = X2[:, bass.ds(b * TPU, TPU), :]
                    dve.tensor_tensor(rows, rows, mo[:], ALU.add).then_inc(s_res, 1)
                    dve.wait_ge(s_res, b + 1)
                    pause(dve, scratch, 3)
                    moments(lambda j: x2_tile(b, j), nst, nmv, s_nst, s_nmv, b)

                def norm2(b):
                    if not at(b, 0):
                        dve.wait_ge(s_stx, 16 * b)
                        dve.wait_ge(s_T2, b)
                    normalise(lambda j: xn2[:, j, :], lambda j: x2_tile(b, j), nmv, nrs, s_nrs, s_xn2, b)

                def pick(b):
                    dve.wait_ge(s_pl, b + 1)
                    if not at(b, 0):
                        dve.wait_ge(s_keep, b)
                    dve.tensor_tensor(lgs[:], PJ[1][:, 0:TPU * NE].rearrange("p (j e) -> p j e", j=TPU),
                                      rbias[:].unsqueeze(1).to_broadcast([P, TPU, NE]), ALU.add).then_inc(s_lg, 1)
                    dve.wait_ge(s_lg, b + 1)
                    pause(dve, scratch, 4)
                    for j in range(TPU):
                        t = dve.max(v8s[:, j, :], lgs[:, j, :])
                    t.then_inc(s_v8, 1)
                    dve.wait_ge(s_v8, b + 1)
                    pause(dve, scratch, 5)
                    for j in range(TPU):
                        t = dve.max_index(i8s[:, j, :], v8s[:, j, :], lgs[:, j, :])
                    t.then_inc(s_i8, 1)
                    dve.tensor_copy(LG[:, bass.ds(b * TPU, TPU), :], lgs[:])
                    dve.tensor_copy(V8[:, bass.ds(b * TPU, TPU), :], v8s[:])
                    dve.wait_ge(s_i8, b + 1)
                    dve.tensor_copy(I8[:, bass.ds(b * TPU, TPU), :], i8s[:]).then_inc(s_keep, 1)

                def body(u, par, front, back):
                    for c in range(NCH):
                        scan(u, c)
                        if c and c - 1 not in POOL_CMUL:
                            times_c(u, c - 1)
                        if c == 0 and back and NCH - 1 not in POOL_CMUL:
                            times_c(u - 1, NCH - 1)
                        if c == 0 and front:
                            x_moments(u + 1)
                        if c == 1 and front:
                            x_norm(u + 1)
                        if c == 2 and back:
                            gate(u - 1, 1 - par)
                        if c == 4 and back:
                            out_moments(u - 1)
                        if c == 5 and back:
                            residual(u - 1)
                        if c == 5 and front:
                            high_parts(u + 1, 1 - par)
                            delta_min(u + 1)
                        if c == 6 and front:
                            delta_max(u + 1, 1 - par)
                        if c == 6 and back:
                            norm2(u - 1)
                    if back:
                        pick(u - 1)

                x_moments(0)
                x_norm(0)
                high_parts(0, 0)
                delta_min(0)
                delta_max(0, 0)
                body(0, 0, True, False)
                body(1, 1, True, True)
                body(2, 0, True, True)
                with dve.Fori(1, UNITS // 2 - 1) as pair:
                    u = pair * 2 + 1
                    body(u, 1, True, True)
                    body(u + 1, 0, True, True)
                body(UNITS - 1, 1, False, True)
                if NCH - 1 not in POOL_CMUL:
                    times_c(UNITS - 1, NCH - 1)
                gate(UNITS - 1, (UNITS - 1) % 2)
                out_moments(UNITS - 1)
                residual(UNITS - 1)
                norm2(UNITS - 1)
                pick(UNITS - 1)

        te_dram = nc.dram_tensor("te_scratch", (4 * P,), I32, kind="Internal").ap()
        with ExitStack() as r:
            def rsem(name):
                return r.enter_context(nc.semaphore(name))

            W = TILES * NE
            TC = -(-SLOT_TILES // P)

            def area(i, n=1):
                return ARENA[:, i * W:(i + n) * W]

            def by_tile(ap):
                return ap.rearrange("p (j e) -> p j e", e=NE)

            pick = [by_tile(area(k)) for k in range(TOPK)]
            oh = area(4)
            tmp = by_tile(area(5))
            tot = area(6)
            incl = area(7)
            scanm = area(8)
            pos = by_tile(area(9))

            def rsb(name, shape, dt=F32):
                return r.enter_context(nc.sbuf_tensor(name, shape, dt))

            up_sb, ones = rsb("up_sb", [P, P]), rsb("ones", [P, P])
            iei, ief = rsb("iei", [P, NE], I32), rsb("ief", [P, NE])
            i8f = rsb("i8f", [P, TILES, TOPK])
            ssum, srec = rsb("ssum", [P, TILES]), rsb("srec", [P, TILES])
            v4 = rsb("v4", [P, TILES, TOPK])
            wsum, wrec = rsb("wsum", [P, TILES]), rsb("wrec", [P, TILES])
            cnti, cnts = rsb("cnti", [P, NE], I32), rsb("cnts", [P, NE], I32)
            ntf, nti, base = rsb("ntf", [P, NE]), rsb("nti", [P, NE]), rsb("base", [P, NE])
            gi, gf = rsb("gi", [P, TC], I32), rsb("gf", [P, TC])
            cmp_ = rsb("cmp_", [P, TC, NE])
            tef, tei = rsb("tef", [P, TC]), rsb("tei", [P, TC], I32)
            idxf = rsb("idxf", [P, TILES, TOPK])
            PR = [r.enter_context(nc.psum_tensor(f"PR{i}", [P, W // 4], F32)) for i in range(4)]
            PT = [r.enter_context(nc.psum_tensor(f"PT{i}", [P, W // 4], F32)) for i in range(4)]

            s_c = rsem("s_c")
            s_iota = rsem("s_iota")
            s_v = rsem("s_v")
            s_oh, s_pr = rsem("s_oh"), rsem("s_pr")
            s_sub, s_ex = rsem("s_sub"), rsem("s_ex")
            s_tc, s_te, s_teo = rsem("s_tc"), rsem("s_te"), rsem("s_teo")
            block = r.enter_context(nc.Block())

            @block.sync
            def _(sp):
                sp.dma_start(up_sb[:], upper).then_inc(s_c, 16)
                sp.wait_ge(s_te, 1)
                with nc.allow_non_contiguous_dma(reason="a few hundred integers"):
                    sp.dma_start(te_dram[0:TC * P].rearrange("(c p) -> p c", p=P), tei[:]).then_inc(s_teo, 16)
                sp.wait_ge(s_teo, 16)

            @block.gpsimd
            def _(pool):
                pool.iota(iei[:], pattern=[[1, NE]], base=0, channel_multiplier=0).then_inc(s_iota, 1)
                pool.iota(gi[:], pattern=[[P, TC]], base=0, channel_multiplier=1).then_inc(s_iota, 1)

            @block.tensor
            def _(pe):
                pe.wait_ge(s_c, 16)
                pe.wait_ge(s_oh, 1)
                for i in range(4):
                    cols = oh[:, i * (W // 4):(i + 1) * (W // 4)]
                    pe.matmul(PR[i][:], up_sb[:], cols, start=True, stop=True)
                    pe.matmul(PT[i][:], ones[:], cols, start=True, stop=True).then_inc(s_pr, 1)

            @block.scalar
            def _(act):
                act.wait_ge(s_sub, 1)
                act.activation(tmp, tmp, ACT.Exp).then_inc(s_ex, 1)
                act.activation(v4[:], v4[:], ACT.Exp).then_inc(s_ex, 1)
                for i in range(4):
                    act.wait_ge(s_pr, i + 1)
                    act.activation(tot.rearrange("p (e j) -> p j e", j=TILES)[:, i * TILES // 4:(i + 1) * TILES // 4, :],
                                   PT[i][:].rearrange("p (j e) -> p j e", e=NE), ACT.Copy).then_inc(s_tc, 1)

            @block.vector
            def _(dve):
                steps = [0]

                def step(ins):
                    steps[0] += 1
                    ins.then_inc(s_v, 1)
                    dve.wait_ge(s_v, steps[0])

                dve.wait_ge(s_iota, 2)
                dve.tensor_copy(i8f[:], I8[:, :, 0:TOPK])
                dve.tensor_copy(gf[:], gi[:])
                dve.memset(ones[:], 1.0)
                step(dve.tensor_copy(ief[:], iei[:]))
                for k in range(TOPK):
                    step(dve.tensor_tensor(pick[k], ief[:].unsqueeze(1).to_broadcast([P, TILES, NE]),
                                           i8f[:, :, k:k + 1].to_broadcast([P, TILES, NE]), ALU.is_equal))
                step(dve.tensor_tensor(by_tile(oh), pick[0], pick[1], ALU.add))
                step(dve.tensor_tensor(by_tile(oh), by_tile(oh), pick[2], ALU.add))
                dve.tensor_tensor(by_tile(oh), by_tile(oh), pick[3], ALU.add).then_inc(s_oh, 1)
                dve.tensor_tensor(v4[:], V8[:, :, 0:TOPK], V8[:, :, 0:1].to_broadcast([P, TILES, TOPK]), ALU.subtract)
                dve.tensor_tensor(tmp, LG[:], V8[:, :, 0:1].to_broadcast([P, TILES, NE]), ALU.subtract).then_inc(s_sub, 1)
                step(dve.memset(scanm, 1.0))
                step(dve.memset(scanm.rearrange("p (e j) -> p e j", j=TILES)[:, :, 0:1], 0.0))
                dve.wait_ge(s_ex, 2)
                step(dve.tensor_reduce(ssum[:], tmp, AX.X, ALU.add))
                step(dve.reciprocal(srec[:], ssum[:]))
                step(dve.tensor_tensor(v4[:], v4[:], srec[:].unsqueeze(2).to_broadcast([P, TILES, TOPK]), ALU.mult))
                step(dve.tensor_reduce(wsum[:], v4[:], AX.X, ALU.add))
                step(dve.tensor_scalar(wsum[:], wsum[:], 1e-12, None, ALU.max))
                step(dve.reciprocal(wrec[:], wsum[:]))
                step(dve.tensor_tensor(WT[:], v4[:], wrec[:].unsqueeze(2).to_broadcast([P, TILES, TOPK]), ALU.mult))
                dve.wait_ge(s_tc, 4)
                step(dve.tensor_tensor_scan(incl, scanm, tot, 0.0, ALU.mult, ALU.add))
                step(dve.tensor_scalar(cnti[:], incl.rearrange("p (e j) -> p e j", j=TILES)[:, :, TILES - 1],
                                       float(P - 1), None, ALU.add))
                step(dve.tensor_scalar(cnts[:], cnti[:], 7, None, ALU.arith_shift_right))
                step(dve.tensor_copy(ntf[:], cnts[:]))
                step(dve.tensor_tensor_scan(nti[:], ones[:, 0:NE], ntf[:], 0.0, ALU.mult, ALU.add))
                step(dve.tensor_tensor(base[:], nti[:], ntf[:], ALU.subtract))
                step(dve.tensor_scalar(base[:], base[:], float(P), None, ALU.mult))
                step(dve.tensor_tensor(cmp_[:], nti[:].unsqueeze(1).to_broadcast([P, TC, NE]),
                                       gf[:].unsqueeze(2).to_broadcast([P, TC, NE]), ALU.is_le))
                step(dve.tensor_reduce(tef[:], cmp_[:], AX.X, ALU.add))
                dve.tensor_scalar(tei[:], tef[:], float(NE - 1), None, ALU.min).then_inc(s_te, 1)
                step(dve.tensor_tensor(incl, incl, tot, ALU.subtract))
                step(dve.tensor_tensor(pos, incl.rearrange("p (e j) -> p j e", j=TILES),
                                       base[:].unsqueeze(1).to_broadcast([P, TILES, NE]), ALU.add))
                for i in range(4):
                    part = pos[:, i * TILES // 4:(i + 1) * TILES // 4, :]
                    dve.wait_ge(s_pr, i + 1)
                    step(dve.tensor_tensor(part, part, PR[i][:].rearrange("p (j e) -> p j e", e=NE), ALU.add))
                for k in range(TOPK):
                    step(dve.tensor_tensor(pick[k], pick[k], pos, ALU.mult))
                    step(dve.tensor_reduce(idxf[:, :, k], pick[k], AX.X, ALU.add))
                step(dve.tensor_copy(IDX[:], idxf[:].rearrange("p j k -> p (j k)")))

        WGU = ARENA[:, 0:NE * 2 * P].rearrange("p (e c) -> p e c", e=NE)
        WD = ARENA[:, NE * 2 * P:NE * 3 * P].rearrange("p (e c) -> p e c", e=NE)
        SH = ARENA[:, NE * 3 * P:NE * 3 * P + TILES * DM].rearrange("p (j d) -> p j d", d=DM)
        NL = UT * TOPK // P
        with ExitStack() as r:
            def rsb(name, shape, dt=F32):
                return r.enter_context(nc.sbuf_tensor(name, shape, dt))

            def rsem(name):
                return r.enter_context(nc.semaphore(name))

            stage = [rsb(f"stage{i}", [P, TPU, DM]) for i in range(2)]
            stidx = [rsb(f"stidx{i}", [P, NL], U32) for i in range(2)]
            xT = [rsb(f"xT{i}", [P, UT]) for i in range(2)]
            sgw, suw, sdw = rsb("sgw", [P, HS]), rsb("suw", [P, HS]), rsb("sdw", [P, HST, DM])
            gs = rsb("gs", [P, 2, UT])
            hsb = rsb("hsb", [P, HST, UT])
            PG = [r.enter_context(nc.psum_tensor(f"PG{i}", [P, UT], F32)) for i in range(2)]
            PU = [r.enter_context(nc.psum_tensor(f"PU{i}", [P, UT], F32)) for i in range(2)]
            PD = [r.enter_context(nc.psum_tensor(f"PD{i}", [P, UT], F32)) for i in range(2)]
            s_ew, s_sw = rsem("s_ew"), rsem("s_sw")
            s_st = [rsem(f"s_st{i}") for i in range(2)]
            s_xT = [rsem(f"s_xT{i}") for i in range(2)]
            s_ix = rsem("s_ix")
            s_sc = [rsem(f"s_sc{i}") for i in range(2)]
            s_pg, s_pu, s_gs, s_hs = rsem("s_pg"), rsem("s_pu"), rsem("s_gs"), rsem("s_hs")
            s_pd2, s_sh = rsem("s_pd2"), rsem("s_sh")
            block = r.enter_context(nc.Block())

            @block.sync
            def _(sp):
                for dst, src in ((sgw[:], sgateT), (suw[:], supT), (sdw[:], sdownT.rearrange("(m p) d -> p m d", p=P))):
                    sp.dma_start(dst, src).then_inc(s_sw, 16)

                def load(u, par, pair):
                    if pair is not None:
                        sp.wait_ge(s_sc[par], 16 * NL * pair)
                    sp.dma_start(stage[par][:], unit_rows(xn2_dram, u)).then_inc(s_st[par], 16)
                load(0, 0, None)
                load(1, 1, None)
                sp.dma_start(WGU, gate_upT).then_inc(s_ew, 16)
                sp.dma_start(WD, downT).then_inc(s_ew, 16)
                with sp.Fori(1, UNITS // 2) as pair:
                    load(pair * 2, 0, pair)
                    load(pair * 2 + 1, 1, pair)
                sp.wait_ge(s_ew, 32)

            @block.gpsimd
            def _(pool):
                def scatter(u, par, pair):
                    if not at(pair, 0):
                        pool.wait_ge(s_sc[par], 16 * NL * pair)
                    pause(pool, scratch, 6)
                    pool.tensor_copy(stidx[par][:], IDX[:, bass.ds(u * NL, NL)]).then_inc(s_ix, 1)
                    pool.wait_ge(s_ix, u + 1)
                    pool.wait_ge(s_st[par], 16 * (pair + 1))
                    pause(pool, scratch, 7)
                    for j in range(TPU):
                        for k in range(TOPK):
                            pool.indirect_dma_start(
                                xs_dram, bass.IndirectOffsetOnAxis(ap=stidx[par][:, j * TOPK + k:j * TOPK + k + 1], axis=0),
                                stage[par][:, j, :], None).then_inc(s_sc[par], 16)
                scatter(0, 0, 0)
                scatter(1, 1, 0)
                with pool.Fori(1, UNITS // 2) as pair:
                    scatter(pair * 2, 0, pair)
                    scatter(pair * 2 + 1, 1, pair)
                for par in range(2):
                    pool.wait_ge(s_sc[par], 16 * NL * (UNITS // 2))

            @block.tensor
            def _(pe):
                pe.wait_ge(s_sw, 48)

                def hidden(u, par, pair, back):
                    pe.wait_ge(s_xT[par], 16 * (pair + 1))
                    for mm in range(HST):
                        n = u * HST + mm
                        if back or mm >= 2:
                            pe.wait_ge(s_hs, n - 1)
                        pe.matmul(PG[mm % 2][:], sgw[:, mm * P:(mm + 1) * P], xT[par][:],
                                  start=True, stop=True).then_inc(s_pg, 1)
                        pe.matmul(PU[mm % 2][:], suw[:, mm * P:(mm + 1) * P], xT[par][:],
                                  start=True, stop=True).then_inc(s_pu, 1)

                def down(u, par, back):
                    pe.wait_ge(s_hs, HST * (u + 1))
                    if back:
                        pe.wait_ge(s_sh, u - 1)
                    for j in range(TPU):
                        for mm in range(HST):
                            t = pe.matmul(PD[par][:, j * P:(j + 1) * P], hsb[:, mm, j * P:(j + 1) * P], sdw[:, mm, :],
                                          start=mm == 0, stop=mm == HST - 1)
                    t.then_inc(s_pd2, 1)
                for u in range(2):
                    hidden(u, u, 0, u > 0)
                    down(u, u, False)
                with pe.Fori(1, UNITS // 2) as pair:
                    for par in range(2):
                        hidden(pair * 2 + par, par, pair, True)
                        down(pair * 2 + par, par, True)

            @block.scalar
            def _(act):
                def load(u, par):
                    act.dma_start(xT[par][:], xn2T_dram[bass.ds(u * P, P), :]).then_inc(s_xT[par], 16)

                def unit(u, par, back, more):
                    for mm in range(HST):
                        n = u * HST + mm
                        act.wait_ge(s_pg, n + 1)
                        if back or mm >= 2:
                            act.wait_ge(s_hs, n - 1)
                        act.activation(gs[:, mm % 2, :], PG[mm % 2][:], ACT.Silu).then_inc(s_gs, 1)
                    act.wait_ge(s_pd2, u + 1)
                    if more:
                        load(u + 2, par)
                    act.activation(SH[:, bass.ds(u * TPU, TPU), :], PD[par][:].rearrange("p (j d) -> p j d", d=DM),
                                   ACT.Copy).then_inc(s_sh, 1)
                load(0, 0)
                load(1, 1)
                unit(0, 0, False, True)
                unit(1, 1, True, True)
                with act.Fori(1, UNITS // 2 - 1) as pair:
                    unit(pair * 2, 0, True, True)
                    unit(pair * 2 + 1, 1, True, True)
                unit(UNITS - 2, 0, True, False)
                unit(UNITS - 1, 1, True, False)

            @block.vector
            def _(dve):
                def unit(u):
                    if not at(u, 0):
                        dve.wait_ge(s_pd2, u)
                    for mm in range(HST):
                        n = u * HST + mm
                        dve.wait_ge(s_gs, n + 1)
                        dve.wait_ge(s_pu, n + 1)
                        dve.tensor_tensor(hsb[:, mm, :], gs[:, mm % 2, :], PU[mm % 2][:], ALU.mult).then_inc(s_hs, 1)
                unit(0)
                with dve.Fori(1, UNITS) as u:
                    unit(u)

        with ExitStack() as r:
            def rsb(name, shape, dt=F32):
                return r.enter_context(nc.sbuf_tensor(name, shape, dt))

            def rsem(name):
                return r.enter_context(nc.semaphore(name))

            NX = 4
            xg = [rsb(f"xg{i}", [P, GT, DM]) for i in range(NX)]
            te = [rsb(f"te{i}", [1, GT], I32) for i in range(NX)]
            xgT = [rsb(f"xgT{i}", [P, GT * P]) for i in range(2)]
            sg = [rsb(f"sg{i}", [P, GT, P]) for i in range(2)]
            hg = [rsb(f"hg{i}", [P, GT, P]) for i in range(2)]
            hgT = [rsb(f"hgT{i}", [P, GT * P]) for i in range(2)]
            yo = [rsb(f"yo{i}", [P, GT, DM]) for i in range(2)]
            PXT = r.enter_context(nc.psum_tensor("PXT", [P, GT * P], F32))
            PHT = r.enter_context(nc.psum_tensor("PHT", [P, GT * P], F32))
            PGU = [r.enter_context(nc.psum_tensor(f"PGU{i}", [P, 2, 2, P], F32)) for i in range(4)]
            PY = [r.enter_context(nc.psum_tensor(f"PY{i}", [P, GT * DM], F32)) for i in range(2)]
            s_xg = [rsem(f"s_xg{i}") for i in range(NX)]
            s_xt, s_xtc = rsem("s_xt"), rsem("s_xtc")
            s_gu, s_sg, s_hg = rsem("s_gu"), rsem("s_sg"), rsem("s_hg")
            s_ht, s_htc, s_y, s_yo = rsem("s_ht"), rsem("s_htc"), rsem("s_y"), rsem("s_yo")
            s_ys = [rsem(f"s_ys{i}") for i in range(2)]
            block = r.enter_context(nc.Block())

            def slot_rows(dram, g):
                return dram[bass.ds(g * GT * P, GT * P), :].rearrange("(j p) d -> p j d", p=P)

            @block.sync
            def _(sp):
                def load(g, i, turn):
                    if turn is not None:
                        sp.wait_ge(s_xt, g - NX + 1)
                    sp.dma_start(xg[i][:], slot_rows(xs_dram, g)).then_inc(s_xg[i], 16)
                for g in range(NX):
                    load(g, g, None)
                with sp.Fori(1, GROUPS // NX) as turn:
                    for i in range(NX):
                        load(turn * NX + i, i, turn)

            @block.gpsimd
            def _(pool):
                def store(g, par, pair):
                    pool.wait_ge(s_yo, g + 1)
                    pool.dma_start(slot_rows(ys_dram, g), yo[par][:]).then_inc(s_ys[par], 16)
                with pool.Fori(0, GROUPS // 2) as pair:
                    store(pair * 2, 0, pair)
                    store(pair * 2 + 1, 1, pair)
                for par in range(2):
                    pool.wait_ge(s_ys[par], 16 * (GROUPS // 2))

            @block.tensor
            def _(pe):
                def experts(first, n):
                    return nc.values_load_multi_w_load_instructions(
                        te_dram[bass.ds(first, n)].unsqueeze(0), engines=[mybir.EngineType.PE], min_val=0,
                        max_val=NE - 1, skip_runtime_bounds_check_because="it is a minimum with NE - 1")[1]

                def tokens_T(g, i, turn):
                    pe.wait_ge(s_xg[i], 16 * (turn + 1))
                    if not at(g, 0):
                        pe.wait_ge(s_xtc, g)
                    for j in range(GT):
                        t = pe.transpose(PXT[:, j * P:(j + 1) * P], xg[i][:, j, :], idf[:])
                    t.then_inc(s_xt, 1)

                def gate_up(g, par, es, back):
                    pe.wait_ge(s_xtc, g + 1)
                    if back:
                        pe.wait_ge(s_hg, 2 * g - 2)
                    for j in range(GT):
                        t = pe.matmul(PGU[2 * par + j // 2][:, j % 2, :, :].rearrange("p a c -> p (a c)"),
                                      xgT[par][:, j * P:(j + 1) * P],
                                      WGU[:, bass.ds(es[j], 1), :].rearrange("p e c -> p (e c)"),
                                      start=True, stop=True)
                        if j % 2:
                            t.then_inc(s_gu, 1)

                def hidden_T(g, par):
                    pe.wait_ge(s_hg, 2 * g + 2)
                    if not at(g, 0):
                        pe.wait_ge(s_htc, g)
                    for j in range(GT):
                        t = pe.transpose(PHT[:, j * P:(j + 1) * P], hg[par][:, j, :], idf[:])
                    t.then_inc(s_ht, 1)

                def down(g, par, es, back):
                    pe.wait_ge(s_htc, g + 1)
                    if back:
                        pe.wait_ge(s_yo, g - 1)
                    for j in range(GT):
                        t = pe.matmul(PY[par][:, j * DM:(j + 1) * DM], hgT[par][:, j * P:(j + 1) * P],
                                      WD[:, bass.ds(es[j], 1), :].rearrange("p e c -> p (e c)"),
                                      start=True, stop=True)
                    t.then_inc(s_y, 1)

                def body(g, par, i, turn, es, before, back, more):
                    if before is not None:
                        hidden_T(g - 1, 1 - par)
                    gate_up(g, par, es, back)
                    if before is not None:
                        down(g - 1, 1 - par, before, back)
                    if more:
                        tokens_T(g + 1, (i + 1) % NX, turn + (i + 1) // NX)

                def turn_of_groups(turn, last):
                    es = experts(turn * (NX * GT) - GT, (NX + 1) * GT)
                    for i in range(NX):
                        body(turn * NX + i, i % 2, i, turn, es[(i + 1) * GT:(i + 2) * GT], es[i * GT:(i + 1) * GT],
                             True, not last or i < NX - 1)
                    return es

                tokens_T(0, 0, 0)
                es = experts(0, NX * GT)
                for g in range(NX):
                    body(g, g % 2, g, 0, es[g * GT:(g + 1) * GT], es[(g - 1) * GT:g * GT] if g else None, g >= 3, True)
                with pe.Fori(1, GROUPS // NX - 1) as turn:
                    turn_of_groups(turn, False)
                es = turn_of_groups(GROUPS // NX - 1, True)
                hidden_T(GROUPS - 1, 1)
                down(GROUPS - 1, 1, es[NX * GT:], True)

            @block.scalar
            def _(act):
                def tokens(g, par):
                    act.wait_ge(s_xt, g + 1)
                    if not (at(g, 0) or at(g, 1)):
                        act.wait_ge(s_gu, 2 * g - 2)
                    act.activation(xgT[par][:], PXT[:], ACT.Copy).then_inc(s_xtc, 1)

                def gates(g, par):
                    for q in range(2):
                        act.wait_ge(s_gu, 2 * g + q + 1)
                        if not (at(g, 0) or at(g, 1)):
                            act.wait_ge(s_hg, 2 * g - 3 + q)
                        act.activation(sg[par][:, 2 * q:2 * q + 2, :], PGU[2 * par + q][:, :, 0, :], ACT.Silu).then_inc(s_sg, 1)
                tokens(0, 0)
                for g in range(2):
                    gates(g, g)
                    tokens(g + 1, 1 - g)
                with act.Fori(1, GROUPS // 2 - 1) as pair:
                    for par in range(2):
                        gates(pair * 2 + par, par)
                        tokens(pair * 2 + par + 1, 1 - par)
                gates(GROUPS - 2, 0)
                tokens(GROUPS - 1, 1)
                gates(GROUPS - 1, 1)

            @block.vector
            def _(dve):
                def hidden(g, par):
                    if not (at(g, 0) or at(g, 1)):
                        dve.wait_ge(s_ht, g - 1)
                    for q in range(2):
                        dve.wait_ge(s_sg, 2 * g + q + 1)
                        dve.tensor_tensor(hg[par][:, 2 * q:2 * q + 2, :], sg[par][:, 2 * q:2 * q + 2, :],
                                          PGU[2 * par + q][:, :, 1, :], ALU.mult).then_inc(s_hg, 1)

                def hidden_T(g, par):
                    dve.wait_ge(s_ht, g + 1)
                    if not (at(g, 0) or at(g, 1)):
                        dve.wait_ge(s_y, g - 1)
                    dve.tensor_copy(hgT[par][:], PHT[:]).then_inc(s_htc, 1)

                def output(g, par, pair):
                    dve.wait_ge(s_y, g + 1)
                    if not at(pair, 0):
                        dve.wait_ge(s_ys[par], 16 * pair)
                    dve.tensor_copy(yo[par][:].rearrange("p j d -> p (j d)"), PY[par][:]).then_inc(s_yo, 1)

                def both(pair):
                    hidden_T(pair * 2 + 1, 1)
                    hidden(pair * 2 + 2, 0)
                    output(pair * 2 + 1, 1, pair)
                    hidden_T(pair * 2 + 2, 0)
                    hidden(pair * 2 + 3, 1)
                    output(pair * 2 + 2, 0, pair + 1)
                hidden(0, 0)
                hidden_T(0, 0)
                hidden(1, 1)
                output(0, 0, 0)
                both(0)
                with dve.Fori(1, GROUPS // 2 - 1) as pair:
                    both(pair)
                hidden_T(GROUPS - 1, 1)
                output(GROUPS - 1, 1, GROUPS // 2 - 1)

        with ExitStack() as r:
            def rsb(name, shape, dt=F32):
                return r.enter_context(nc.sbuf_tensor(name, shape, dt))

            def rsem(name):
                return r.enter_context(nc.semaphore(name))

            gidx = [rsb(f"gidx{i}", [P, NL], U32) for i in range(2)]
            rows = [rsb(f"rows{i}", [P, TPU, TOPK, DM]) for i in range(2)]
            fst, fmv = rsb("fst", [P, TPU, 6]), rsb("fmv", [P, TPU, 2])
            fln, frs = rsb("fln", [P, TPU]), rsb("frs", [P, TPU])
            fw = rsb("fw", [P, TPU, TOPK])
            acc = rsb("acc", [P, TPU, DM])
            fo = [rsb(f"fo{i}", [P, TPU, DM]) for i in range(2)]
            s_gi, s_fw, s_acc = rsem("s_gi"), rsem("s_fw"), rsem("s_acc")
            s_g = [rsem(f"s_g{i}") for i in range(2)]
            s_fst, s_fmv, s_fln, s_frs, s_fn, s_fo = (rsem(n) for n in ("s_fst", "s_fmv", "s_fln", "s_frs", "s_fn", "s_fo"))
            s_out = [rsem(f"s_out{i}") for i in range(2)]
            block = r.enter_context(nc.Block())

            @block.gpsimd
            def _(pool):
                def gather(u, par, pair):
                    if not at(pair, 0):
                        pool.wait_ge(s_g[par], 16 * NL * pair)
                    pause(pool, scratch, 8)
                    pool.tensor_copy(gidx[par][:], IDX[:, bass.ds(u * NL, NL)]).then_inc(s_gi, 1)
                    pool.wait_ge(s_gi, u + 1)
                    if not (at(u, 0) or at(u, 1)):
                        pool.wait_ge(s_acc, (u - 1) * TOPK)
                    pause(pool, scratch, 9)
                    for j in range(TPU):
                        for k in range(TOPK):
                            pool.indirect_dma_start(
                                rows[par][:, j, k, :], None, ys_dram,
                                bass.IndirectOffsetOnAxis(ap=gidx[par][:, j * TOPK + k:j * TOPK + k + 1], axis=0)
                            ).then_inc(s_g[par], 16)
                gather(0, 0, 0)
                gather(1, 1, 0)
                with pool.Fori(1, UNITS // 2) as pair:
                    gather(pair * 2, 0, pair)
                    gather(pair * 2 + 1, 1, pair)

            @block.vector
            def _(dve):
                def unit(u, par, pair):
                    if not at(u, 0):
                        dve.wait_ge(s_acc, u * TOPK)
                    dve.tensor_copy(fw[:], WT[:, bass.ds(u * TPU, TPU), :]).then_inc(s_fw, 1)
                    dve.wait_ge(s_fw, u + 1)
                    dve.wait_ge(s_g[par], 16 * NL * (pair + 1))
                    for k in range(TOPK):
                        if k:
                            dve.wait_ge(s_acc, u * TOPK + k)
                        for j in range(TPU):
                            sh = SH[:, bass.ds(u * TPU + j, 1), :].rearrange("p j d -> p (j d)")
                            t = dve.scalar_tensor_tensor(out=acc[:, j, :], in0=rows[par][:, j, k, :],
                                                         scalar=fw[:, j, k:k + 1], in1=acc[:, j, :] if k else sh,
                                                         op0=ALU.mult, op1=ALU.add)
                        t.then_inc(s_acc, 1)
                    dve.wait_ge(s_acc, u * TOPK + TOPK)
                    pause(dve, scratch, 10)
                    for j in range(TPU):
                        t = dve.bn_stats(fst[:, j, :], acc[:, j, :])
                    t.then_inc(s_fst, 1)
                    dve.wait_ge(s_fst, u + 1)
                    pause(dve, scratch, 11)
                    for j in range(TPU):
                        t = dve.bn_aggr(fmv[:, j, :], fst[:, j, :])
                    t.then_inc(s_fmv, 1)
                    dve.wait_ge(s_frs, u + 1)
                    if not at(pair, 0):
                        dve.wait_ge(s_out[par], 16 * pair)
                    for j in range(TPU):
                        t = dve.tensor_scalar(fo[par][:, j, :], acc[:, j, :], fmv[:, j, 0:1], frs[:, j:j + 1],
                                              ALU.subtract, ALU.mult)
                    t.then_inc(s_fn, 1)
                    dve.wait_ge(s_fn, u + 1)
                    dve.tensor_tensor(fo[par][:], fo[par][:], X2[:, bass.ds(u * TPU, TPU), :], ALU.add).then_inc(s_fo, 1)
                unit(0, 0, 0)
                unit(1, 1, 0)
                with dve.Fori(1, UNITS // 2) as pair:
                    unit(pair * 2, 0, pair)
                    unit(pair * 2 + 1, 1, pair)

            @block.scalar
            def _(act):
                with act.Fori(0, UNITS) as u:
                    act.preload_act_table_set(EXP_LN)
                    act.wait_ge(s_fmv, u + 1)
                    act.activation(fln[:], fmv[:, :, 1], ACT.Ln, bias=eps[:]).then_inc(s_fln, 1)
                    act.wait_ge(s_fln, u + 1)
                    act.activation(frs[:], fln[:], ACT.Exp, scale=-0.5).then_inc(s_frs, 1)

            @block.sync
            def _(sp):
                with sp.Fori(0, UNITS // 2) as pair:
                    for par in range(2):
                        sp.wait_ge(s_fo, pair * 2 + par + 1)
                        sp.dma_start(unit_rows(out, pair * 2 + par), fo[par][:]).then_inc(s_out[par], 16)
                for par in range(2):
                    sp.wait_ge(s_out[par], 16 * (UNITS // 2))


def kernel(**inputs):
    import concourse.bacc as _bacc
    from concourse.bass_utils import run_bass_kernel_spmd as _run

    a = {k.removeprefix("L0_attn_").removeprefix("L0_ffn_"): np.asarray(v) for k, v in inputs.items()}
    layout = {
        "x": a["x"].reshape(TOK, DM),
        "W_inT": a["W_in"].T,
        "w_convT": a["w_conv"].T,
        "b_conv": a["b_conv"].reshape(NH, P).T,
        "W_x": a["W_x"],
        "W_xT": a["W_x"].T,
        "W_dtT": a["W_dt"].T,
        "b_dt": a["b_dt"].reshape(NH, P).T,
        "A_log": a["A_log"],
        "Dv": a["D"].reshape(NH, P).T,
        "W_outT": a["W_out"].T,
        "routerT": a["router_w"].T,
        "router_bias": a["router_bias"],
        "gate_upT": np.stack([a["gate_w"], a["up_w"]], 1).transpose(3, 0, 1, 2).reshape(DM, NE, 2 * P),
        "downT": a["down_w"].transpose(2, 0, 1),
        "sgateT": a["sgate_w"].T,
        "supT": a["sup_w"].T,
        "sdownT": a["sdown_w"].T,
        "sel": np.repeat(np.tile(np.eye(2 * NS, dtype=np.float32), (3, 1)), P, axis=1),
        "ident": np.eye(P, dtype=np.float32),
        "upper": np.triu(np.ones((P, P), np.float32), 1),
    }
    nc = _bacc.Bacc("TRN2", target_bir_lowering=False, num_devices=1)
    arrays, args = {}, []
    for name, v in layout.items():
        v = np.ascontiguousarray(v)
        arrays[f"in_{name}"] = v
        args.append(nc.dram_tensor(f"in_{name}", v.shape, mybir.dt.from_np(v.dtype), kind="ExternalInput").ap())
    args.append(nc.dram_tensor("out_0", (TOK, DM), F32, kind="ExternalOutput").ap())
    mamba_moe_kernel(nc, *args)
    r = _run(nc, [arrays], core_ids=[0])
    return r.results[0]["out_0"].reshape(BATCH, SEQ, DM)
```

```python
import numpy as np
import concourse.bass as bass
from concourse import mybir
from contextlib import ExitStack

F32 = mybir.dt.float32
BF16 = mybir.dt.bfloat16
U32 = mybir.dt.uint32
I32 = mybir.dt.int32
ALU = mybir.AluOpType
ACT = mybir.ActivationFunctionType
AX = mybir.AxisListType

P = 128
BATCH, SEQ = 32, 256
DM = 128
DI = 256
NS = 16
KC = 4
NH = DI // P
TOK = BATCH * SEQ
UB = 2
UT = UB * SEQ
UNITS = TOK // UT
TPU = UT // P
TILES = TOK // P
SG = 4
NSG = NS // SG
NCH = NSG * NH
NE, TOPK = 32, 4
HS = P * TOPK
HST = HS // P
SLOT_TILES = TOK * TOPK // P + NE
SLOTS = SLOT_TILES * P
GT = 4
GROUPS = SLOT_TILES // GT
EPS = 1e-5
EXP_LN = "natural_log_exp_and_others"
A_RING, H_RING = 2, 4
B, C = 0, 1
ARENA_COLS = (A_RING + H_RING + 4) * SG * UT
POOL_CMUL = (3, 7)


def at(u, n):
    return isinstance(u, int) and u == n


def has(u):
    return not isinstance(u, int) or 0 <= u < UNITS


def pause(eng, scratch, place):
    eng.tensor_tensor(scratch[:, place:place + 1], scratch[:, 0:1], scratch[:, 0:1], ALU.mult)


def mamba_moe_kernel(nc, x, W_inT, w_convT, b_conv, W_x, W_xT, W_dtT, b_dt, A_log, Dv, W_outT,
                     routerT, router_bias, gate_upT, downT, sgateT, supT, sdownT,
                     sel, ident, upper, out):
    xs_dram = nc.dram_tensor("xs_scratch", (SLOTS, DM), F32, kind="Internal").ap()
    ys_dram = nc.dram_tensor("ys_scratch", (SLOTS, DM), F32, kind="Internal").ap()
    xn2_dram = nc.dram_tensor("xn2_scratch", (TOK, DM), F32, kind="Internal").ap()
    xn2T_dram = nc.dram_tensor("xn2T_scratch", (UNITS * P, UT), F32, kind="Internal").ap()

    def unit_rows(dram, u):
        return dram[bass.ds(u * UT, UT), :].rearrange("(j p) d -> p j d", p=P)

    with ExitStack() as ctx:
        def sb(name, shape, dt=F32):
            return ctx.enter_context(nc.sbuf_tensor(name, shape, dt))

        def sem(name):
            return ctx.enter_context(nc.semaphore(name))

        X2 = sb("X2", [P, TILES, DM])
        LG = sb("LG", [P, TILES, NE])
        V8 = sb("V8", [P, TILES, 8])
        I8 = sb("I8", [P, TILES, 8], U32)
        IDX = sb("IDX", [P, TILES * TOPK], U32)
        WT = sb("WT", [P, TILES, TOPK])

        idf = sb("idf", [P, P])
        eps = sb("eps", [P, 1])
        s_eps = sem("s_eps")
        scratch = sb("scratch", [P, 16])
        ARENA = sb("ARENA", [P, ARENA_COLS])

        with ExitStack() as m:
            def msb(name, shape, dt=F32):
                return m.enter_context(nc.sbuf_tensor(name, shape, dt))

            def msem(name):
                return m.enter_context(nc.semaphore(name))

            CW = SG * UT

            def ring(base, n):
                return [ARENA[:, base + i * CW:base + (i + 1) * CW].rearrange("p (s t) -> p s t", s=SG)
                        for i in range(n)]

            decay = ring(0, A_RING)
            state = ring(A_RING * CW, H_RING)
            Bbc = ring((A_RING + H_RING) * CW, 2)
            Cbc = ring((A_RING + H_RING + 2) * CW, 2)
            setup = ARENA[:, (A_RING + H_RING) * CW:(A_RING + H_RING + 4) * CW]
            self32 = setup[0:3 * 2 * NS, 0:2 * NS * P]
            o = 2 * NS * P
            winx = setup[:, o:o + DI]
            wcv = setup[:, o + DI:o + DI + KC * DI]
            o += DI + KC * DI
            wxd = setup[:, o:o + NH * DI].rearrange("p (h c) -> p h c", h=NH)
            o += NH * DI
            wdt = setup[:, o:o + NH * DI].rearrange("p (h c) -> p h c", h=NH)
            winz = msb("winz", [P, DI])
            wcomb = msb("wcomb", [P, KC, DI])
            bcv = msb("bcv", [P, NH])
            bdt = msb("bdt", [P, NH])
            wbc = msb("wbc", [P, NH, 3, 2 * NS])
            wdelta = msb("wdelta", [P, NH, DI])
            Apos = msb("Apos", [P, NH, NS])
            Aneg = msb("Aneg", [P, NH, NS])
            Dsb = msb("Dsb", [P, NH])
            wout = msb("wout", [P, NH, DM])
            wr = msb("wr", [P, NE])
            rbias = msb("rbias", [P, NE])
            selb = msb("selb", [3 * 2 * NS, 2 * NS, P], BF16)
            zrow = msb("zrow", [P, 1024])

            xst = msb("xst", [P, TPU, 6])
            xmv = msb("xmv", [P, TPU, 2])
            xln = msb("xln", [P, TPU])
            xrs = msb("xrs", [P, TPU])
            xn = msb("xn", [P, TPU, DM])
            xnT = msb("xnT", [P, UB, KC - 1 + SEQ])
            xc = msb("xc", [P, 2, NH, UT])
            sz = msb("sz", [P, 2, NH, UT])
            dl = msb("dl", [P, 2, NH, UB, SEQ])
            dtmp = msb("dtmp", [P, NH, UT])
            bcs = msb("bcs", [96, 2, UT], BF16)
            r1 = msb("r1", [96, UT])
            r2 = msb("r2", [96, UT])
            yg = msb("yg", [P, NH, UT])
            mst = msb("mst", [P, TPU, 6])
            mmv = msb("mmv", [P, TPU, 2])
            mln = msb("mln", [P, TPU])
            mrs = msb("mrs", [P, TPU])
            mo = msb("mo", [P, TPU, DM])
            nst = msb("nst", [P, TPU, 6])
            nmv = msb("nmv", [P, TPU, 2])
            nln = msb("nln", [P, TPU])
            nrs = msb("nrs", [P, TPU])
            xn2 = msb("xn2", [P, TPU, DM])
            xn2T = msb("xn2T", [P, UT])
            lgs = msb("lgs", [P, TPU, NE])
            v8s = msb("v8s", [P, TPU, 8])
            i8s = msb("i8s", [P, TPU, 8], U32)

            Y = [m.enter_context(nc.psum_tensor(f"Y{h}", [P, UT], F32)) for h in range(NH)]
            BCP = [m.enter_context(nc.psum_tensor(f"BCP{i}", [P, UT], F32)) for i in range(3)]
            BCP_OF, BCP_AGO = (0, 1, 2, 1), (4, 2, 4, 2)
            PJ = [m.enter_context(nc.psum_tensor(f"PJ{i}", [P, UT], F32)) for i in range(2)]
            PK = m.enter_context(nc.psum_tensor("PK", [P, UT], F32))

            s_w = msem("s_w")
            s_x0, s_x1, s_xr = msem("s_x0"), msem("s_x1"), msem("s_xr")
            s_set = msem("s_set")
            s_wc = msem("s_wc")
            s_wdm, s_wdc = msem("s_wdm"), msem("s_wdc")
            s_ap, s_an = msem("s_ap"), msem("s_an")
            s_zero = msem("s_zero")
            s_xst, s_xmv, s_xln, s_xrs, s_xn = (msem(n) for n in ("s_xst", "s_xmv", "s_xln", "s_xrs", "s_xn"))
            s_T, s_xnT = msem("s_T"), msem("s_xnT")
            s_pc = [msem(f"s_pc{h}") for h in range(NH)]
            s_xc = [msem(f"s_xc{h}") for h in range(NH)]
            s_pz = [msem(f"s_pz{h}") for h in range(NH)]
            s_sz = [msem(f"s_sz{h}") for h in range(NH)]
            s_pbc, s_hi, s_r1 = msem("s_pbc"), msem("s_hi"), msem("s_r1")
            s_mid, s_r2, s_bcs = msem("s_mid"), msem("s_r2"), msem("s_bcs")
            s_pd = [msem(f"s_pd{h}") for h in range(NH)]
            s_dm = [msem(f"s_dm{h}") for h in range(NH)]
            s_de = [msem(f"s_de{h}") for h in range(NH)]
            s_dn = [msem(f"s_dn{h}") for h in range(NH)]
            s_dl = [msem(f"s_dl{h}") for h in range(NH)]
            s_bp, s_bcp = msem("s_bp"), msem("s_bcp")
            s_exp, s_bx, s_scan = msem("s_exp"), msem("s_bx"), msem("s_scan")
            s_cmv, s_cmp = msem("s_cmv"), msem("s_cmp")
            s_sum = msem("s_sum")
            s_yd, s_yg, s_po = msem("s_yd"), msem("s_yg"), msem("s_po")
            s_mst, s_mmv, s_mln, s_mrs, s_mo = (msem(n) for n in ("s_mst", "s_mmv", "s_mln", "s_mrs", "s_mo"))
            s_res, s_nst, s_nmv, s_nln, s_nrs = (msem(n) for n in ("s_res", "s_nst", "s_nmv", "s_nln", "s_nrs"))
            s_xn2, s_T2, s_xn2T = msem("s_xn2"), msem("s_T2"), msem("s_xn2T")
            s_pl, s_lg, s_v8, s_i8, s_keep = (msem(n) for n in ("s_pl", "s_lg", "s_v8", "s_i8", "s_keep"))
            s_stx, s_stT = msem("s_stx"), msem("s_stT")

            NWD = 20

            def nvec(u, c):
                p = sum(k < c for k in POOL_CMUL)
                return u * (NCH - len(POOL_CMUL)) + c - p

            def npool(u, c):
                return u * len(POOL_CMUL) + sum(k < c for k in POOL_CMUL)

            block = m.enter_context(nc.Block())

            @block.sync
            def _(sp):
                sp.dma_start(X2[:, 0:TPU, :], unit_rows(x, 0)).then_inc(s_x0, 16)
                loads = [
                    (winx, W_inT[:, 0:DI]), (winz[:], W_inT[:, DI:2 * DI]),
                    (wcv, w_convT.rearrange("k c -> (k c)").partition_broadcast(P)),
                    (bcv[:], b_conv),
                    (bdt[:], b_dt),
                    (wxd, W_x[0:DI, :].rearrange("(h p) c -> p h c", p=P)),
                    (wdt, W_dtT.rearrange("(h p) c -> p h c", p=P)),
                    (Apos[:], A_log.rearrange("(h p) s -> p h s", p=P)),
                    (Dsb[:], Dv),
                    (wout[:], W_outT.rearrange("(h p) c -> p h c", p=P)),
                    (wr[:], routerT), (rbias[:], router_bias.partition_broadcast(P)),
                    (self32, sel), (idf[:], ident),
                ] + [(wbc[:, h, r, :], W_xT[h * P:(h + 1) * P, DI:DI + 2 * NS]) for h in range(NH) for r in range(3)]
                assert len(loads) == NWD
                for dst, src in loads:
                    sp.dma_start(dst, src).then_inc(s_w, 16)
                sp.dma_start(X2[:, TPU:2 * TPU, :], unit_rows(x, 1)).then_inc(s_x1, 16)
                sp.dma_start(X2[:, 2 * TPU:TILES, :],
                             x[2 * UT:TOK, :].rearrange("(j p) d -> p j d", p=P)).then_inc(s_xr, 16)
                sp.wait_ge(s_set, 1)
                for z in range(SLOT_TILES // 8):
                    sp.dma_start(xs_dram[z * 8 * P:(z + 1) * 8 * P, :].rearrange("(p r) d -> p (r d)", p=P),
                                 zrow[:]).then_inc(s_zero, 16)

                def store(u):
                    sp.wait_ge(s_xn2, u + 1)
                    sp.dma_start(unit_rows(xn2_dram, u), xn2[:]).then_inc(s_stx, 16)
                    sp.wait_ge(s_xn2T, u + 1)
                    sp.dma_start(xn2T_dram[bass.ds(u * P, P), :], xn2T[:]).then_inc(s_stT, 16)
                with sp.Fori(0, UNITS) as u:
                    store(u)
                sp.wait_ge(s_stx, 16 * UNITS)
                sp.wait_ge(s_stT, 16 * UNITS)
                sp.wait_ge(s_zero, 16 * (SLOT_TILES // 8))

            @block.tensor
            def _(pe):
                pe.wait_ge(s_w, 16 * NWD)
                for kc in range(NH):
                    for mm in range(NH):
                        last = pe.matmul(PJ[kc][:, 0:DI], wxd[:, mm, kc * P:(kc + 1) * P], wdt[:, mm, :],
                                         start=mm == 0, stop=mm == NH - 1)
                    last.then_inc(s_wdm, 1)

                def transposed(f):
                    if not has(f):
                        return
                    pe.wait_ge(s_xn, f + 1)
                    if at(f, 0):
                        pe.wait_ge(s_wdc, NH)
                    else:
                        pe.wait_ge(s_dl[0], f)
                    for j in range(TPU):
                        t = pe.transpose(PJ[1][:, j * P:(j + 1) * P], xn[:, j, :], idf[:])
                    t.then_inc(s_T, 1)

                def project_x(f, h):
                    if not has(f):
                        return
                    if h == 0:
                        pe.wait_ge(s_xnT, f + 1)
                        if at(f, 0):
                            pe.wait_ge(s_wc, KC)
                        else:
                            pe.wait_ge(s_dl[1], f)
                    for k in range(KC):
                        t = pe.matmul(PJ[h][:].rearrange("p (b t) -> p b t", b=UB),
                                      wcomb[:, k, h * P:(h + 1) * P],
                                      xnT[:, :, k:k + SEQ], start=k == 0, stop=k == KC - 1)
                    t.then_inc(s_pc[h], 1)

                def project_z(f, h):
                    if not has(f):
                        return
                    pe.wait_ge(s_xc[h], f + 1)
                    pe.matmul(PJ[h][:].rearrange("p (b t) -> p b t", b=UB), winz[:, h * P:(h + 1) * P],
                              xnT[:, :, KC - 1:KC - 1 + SEQ], start=True, stop=True).then_inc(s_pz[h], 1)

                def project_bc(f, par):
                    if not has(f):
                        return
                    pe.wait_ge(s_sz[0], f + 1)
                    for h in range(NH):
                        t = pe.matmul(PJ[0][0:96, :], wbc[:, h, :, :].rearrange("p r n -> p (r n)"),
                                      xc[:, par, h, :], start=h == 0, stop=h == NH - 1)
                    t.then_inc(s_pbc, 1)

                def project_delta(f, par, o):
                    if not has(f):
                        return
                    if o == 0:
                        pe.wait_ge(s_sz[1], f + 1)
                    else:
                        pe.wait_ge(s_r1, f + 1)
                    for h in range(NH):
                        t = pe.matmul(PJ[1 - o][:], wdelta[:, h, o * P:(o + 1) * P], xc[:, par, h, :],
                                      start=h == 0, stop=h == NH - 1)
                    t.then_inc(s_pd[o], 1)

                def broadcast(u, par, sg, which, *rows):
                    if not has(u):
                        return
                    for i in rows:
                        if which == B and sg == 0 and i == 0:
                            pe.wait_ge(s_bcs, u + 1)
                        k = (sg * 2 + which) * SG + i
                        if not (at(u, 0) and k < BCP_AGO[i]):
                            pe.wait_ge(s_bcp, u * (2 * NS) + k - BCP_AGO[i] + 1)
                        pe.matmul(BCP[BCP_OF[i]][:], selb[:, which * NS + sg * SG + i, :], bcs[:, par, :],
                                  start=True, stop=True).then_inc(s_bp, 1)

                def sum_states(u, c):
                    if not has(u):
                        return
                    sg, h = c // NH, c % NH
                    if c in POOL_CMUL:
                        pe.wait_ge(s_cmp, npool(u, c) + 1)
                    else:
                        pe.wait_ge(s_cmv, nvec(u, c) + 1)
                    if sg == 0 and not at(u, 0):
                        pe.wait_ge(s_yd, u * NH - 1 + h)
                    for s in range(SG):
                        t = pe.matmul(Y[h][:], idf[:], state[c % H_RING][:, s, :],
                                      start=sg == 0 and s == 0, stop=sg == NSG - 1 and s == SG - 1)
                    t.then_inc(s_sum, 1)

                def out_proj(b):
                    if not has(b):
                        return
                    pe.wait_ge(s_yg, b + 1)
                    if not at(b, 0):
                        pe.wait_ge(s_lg, b)
                    for j in range(TPU):
                        for h in range(NH):
                            t = pe.matmul(PK[:, j * P:(j + 1) * P], yg[:, h, j * P:(j + 1) * P], wout[:, h, :],
                                          start=h == 0, stop=h == NH - 1)
                    t.then_inc(s_po, 1)

                def transposed2(b):
                    if not has(b):
                        return
                    pe.wait_ge(s_xn2, b + 1)
                    for j in range(TPU):
                        t = pe.transpose(PK[:, j * P:(j + 1) * P], xn2[:, j, :], idf[:])
                    t.then_inc(s_T2, 1)

                def logits(b):
                    if not has(b):
                        return
                    pe.wait_ge(s_xn2T, b + 1)
                    for j in range(TPU):
                        t = pe.matmul(PK[:, j * NE:(j + 1) * NE], xn2T[:, j * P:(j + 1) * P], wr[:],
                                      start=True, stop=True)
                    t.then_inc(s_pl, 1)

                def body(u, par):
                    broadcast(u, par, 1, B, 0)
                    transposed(u + 1)
                    broadcast(u, par, 1, B, 1, 2)
                    sum_states(u - 1, 6)
                    broadcast(u, par, 1, B, 3)
                    broadcast(u, par, 1, C, 0)
                    project_x(u + 1, 0)
                    broadcast(u, par, 1, C, 1, 2)
                    sum_states(u - 1, 7)
                    broadcast(u, par, 1, C, 3)
                    broadcast(u, par, 2, B, 0)
                    project_x(u + 1, 1)
                    broadcast(u, par, 2, B, 1)
                    logits(u - 2)
                    broadcast(u, par, 2, B, 2)
                    sum_states(u, 0)
                    broadcast(u, par, 2, B, 3)
                    project_z(u + 1, 0)
                    broadcast(u, par, 2, C, 0)
                    project_z(u + 1, 1)
                    broadcast(u, par, 2, C, 1, 2)
                    sum_states(u, 1)
                    broadcast(u, par, 2, C, 3)
                    broadcast(u, par, 3, B, 0)
                    out_proj(u - 1)
                    broadcast(u, par, 3, B, 1)
                    project_bc(u + 1, 1 - par)
                    broadcast(u, par, 3, B, 2)
                    sum_states(u, 2)
                    broadcast(u, par, 3, B, 3)
                    project_delta(u + 1, 1 - par, 0)
                    broadcast(u, par, 3, C, 0, 1, 2)
                    sum_states(u, 3)
                    broadcast(u, par, 3, C, 3)
                    broadcast(u + 1, 1 - par, 0, B, 0)
                    project_delta(u + 1, 1 - par, 1)
                    broadcast(u + 1, 1 - par, 0, B, 1, 2)
                    sum_states(u, 4)
                    broadcast(u + 1, 1 - par, 0, B, 3)
                    transposed2(u - 1)
                    broadcast(u + 1, 1 - par, 0, C, 0, 1, 2)
                    sum_states(u, 5)
                    broadcast(u + 1, 1 - par, 0, C, 3)

                for n in range(-2, 3):
                    body(n, n % 2)
                with pe.Fori(1, UNITS // 2 - 2) as pair:
                    u = pair * 2 + 1
                    body(u, 1)
                    body(u + 1, 0)
                for n in range(UNITS - 3, UNITS + 2):
                    body(n, n % 2)

            @block.scalar
            def _(act):
                act.wait_ge(s_eps, 2)
                act.wait_ge(s_set, 4)
                act.wait_ge(s_w, 16 * NWD)
                act.activation(Apos[:], Apos[:], ACT.Exp).then_inc(s_ap, 1)
                act.activation(selb[:], self32.rearrange("p (s m) -> p s m", s=2 * NS), ACT.Copy).then_inc(s_ap, 1)
                for kc in range(NH):
                    act.wait_ge(s_wdm, kc + 1)
                    act.activation(wdelta[:, kc, :], PJ[kc][:, 0:DI], ACT.Copy).then_inc(s_wdc, 1)

                def rstd(var, ln, rs, s_mv, s_ln, s_rs, u):
                    if not has(u):
                        return
                    act.wait_ge(s_mv, u + 1)
                    act.activation(ln[:], var[:, :, 1], ACT.Ln, bias=eps[:]).then_inc(s_ln, 1)
                    act.wait_ge(s_ln, u + 1)
                    act.activation(rs[:], ln[:], ACT.Exp, scale=-0.5).then_inc(s_rs, 1)

                def copy_xnT(f):
                    if not has(f):
                        return
                    act.wait_ge(s_T, f + 1)
                    if not at(f, 0):
                        for h in range(NH):
                            act.wait_ge(s_pz[h], f)
                    act.activation(xnT[:, :, KC - 1:KC - 1 + SEQ], PJ[1][:].rearrange("p (b t) -> p b t", b=UB),
                                   ACT.Copy).then_inc(s_xnT, 1)

                def silu_x(f, par, h):
                    if not has(f):
                        return
                    if h == 0 and not (at(f, 0) or at(f, 1)):
                        act.wait_ge(s_yg, f - 1)
                    act.wait_ge(s_pc[h], f + 1)
                    act.activation(xc[:, par, h, :], PJ[h][:], ACT.Silu, bias=bcv[:, h:h + 1]).then_inc(s_xc[h], 1)

                def silu_z(f, par, h):
                    if not has(f):
                        return
                    act.wait_ge(s_pz[h], f + 1)
                    act.activation(sz[:, par, h, :], PJ[h][:], ACT.Silu).then_inc(s_sz[h], 1)
                    if h == NH - 1:
                        act.preload_act_table_set(EXP_LN)

                def exp_delta(f, h):
                    if not has(f):
                        return
                    act.wait_ge(s_dm[h], f + 1)
                    act.activation(dtmp[:, h, :], dtmp[:, h, :], ACT.Exp).then_inc(s_de[h], 1)

                def ln_delta(f, h):
                    if not has(f):
                        return
                    act.wait_ge(s_de[h], f + 1)
                    act.activation(dtmp[:, h, :], dtmp[:, h, :], ACT.Ln, bias=1.0).then_inc(s_dn[h], 1)

                def copies(u, sg, which, *rows):
                    if not has(u):
                        return
                    for i in rows:
                        k = (sg * 2 + which) * SG + i
                        act.wait_ge(s_bp, u * (2 * NS) + k + 1)
                        if i == 0 and not (at(u, 0) and sg < 2):
                            v, c = (u, (sg - 1) * NH) if sg else (u - 1, NCH - NH)
                            if which == B:
                                act.wait_ge(s_bx, v * NCH + c)
                            else:
                                act.wait_ge(s_cmv, nvec(v, c))
                                if not at(npool(v, c), 0):
                                    act.wait_ge(s_cmp, npool(v, c))
                        act.activation((Bbc, Cbc)[which][sg % 2][:, i, :], BCP[BCP_OF[i]][:],
                                       ACT.Copy).then_inc(s_bcp, 1)

                def decays(u, par, c):
                    if not has(u):
                        return
                    sg, h = c // NH, c % NH
                    if sg == 0:
                        act.wait_ge(s_dl[h], u + 1)
                    if not (at(u, 0) and c < A_RING):
                        act.wait_ge(s_scan, u * NCH + c - A_RING + 1)
                    a = decay[c % A_RING].rearrange("p s (b t) -> p s b t", b=UB)
                    for s in range(SG):
                        t = act.activation(a[:, s, :, 1:SEQ], dl[:, par, h, :, 1:SEQ], ACT.Exp,
                                           scale=Aneg[:, h, sg * SG + s:sg * SG + s + 1])
                    t.then_inc(s_exp, 1)

                def copy_xn2T(b):
                    if not has(b):
                        return
                    act.wait_ge(s_T2, b + 1)
                    if not at(b, 0):
                        act.wait_ge(s_stT, 16 * b)
                        act.wait_ge(s_pl, b)
                    act.activation(xn2T[:], PK[:], ACT.Copy).then_inc(s_xn2T, 1)

                def body(u, par):
                    copy_xnT(u + 1)
                    copies(u, 1, B, 0, 1)
                    decays(u, par, 1)
                    copies(u, 1, B, 2, 3)
                    decays(u, par, 2)
                    copies(u, 1, C, 0, 1)
                    copy_xn2T(u - 2)
                    copies(u, 1, C, 2)
                    rstd(xmv, xln, xrs, s_xmv, s_xln, s_xrs, u + 2)
                    copies(u, 1, C, 3)
                    copies(u, 2, B, 0)
                    decays(u, par, 3)
                    copies(u, 2, B, 1)
                    silu_x(u + 1, 1 - par, 0)
                    silu_x(u + 1, 1 - par, 1)
                    copies(u, 2, B, 2, 3)
                    copies(u, 2, C, 0)
                    silu_z(u + 1, 1 - par, 0)
                    copies(u, 2, C, 1, 2)
                    silu_z(u + 1, 1 - par, 1)
                    copies(u, 2, C, 3)
                    decays(u, par, 4)
                    copies(u, 3, B, 0)
                    rstd(mmv, mln, mrs, s_mmv, s_mln, s_mrs, u - 1)
                    copies(u, 3, B, 1)
                    decays(u, par, 5)
                    copies(u, 3, B, 2, 3)
                    copies(u, 3, C, 0, 1)
                    decays(u, par, 6)
                    exp_delta(u + 1, 0)
                    copies(u, 3, C, 2)
                    rstd(nmv, nln, nrs, s_nmv, s_nln, s_nrs, u - 1)
                    copies(u, 3, C, 3)
                    copies(u + 1, 0, B, 0, 1)
                    decays(u, par, 7)
                    copies(u + 1, 0, B, 2)
                    ln_delta(u + 1, 0)
                    copies(u + 1, 0, B, 3)
                    exp_delta(u + 1, 1)
                    ln_delta(u + 1, 1)
                    copies(u + 1, 0, C, 0, 1, 2, 3)
                    decays(u + 1, 1 - par, 0)

                act.wait_ge(s_an, 1)
                act.wait_ge(s_ap, 2)
                act.preload_act_table_set(EXP_LN)
                for n in range(-2, 3):
                    body(n, n % 2)
                with act.Fori(1, UNITS // 2 - 2) as pair:
                    u = pair * 2 + 1
                    act.preload_act_table_set(EXP_LN)
                    body(u, 1)
                    body(u + 1, 0)
                for n in range(UNITS - 3, UNITS + 2):
                    body(n, n % 2)

            @block.gpsimd
            def _(pool):
                zero = scratch[:, 0:1].to_broadcast([P, UT])

                def parts(f, par):
                    if not has(f):
                        return
                    if not at(f, 0):
                        pool.wait_ge(s_bx, (f - 1) * NCH + 6)
                        if len(POOL_CMUL):
                            pool.wait_ge(s_cmp, npool(f - 1, 5))
                    pool.wait_ge(s_r1, f + 1)
                    pool.tensor_tensor(bcs[32:64, par, :], r1[32:64, :], zero[32:64], ALU.add).then_inc(s_mid, 1)
                    pool.wait_ge(s_mid, 2 * f + 1)
                    pool.tensor_tensor(bcs[64:96, par, :], r1[64:96, :], zero[64:96], ALU.add).then_inc(s_mid, 1)
                    pool.wait_ge(s_mid, 2 * f + 2)
                    pool.tensor_tensor(r2[64:96, :], r1[64:96, :], bcs[64:96, par, :], ALU.subtract).then_inc(s_r2, 1)
                    pool.wait_ge(s_r2, f + 1)
                    pool.tensor_tensor(bcs[64:96, par, :], r2[64:96, :], zero[64:96], ALU.add).then_inc(s_bcs, 1)
                    pool.wait_ge(s_bcs, f + 1)

                def times_b(u, par, c):
                    if not has(u):
                        return
                    sg, h = c // NH, c % NH
                    n = u * NCH + c
                    if sg == 0:
                        pool.wait_ge(s_xc[h], u + 1)
                    pool.wait_ge(s_bcp, u * (2 * NS) + (sg * 2 + 1) * SG)
                    if not (at(u, 0) and c < H_RING):
                        pool.wait_ge(s_sum, n - H_RING + 1)
                    pool.tensor_tensor(state[c % H_RING], Bbc[sg % 2],
                                       xc[:, par, h, :].unsqueeze(1).to_broadcast([P, SG, UT]),
                                       ALU.mult).then_inc(s_bx, 1)

                def times_c(u, c):
                    if not has(u):
                        return
                    sg = c // NH
                    pool.wait_ge(s_scan, u * NCH + c + 1)
                    pool.wait_ge(s_bcp, u * (2 * NS) + (sg * 2 + 2) * SG)
                    pool.tensor_tensor(state[c % H_RING], state[c % H_RING], Cbc[sg % 2], ALU.mult).then_inc(s_cmp, 1)

                def body(u, par):
                    times_b(u, par, 0)
                    times_c(u - 1, 7)
                    times_b(u, par, 1)
                    times_b(u, par, 2)
                    times_b(u, par, 3)
                    times_b(u, par, 4)
                    times_c(u, 3)
                    times_b(u, par, 5)
                    parts(u + 1, 1 - par)
                    times_b(u, par, 6)
                    times_b(u, par, 7)

                pool.wait_ge(s_eps, 2)
                for n in range(-2, 3):
                    body(n, n % 2)
                with pool.Fori(1, UNITS // 2 - 2) as pair:
                    u = pair * 2 + 1
                    body(u, 1)
                    body(u + 1, 0)
                for n in range(UNITS - 3, UNITS + 2):
                    body(n, n % 2)

            @block.vector
            def _(dve):
                dve.memset(eps[:], EPS).then_inc(s_eps, 1)
                dve.memset(scratch[:], 0.0).then_inc(s_eps, 1)
                dve.memset(zrow[:], 0.0).then_inc(s_set, 1)
                dve.memset(xnT[:], 0.0).then_inc(s_set, 1)
                for a in decay:
                    dve.memset(a, 0.0).then_inc(s_set, 1)
                dve.wait_ge(s_w, 16 * NWD)
                for k in range(KC):
                    dve.tensor_tensor(wcomb[:, k, :], winx, wcv[:, k * DI:(k + 1) * DI], ALU.mult).then_inc(s_wc, 1)
                dve.wait_ge(s_ap, 1)
                dve.tensor_scalar(Aneg[:], Apos[:], -1.0, None, ALU.mult).then_inc(s_an, 1)

                def x2_tile(u, j):
                    return X2[:, bass.ds(u * TPU + j, 1), :].rearrange("p j d -> p (j d)")

                def moments(src, st, mv, s_st, s_mv, u):
                    for j in range(TPU):
                        t = dve.bn_stats(st[:, j, :], src(j))
                    t.then_inc(s_st, 1)
                    dve.wait_ge(s_st, u + 1)
                    pause(dve, scratch, 1)
                    for j in range(TPU):
                        t = dve.bn_aggr(mv[:, j, :], st[:, j, :])
                    t.then_inc(s_mv, 1)

                def normalise(dst, src, mv, rs, s_rs, s_done, u):
                    dve.wait_ge(s_rs, u + 1)
                    for j in range(TPU):
                        t = dve.tensor_scalar(dst(j), src(j), mv[:, j, 0:1], rs[:, j:j + 1], ALU.subtract, ALU.mult)
                    t.then_inc(s_done, 1)

                def x_moments(f):
                    if not has(f):
                        return
                    if at(f, 0):
                        dve.wait_ge(s_x0, 16)
                    elif at(f, 1):
                        dve.wait_ge(s_x1, 16)
                    else:
                        dve.wait_ge(s_xr, 16)
                    moments(lambda j: x2_tile(f, j), xst, xmv, s_xst, s_xmv, f)

                def x_norm(f):
                    if not has(f):
                        return
                    if not at(f, 0):
                        dve.wait_ge(s_T, f)
                    normalise(lambda j: xn[:, j, :], lambda j: x2_tile(f, j), xmv, xrs, s_xrs, s_xn, f)

                def high_parts(f, par):
                    if not has(f):
                        return
                    dve.wait_ge(s_pbc, f + 1)
                    if not at(f, 0):
                        dve.wait_ge(s_bcs, f)
                    dve.tensor_copy(bcs[:, par, :], PJ[0][0:96, :]).then_inc(s_hi, 1)
                    dve.wait_ge(s_hi, f + 1)
                    dve.tensor_tensor(r1[:], PJ[0][0:96, :], bcs[:, par, :], ALU.subtract).then_inc(s_r1, 1)

                def delta_min(f, h):
                    if not has(f):
                        return
                    dve.wait_ge(s_pd[h], f + 1)
                    dve.tensor_scalar(dtmp[:, h, :], PJ[1 - h][:], bdt[:, h:h + 1], 40.0,
                                      ALU.add, ALU.min).then_inc(s_dm[h], 1)

                def delta_max(f, par, h):
                    if not has(f):
                        return
                    dve.wait_ge(s_dn[h], f + 1)
                    dve.scalar_tensor_tensor(out=dl[:, par, h, :, :].rearrange("p b t -> p (b t)"),
                                             in0=PJ[1 - h][:], scalar=bdt[:, h:h + 1], in1=dtmp[:, h, :],
                                             op0=ALU.add, op1=ALU.max).then_inc(s_dl[h], 1)

                def scan(u, c):
                    if not has(u):
                        return
                    n = u * NCH + c
                    dve.wait_ge(s_bx, n + 1)
                    dve.wait_ge(s_exp, n + 1)
                    st = state[c % H_RING].rearrange("p s t -> p (s t)")
                    dve.tensor_tensor_scan(st, decay[c % A_RING].rearrange("p s t -> p (s t)"), st,
                                           0.0, ALU.mult, ALU.add).then_inc(s_scan, 1)

                def times_c(u, c):
                    if not has(u):
                        return
                    sg = c // NH
                    dve.wait_ge(s_scan, u * NCH + c + 1)
                    dve.wait_ge(s_bcp, u * (2 * NS) + (sg * 2 + 2) * SG)
                    dve.tensor_tensor(state[c % H_RING], state[c % H_RING], Cbc[sg % 2], ALU.mult).then_inc(s_cmv, 1)

                def add_d(b, par, h):
                    if not has(b):
                        return
                    dve.wait_ge(s_sum, b * NCH + NCH - 1 + h)
                    if not at(b, 0):
                        dve.wait_ge(s_po, b)
                    dve.scalar_tensor_tensor(out=yg[:, h, :], in0=xc[:, par, h, :], scalar=Dsb[:, h:h + 1],
                                             in1=Y[h][:], op0=ALU.mult, op1=ALU.add).then_inc(s_yd, 1)

                def gate(b, par):
                    if not has(b):
                        return
                    dve.wait_ge(s_yd, (b + 1) * NH)
                    dve.tensor_tensor(yg[:], yg[:], sz[:, par, :, :], ALU.mult).then_inc(s_yg, 1)

                def out_moments(b):
                    if not has(b):
                        return
                    dve.wait_ge(s_po, b + 1)
                    pause(dve, scratch, 2)
                    moments(lambda j: PK[:, j * P:(j + 1) * P], mst, mmv, s_mst, s_mmv, b)

                def out_norm(b):
                    if not has(b):
                        return
                    normalise(lambda j: mo[:, j, :], lambda j: PK[:, j * P:(j + 1) * P], mmv, mrs, s_mrs, s_mo, b)

                def residual(b):
                    if not has(b):
                        return
                    dve.wait_ge(s_mo, b + 1)
                    rows = X2[:, bass.ds(b * TPU, TPU), :]
                    dve.tensor_tensor(rows, rows, mo[:], ALU.add).then_inc(s_res, 1)
                    dve.wait_ge(s_res, b + 1)
                    pause(dve, scratch, 3)
                    moments(lambda j: x2_tile(b, j), nst, nmv, s_nst, s_nmv, b)

                def norm2(b):
                    if not has(b):
                        return
                    if not at(b, 0):
                        dve.wait_ge(s_stx, 16 * b)
                        dve.wait_ge(s_T2, b)
                    normalise(lambda j: xn2[:, j, :], lambda j: x2_tile(b, j), nmv, nrs, s_nrs, s_xn2, b)

                def pick(b):
                    if not has(b):
                        return
                    dve.wait_ge(s_pl, b + 1)
                    if not at(b, 0):
                        dve.wait_ge(s_keep, b)
                    dve.tensor_tensor(lgs[:], PK[:, 0:TPU * NE].rearrange("p (j e) -> p j e", j=TPU),
                                      rbias[:].unsqueeze(1).to_broadcast([P, TPU, NE]), ALU.add).then_inc(s_lg, 1)
                    dve.wait_ge(s_lg, b + 1)
                    pause(dve, scratch, 4)
                    for j in range(TPU):
                        t = dve.max(v8s[:, j, :], lgs[:, j, :])
                    t.then_inc(s_v8, 1)
                    dve.wait_ge(s_v8, b + 1)
                    pause(dve, scratch, 5)
                    for j in range(TPU):
                        t = dve.max_index(i8s[:, j, :], v8s[:, j, :], lgs[:, j, :])
                    t.then_inc(s_i8, 1)
                    dve.tensor_copy(LG[:, bass.ds(b * TPU, TPU), :], lgs[:])
                    dve.tensor_copy(V8[:, bass.ds(b * TPU, TPU), :], v8s[:])
                    dve.wait_ge(s_i8, b + 1)
                    dve.tensor_copy(I8[:, bass.ds(b * TPU, TPU), :], i8s[:]).then_inc(s_keep, 1)

                def body(u, par):
                    x_moments(u + 2)
                    scan(u, 0)
                    scan(u, 1)
                    x_norm(u + 2)
                    add_d(u - 1, 1 - par, 0)
                    times_c(u, 0)
                    add_d(u - 1, 1 - par, 1)
                    gate(u - 1, 1 - par)
                    scan(u, 2)
                    times_c(u, 1)
                    scan(u, 3)
                    pick(u - 2)
                    times_c(u, 2)
                    out_moments(u - 1)
                    high_parts(u + 1, 1 - par)
                    scan(u, 4)
                    out_norm(u - 1)
                    scan(u, 5)
                    delta_min(u + 1, 0)
                    residual(u - 1)
                    times_c(u, 4)
                    scan(u, 6)
                    norm2(u - 1)
                    times_c(u, 5)
                    delta_min(u + 1, 1)
                    scan(u, 7)
                    delta_max(u + 1, 1 - par, 0)
                    times_c(u, 6)
                    delta_max(u + 1, 1 - par, 1)

                for n in range(-2, 3):
                    body(n, n % 2)
                with dve.Fori(1, UNITS // 2 - 2) as pair:
                    u = pair * 2 + 1
                    body(u, 1)
                    body(u + 1, 0)
                for n in range(UNITS - 3, UNITS + 2):
                    body(n, n % 2)


        te_dram = nc.dram_tensor("te_scratch", (4 * P,), I32, kind="Internal").ap()
        with ExitStack() as r:
            def rsem(name):
                return r.enter_context(nc.semaphore(name))

            W = TILES * NE
            TC = -(-SLOT_TILES // P)

            def area(i, n=1):
                return ARENA[:, i * W:(i + n) * W]

            def by_tile(ap):
                return ap.rearrange("p (j e) -> p j e", e=NE)

            pick = [by_tile(area(k)) for k in range(TOPK)]
            oh = area(4)
            tmp = by_tile(area(5))
            tot = area(6)
            incl = area(7)
            scanm = area(8)
            pos = by_tile(area(9))

            def rsb(name, shape, dt=F32):
                return r.enter_context(nc.sbuf_tensor(name, shape, dt))

            up_sb, ones = rsb("up_sb", [P, P]), rsb("ones", [P, P])
            iei, ief = rsb("iei", [P, NE], I32), rsb("ief", [P, NE])
            i8f = rsb("i8f", [P, TILES, TOPK])
            ssum, srec = rsb("ssum", [P, TILES]), rsb("srec", [P, TILES])
            v4 = rsb("v4", [P, TILES, TOPK])
            wsum, wrec = rsb("wsum", [P, TILES]), rsb("wrec", [P, TILES])
            cnti, cnts = rsb("cnti", [P, NE], I32), rsb("cnts", [P, NE], I32)
            ntf, nti, base = rsb("ntf", [P, NE]), rsb("nti", [P, NE]), rsb("base", [P, NE])
            gi, gf = rsb("gi", [P, TC], I32), rsb("gf", [P, TC])
            cmp_ = rsb("cmp_", [P, TC, NE])
            tef, tei = rsb("tef", [P, TC]), rsb("tei", [P, TC], I32)
            idxf = rsb("idxf", [P, TILES, TOPK])
            PR = [r.enter_context(nc.psum_tensor(f"PR{i}", [P, W // 4], F32)) for i in range(4)]
            PT = [r.enter_context(nc.psum_tensor(f"PT{i}", [P, W // 4], F32)) for i in range(4)]

            s_c = rsem("s_c")
            s_iota = rsem("s_iota")
            s_v = rsem("s_v")
            s_oh, s_pr = rsem("s_oh"), rsem("s_pr")
            s_sub, s_ex = rsem("s_sub"), rsem("s_ex")
            s_tc, s_te, s_teo = rsem("s_tc"), rsem("s_te"), rsem("s_teo")
            block = r.enter_context(nc.Block())

            @block.sync
            def _(sp):
                sp.dma_start(up_sb[:], upper).then_inc(s_c, 16)
                sp.wait_ge(s_te, 1)
                with nc.allow_non_contiguous_dma(reason="a few hundred integers"):
                    sp.dma_start(te_dram[0:TC * P].rearrange("(c p) -> p c", p=P), tei[:]).then_inc(s_teo, 16)
                sp.wait_ge(s_teo, 16)

            @block.gpsimd
            def _(pool):
                pool.iota(iei[:], pattern=[[1, NE]], base=0, channel_multiplier=0).then_inc(s_iota, 1)
                pool.iota(gi[:], pattern=[[P, TC]], base=0, channel_multiplier=1).then_inc(s_iota, 1)

            @block.tensor
            def _(pe):
                pe.wait_ge(s_c, 16)
                pe.wait_ge(s_oh, 1)
                for i in range(4):
                    cols = oh[:, i * (W // 4):(i + 1) * (W // 4)]
                    pe.matmul(PR[i][:], up_sb[:], cols, start=True, stop=True)
                    pe.matmul(PT[i][:], ones[:], cols, start=True, stop=True).then_inc(s_pr, 1)

            @block.scalar
            def _(act):
                act.wait_ge(s_sub, 1)
                act.activation(tmp, tmp, ACT.Exp).then_inc(s_ex, 1)
                act.activation(v4[:], v4[:], ACT.Exp).then_inc(s_ex, 1)
                for i in range(4):
                    act.wait_ge(s_pr, i + 1)
                    act.activation(tot.rearrange("p (e j) -> p j e", j=TILES)[:, i * TILES // 4:(i + 1) * TILES // 4, :],
                                   PT[i][:].rearrange("p (j e) -> p j e", e=NE), ACT.Copy).then_inc(s_tc, 1)

            @block.vector
            def _(dve):
                steps = [0]

                def step(ins):
                    steps[0] += 1
                    ins.then_inc(s_v, 1)
                    dve.wait_ge(s_v, steps[0])

                dve.wait_ge(s_iota, 2)
                dve.tensor_copy(i8f[:], I8[:, :, 0:TOPK])
                dve.tensor_copy(gf[:], gi[:])
                dve.memset(ones[:], 1.0)
                step(dve.tensor_copy(ief[:], iei[:]))
                for k in range(TOPK):
                    step(dve.tensor_tensor(pick[k], ief[:].unsqueeze(1).to_broadcast([P, TILES, NE]),
                                           i8f[:, :, k:k + 1].to_broadcast([P, TILES, NE]), ALU.is_equal))
                step(dve.tensor_tensor(by_tile(oh), pick[0], pick[1], ALU.add))
                step(dve.tensor_tensor(by_tile(oh), by_tile(oh), pick[2], ALU.add))
                dve.tensor_tensor(by_tile(oh), by_tile(oh), pick[3], ALU.add).then_inc(s_oh, 1)
                dve.tensor_tensor(v4[:], V8[:, :, 0:TOPK], V8[:, :, 0:1].to_broadcast([P, TILES, TOPK]), ALU.subtract)
                dve.tensor_tensor(tmp, LG[:], V8[:, :, 0:1].to_broadcast([P, TILES, NE]), ALU.subtract).then_inc(s_sub, 1)
                step(dve.memset(scanm, 1.0))
                step(dve.memset(scanm.rearrange("p (e j) -> p e j", j=TILES)[:, :, 0:1], 0.0))
                dve.wait_ge(s_ex, 2)
                step(dve.tensor_reduce(ssum[:], tmp, AX.X, ALU.add))
                step(dve.reciprocal(srec[:], ssum[:]))
                step(dve.tensor_tensor(v4[:], v4[:], srec[:].unsqueeze(2).to_broadcast([P, TILES, TOPK]), ALU.mult))
                step(dve.tensor_reduce(wsum[:], v4[:], AX.X, ALU.add))
                step(dve.tensor_scalar(wsum[:], wsum[:], 1e-12, None, ALU.max))
                step(dve.reciprocal(wrec[:], wsum[:]))
                step(dve.tensor_tensor(WT[:], v4[:], wrec[:].unsqueeze(2).to_broadcast([P, TILES, TOPK]), ALU.mult))
                dve.wait_ge(s_tc, 4)
                step(dve.tensor_tensor_scan(incl, scanm, tot, 0.0, ALU.mult, ALU.add))
                step(dve.tensor_scalar(cnti[:], incl.rearrange("p (e j) -> p e j", j=TILES)[:, :, TILES - 1],
                                       float(P - 1), None, ALU.add))
                step(dve.tensor_scalar(cnts[:], cnti[:], 7, None, ALU.arith_shift_right))
                step(dve.tensor_copy(ntf[:], cnts[:]))
                step(dve.tensor_tensor_scan(nti[:], ones[:, 0:NE], ntf[:], 0.0, ALU.mult, ALU.add))
                step(dve.tensor_tensor(base[:], nti[:], ntf[:], ALU.subtract))
                step(dve.tensor_scalar(base[:], base[:], float(P), None, ALU.mult))
                step(dve.tensor_tensor(cmp_[:], nti[:].unsqueeze(1).to_broadcast([P, TC, NE]),
                                       gf[:].unsqueeze(2).to_broadcast([P, TC, NE]), ALU.is_le))
                step(dve.tensor_reduce(tef[:], cmp_[:], AX.X, ALU.add))
                dve.tensor_scalar(tei[:], tef[:], float(NE - 1), None, ALU.min).then_inc(s_te, 1)
                step(dve.tensor_tensor(incl, incl, tot, ALU.subtract))
                step(dve.tensor_tensor(pos, incl.rearrange("p (e j) -> p j e", j=TILES),
                                       base[:].unsqueeze(1).to_broadcast([P, TILES, NE]), ALU.add))
                for i in range(4):
                    part = pos[:, i * TILES // 4:(i + 1) * TILES // 4, :]
                    dve.wait_ge(s_pr, i + 1)
                    step(dve.tensor_tensor(part, part, PR[i][:].rearrange("p (j e) -> p j e", e=NE), ALU.add))
                for k in range(TOPK):
                    step(dve.tensor_tensor(pick[k], pick[k], pos, ALU.mult))
                    step(dve.tensor_reduce(idxf[:, :, k], pick[k], AX.X, ALU.add))
                step(dve.tensor_copy(IDX[:], idxf[:].rearrange("p j k -> p (j k)")))

        WGU = ARENA[:, 0:NE * 2 * P].rearrange("p (e c) -> p e c", e=NE)
        WD = ARENA[:, NE * 2 * P:NE * 3 * P].rearrange("p (e c) -> p e c", e=NE)
        SH = ARENA[:, NE * 3 * P:NE * 3 * P + TILES * DM].rearrange("p (j d) -> p j d", d=DM)
        NL = UT * TOPK // P
        with ExitStack() as r:
            def rsb(name, shape, dt=F32):
                return r.enter_context(nc.sbuf_tensor(name, shape, dt))

            def rsem(name):
                return r.enter_context(nc.semaphore(name))

            stage = [rsb(f"stage{i}", [P, TPU, DM]) for i in range(2)]
            stidx = [rsb(f"stidx{i}", [P, NL], U32) for i in range(2)]
            xT = [rsb(f"xT{i}", [P, UT]) for i in range(2)]
            sgw, suw, sdw = rsb("sgw", [P, HS]), rsb("suw", [P, HS]), rsb("sdw", [P, HST, DM])
            gs = rsb("gs", [P, 2, UT])
            hsb = rsb("hsb", [P, HST, UT])
            PG = [r.enter_context(nc.psum_tensor(f"PG{i}", [P, UT], F32)) for i in range(2)]
            PU = [r.enter_context(nc.psum_tensor(f"PU{i}", [P, UT], F32)) for i in range(2)]
            PD = [r.enter_context(nc.psum_tensor(f"PD{i}", [P, UT], F32)) for i in range(2)]
            s_ew, s_sw = rsem("s_ew"), rsem("s_sw")
            s_st = [rsem(f"s_st{i}") for i in range(2)]
            s_xT = [rsem(f"s_xT{i}") for i in range(2)]
            s_ix = rsem("s_ix")
            s_sc = [rsem(f"s_sc{i}") for i in range(2)]
            s_pg, s_pu, s_gs, s_hs = rsem("s_pg"), rsem("s_pu"), rsem("s_gs"), rsem("s_hs")
            s_pd2, s_sh = rsem("s_pd2"), rsem("s_sh")
            block = r.enter_context(nc.Block())

            @block.sync
            def _(sp):
                for dst, src in ((sgw[:], sgateT), (suw[:], supT), (sdw[:], sdownT.rearrange("(m p) d -> p m d", p=P))):
                    sp.dma_start(dst, src).then_inc(s_sw, 16)

                def load(u, par, pair):
                    if pair is not None:
                        sp.wait_ge(s_sc[par], 16 * NL * pair)
                    sp.dma_start(stage[par][:], unit_rows(xn2_dram, u)).then_inc(s_st[par], 16)
                load(0, 0, None)
                load(1, 1, None)
                sp.dma_start(WGU, gate_upT).then_inc(s_ew, 16)
                sp.dma_start(WD, downT).then_inc(s_ew, 16)
                with sp.Fori(1, UNITS // 2) as pair:
                    load(pair * 2, 0, pair)
                    load(pair * 2 + 1, 1, pair)
                sp.wait_ge(s_ew, 32)

            @block.gpsimd
            def _(pool):
                def scatter(u, par, pair):
                    if not at(pair, 0):
                        pool.wait_ge(s_sc[par], 16 * NL * pair)
                    pause(pool, scratch, 6)
                    pool.tensor_copy(stidx[par][:], IDX[:, bass.ds(u * NL, NL)]).then_inc(s_ix, 1)
                    pool.wait_ge(s_ix, u + 1)
                    pool.wait_ge(s_st[par], 16 * (pair + 1))
                    pause(pool, scratch, 7)
                    for j in range(TPU):
                        for k in range(TOPK):
                            pool.indirect_dma_start(
                                xs_dram, bass.IndirectOffsetOnAxis(ap=stidx[par][:, j * TOPK + k:j * TOPK + k + 1], axis=0),
                                stage[par][:, j, :], None).then_inc(s_sc[par], 16)
                scatter(0, 0, 0)
                scatter(1, 1, 0)
                with pool.Fori(1, UNITS // 2) as pair:
                    scatter(pair * 2, 0, pair)
                    scatter(pair * 2 + 1, 1, pair)
                for par in range(2):
                    pool.wait_ge(s_sc[par], 16 * NL * (UNITS // 2))

            @block.tensor
            def _(pe):
                pe.wait_ge(s_sw, 48)

                def hidden(u, par, pair, back):
                    pe.wait_ge(s_xT[par], 16 * (pair + 1))
                    for mm in range(HST):
                        n = u * HST + mm
                        if back or mm >= 2:
                            pe.wait_ge(s_hs, n - 1)
                        pe.matmul(PG[mm % 2][:], sgw[:, mm * P:(mm + 1) * P], xT[par][:],
                                  start=True, stop=True).then_inc(s_pg, 1)
                        pe.matmul(PU[mm % 2][:], suw[:, mm * P:(mm + 1) * P], xT[par][:],
                                  start=True, stop=True).then_inc(s_pu, 1)

                def down(u, par, back):
                    pe.wait_ge(s_hs, HST * (u + 1))
                    if back:
                        pe.wait_ge(s_sh, u - 1)
                    for j in range(TPU):
                        for mm in range(HST):
                            t = pe.matmul(PD[par][:, j * P:(j + 1) * P], hsb[:, mm, j * P:(j + 1) * P], sdw[:, mm, :],
                                          start=mm == 0, stop=mm == HST - 1)
                    t.then_inc(s_pd2, 1)
                for u in range(2):
                    hidden(u, u, 0, u > 0)
                    down(u, u, False)
                with pe.Fori(1, UNITS // 2) as pair:
                    for par in range(2):
                        hidden(pair * 2 + par, par, pair, True)
                        down(pair * 2 + par, par, True)

            @block.scalar
            def _(act):
                def load(u, par):
                    act.dma_start(xT[par][:], xn2T_dram[bass.ds(u * P, P), :]).then_inc(s_xT[par], 16)

                def unit(u, par, back, more):
                    for mm in range(HST):
                        n = u * HST + mm
                        act.wait_ge(s_pg, n + 1)
                        if back or mm >= 2:
                            act.wait_ge(s_hs, n - 1)
                        act.activation(gs[:, mm % 2, :], PG[mm % 2][:], ACT.Silu).then_inc(s_gs, 1)
                    act.wait_ge(s_pd2, u + 1)
                    if more:
                        load(u + 2, par)
                    act.activation(SH[:, bass.ds(u * TPU, TPU), :], PD[par][:].rearrange("p (j d) -> p j d", d=DM),
                                   ACT.Copy).then_inc(s_sh, 1)
                load(0, 0)
                load(1, 1)
                unit(0, 0, False, True)
                unit(1, 1, True, True)
                with act.Fori(1, UNITS // 2 - 1) as pair:
                    unit(pair * 2, 0, True, True)
                    unit(pair * 2 + 1, 1, True, True)
                unit(UNITS - 2, 0, True, False)
                unit(UNITS - 1, 1, True, False)

            @block.vector
            def _(dve):
                def unit(u):
                    if not at(u, 0):
                        dve.wait_ge(s_pd2, u)
                    for mm in range(HST):
                        n = u * HST + mm
                        dve.wait_ge(s_gs, n + 1)
                        dve.wait_ge(s_pu, n + 1)
                        dve.tensor_tensor(hsb[:, mm, :], gs[:, mm % 2, :], PU[mm % 2][:], ALU.mult).then_inc(s_hs, 1)
                unit(0)
                with dve.Fori(1, UNITS) as u:
                    unit(u)

        with ExitStack() as r:
            def rsb(name, shape, dt=F32):
                return r.enter_context(nc.sbuf_tensor(name, shape, dt))

            def rsem(name):
                return r.enter_context(nc.semaphore(name))

            NX = 4
            xg = [rsb(f"xg{i}", [P, GT, DM]) for i in range(NX)]
            te = [rsb(f"te{i}", [1, GT], I32) for i in range(NX)]
            xgT = [rsb(f"xgT{i}", [P, GT * P]) for i in range(2)]
            sg = [rsb(f"sg{i}", [P, GT, P]) for i in range(2)]
            hg = [rsb(f"hg{i}", [P, GT, P]) for i in range(2)]
            hgT = [rsb(f"hgT{i}", [P, GT * P]) for i in range(2)]
            yo = [rsb(f"yo{i}", [P, GT, DM]) for i in range(2)]
            PXT = r.enter_context(nc.psum_tensor("PXT", [P, GT * P], F32))
            PHT = r.enter_context(nc.psum_tensor("PHT", [P, GT * P], F32))
            PGU = [r.enter_context(nc.psum_tensor(f"PGU{i}", [P, 2, 2, P], F32)) for i in range(4)]
            PY = [r.enter_context(nc.psum_tensor(f"PY{i}", [P, GT * DM], F32)) for i in range(2)]
            s_xg = [rsem(f"s_xg{i}") for i in range(NX)]
            s_xt, s_xtc = rsem("s_xt"), rsem("s_xtc")
            s_gu, s_sg, s_hg = rsem("s_gu"), rsem("s_sg"), rsem("s_hg")
            s_ht, s_htc, s_y, s_yo = rsem("s_ht"), rsem("s_htc"), rsem("s_y"), rsem("s_yo")
            s_ys = [rsem(f"s_ys{i}") for i in range(2)]
            block = r.enter_context(nc.Block())

            def slot_rows(dram, g):
                return dram[bass.ds(g * GT * P, GT * P), :].rearrange("(j p) d -> p j d", p=P)

            @block.sync
            def _(sp):
                def load(g, i, turn):
                    if turn is not None:
                        sp.wait_ge(s_xt, g - NX + 1)
                    sp.dma_start(xg[i][:], slot_rows(xs_dram, g)).then_inc(s_xg[i], 16)
                for g in range(NX):
                    load(g, g, None)
                with sp.Fori(1, GROUPS // NX) as turn:
                    for i in range(NX):
                        load(turn * NX + i, i, turn)

            @block.gpsimd
            def _(pool):
                def store(g, par, pair):
                    pool.wait_ge(s_yo, g + 1)
                    pool.dma_start(slot_rows(ys_dram, g), yo[par][:]).then_inc(s_ys[par], 16)
                with pool.Fori(0, GROUPS // 2) as pair:
                    store(pair * 2, 0, pair)
                    store(pair * 2 + 1, 1, pair)
                for par in range(2):
                    pool.wait_ge(s_ys[par], 16 * (GROUPS // 2))

            @block.tensor
            def _(pe):
                def experts(first, n):
                    return nc.values_load_multi_w_load_instructions(
                        te_dram[bass.ds(first, n)].unsqueeze(0), engines=[mybir.EngineType.PE], min_val=0,
                        max_val=NE - 1, skip_runtime_bounds_check_because="it is a minimum with NE - 1")[1]

                def tokens_T(g, i, turn):
                    pe.wait_ge(s_xg[i], 16 * (turn + 1))
                    if not at(g, 0):
                        pe.wait_ge(s_xtc, g)
                    for j in range(GT):
                        t = pe.transpose(PXT[:, j * P:(j + 1) * P], xg[i][:, j, :], idf[:])
                    t.then_inc(s_xt, 1)

                def gate_up(g, par, es, back):
                    pe.wait_ge(s_xtc, g + 1)
                    if back:
                        pe.wait_ge(s_hg, 2 * g - 2)
                    for j in range(GT):
                        t = pe.matmul(PGU[2 * par + j // 2][:, j % 2, :, :].rearrange("p a c -> p (a c)"),
                                      xgT[par][:, j * P:(j + 1) * P],
                                      WGU[:, bass.ds(es[j], 1), :].rearrange("p e c -> p (e c)"),
                                      start=True, stop=True)
                        if j % 2:
                            t.then_inc(s_gu, 1)

                def hidden_T(g, par):
                    pe.wait_ge(s_hg, 2 * g + 2)
                    if not at(g, 0):
                        pe.wait_ge(s_htc, g)
                    for j in range(GT):
                        t = pe.transpose(PHT[:, j * P:(j + 1) * P], hg[par][:, j, :], idf[:])
                    t.then_inc(s_ht, 1)

                def down(g, par, es, back):
                    pe.wait_ge(s_htc, g + 1)
                    if back:
                        pe.wait_ge(s_yo, g - 1)
                    for j in range(GT):
                        t = pe.matmul(PY[par][:, j * DM:(j + 1) * DM], hgT[par][:, j * P:(j + 1) * P],
                                      WD[:, bass.ds(es[j], 1), :].rearrange("p e c -> p (e c)"),
                                      start=True, stop=True)
                    t.then_inc(s_y, 1)

                def body(g, par, i, turn, es, before, back, more):
                    if before is not None:
                        hidden_T(g - 1, 1 - par)
                    gate_up(g, par, es, back)
                    if before is not None:
                        down(g - 1, 1 - par, before, back)
                    if more:
                        tokens_T(g + 1, (i + 1) % NX, turn + (i + 1) // NX)

                def turn_of_groups(turn, last):
                    es = experts(turn * (NX * GT) - GT, (NX + 1) * GT)
                    for i in range(NX):
                        body(turn * NX + i, i % 2, i, turn, es[(i + 1) * GT:(i + 2) * GT], es[i * GT:(i + 1) * GT],
                             True, not last or i < NX - 1)
                    return es

                tokens_T(0, 0, 0)
                es = experts(0, NX * GT)
                for g in range(NX):
                    body(g, g % 2, g, 0, es[g * GT:(g + 1) * GT], es[(g - 1) * GT:g * GT] if g else None, g >= 3, True)
                with pe.Fori(1, GROUPS // NX - 1) as turn:
                    turn_of_groups(turn, False)
                es = turn_of_groups(GROUPS // NX - 1, True)
                hidden_T(GROUPS - 1, 1)
                down(GROUPS - 1, 1, es[NX * GT:], True)

            @block.scalar
            def _(act):
                def tokens(g, par):
                    act.wait_ge(s_xt, g + 1)
                    if not (at(g, 0) or at(g, 1)):
                        act.wait_ge(s_gu, 2 * g - 2)
                    act.activation(xgT[par][:], PXT[:], ACT.Copy).then_inc(s_xtc, 1)

                def gates(g, par):
                    for q in range(2):
                        act.wait_ge(s_gu, 2 * g + q + 1)
                        if not (at(g, 0) or at(g, 1)):
                            act.wait_ge(s_hg, 2 * g - 3 + q)
                        act.activation(sg[par][:, 2 * q:2 * q + 2, :], PGU[2 * par + q][:, :, 0, :], ACT.Silu).then_inc(s_sg, 1)
                tokens(0, 0)
                for g in range(2):
                    gates(g, g)
                    tokens(g + 1, 1 - g)
                with act.Fori(1, GROUPS // 2 - 1) as pair:
                    for par in range(2):
                        gates(pair * 2 + par, par)
                        tokens(pair * 2 + par + 1, 1 - par)
                gates(GROUPS - 2, 0)
                tokens(GROUPS - 1, 1)
                gates(GROUPS - 1, 1)

            @block.vector
            def _(dve):
                def hidden(g, par):
                    if not (at(g, 0) or at(g, 1)):
                        dve.wait_ge(s_ht, g - 1)
                    for q in range(2):
                        dve.wait_ge(s_sg, 2 * g + q + 1)
                        dve.tensor_tensor(hg[par][:, 2 * q:2 * q + 2, :], sg[par][:, 2 * q:2 * q + 2, :],
                                          PGU[2 * par + q][:, :, 1, :], ALU.mult).then_inc(s_hg, 1)

                def hidden_T(g, par):
                    dve.wait_ge(s_ht, g + 1)
                    if not (at(g, 0) or at(g, 1)):
                        dve.wait_ge(s_y, g - 1)
                    dve.tensor_copy(hgT[par][:], PHT[:]).then_inc(s_htc, 1)

                def output(g, par, pair):
                    dve.wait_ge(s_y, g + 1)
                    if not at(pair, 0):
                        dve.wait_ge(s_ys[par], 16 * pair)
                    dve.tensor_copy(yo[par][:].rearrange("p j d -> p (j d)"), PY[par][:]).then_inc(s_yo, 1)

                def both(pair):
                    hidden_T(pair * 2 + 1, 1)
                    hidden(pair * 2 + 2, 0)
                    output(pair * 2 + 1, 1, pair)
                    hidden_T(pair * 2 + 2, 0)
                    hidden(pair * 2 + 3, 1)
                    output(pair * 2 + 2, 0, pair + 1)
                hidden(0, 0)
                hidden_T(0, 0)
                hidden(1, 1)
                output(0, 0, 0)
                both(0)
                with dve.Fori(1, GROUPS // 2 - 1) as pair:
                    both(pair)
                hidden_T(GROUPS - 1, 1)
                output(GROUPS - 1, 1, GROUPS // 2 - 1)

        with ExitStack() as r:
            def rsb(name, shape, dt=F32):
                return r.enter_context(nc.sbuf_tensor(name, shape, dt))

            def rsem(name):
                return r.enter_context(nc.semaphore(name))

            gidx = [rsb(f"gidx{i}", [P, NL], U32) for i in range(2)]
            rows = [rsb(f"rows{i}", [P, TPU, TOPK, DM]) for i in range(2)]
            fst, fmv = rsb("fst", [P, TPU, 6]), rsb("fmv", [P, TPU, 2])
            fln, frs = rsb("fln", [P, TPU]), rsb("frs", [P, TPU])
            fw = rsb("fw", [P, TPU, TOPK])
            acc = rsb("acc", [P, TPU, DM])
            fo = [rsb(f"fo{i}", [P, TPU, DM]) for i in range(2)]
            s_gi, s_fw, s_acc = rsem("s_gi"), rsem("s_fw"), rsem("s_acc")
            s_g = [rsem(f"s_g{i}") for i in range(2)]
            s_fst, s_fmv, s_fln, s_frs, s_fn, s_fo = (rsem(n) for n in ("s_fst", "s_fmv", "s_fln", "s_frs", "s_fn", "s_fo"))
            s_out = [rsem(f"s_out{i}") for i in range(2)]
            block = r.enter_context(nc.Block())

            @block.gpsimd
            def _(pool):
                def gather(u, par, pair):
                    if not at(pair, 0):
                        pool.wait_ge(s_g[par], 16 * NL * pair)
                    pause(pool, scratch, 8)
                    pool.tensor_copy(gidx[par][:], IDX[:, bass.ds(u * NL, NL)]).then_inc(s_gi, 1)
                    pool.wait_ge(s_gi, u + 1)
                    if not (at(u, 0) or at(u, 1)):
                        pool.wait_ge(s_acc, (u - 1) * TOPK)
                    pause(pool, scratch, 9)
                    for j in range(TPU):
                        for k in range(TOPK):
                            pool.indirect_dma_start(
                                rows[par][:, j, k, :], None, ys_dram,
                                bass.IndirectOffsetOnAxis(ap=gidx[par][:, j * TOPK + k:j * TOPK + k + 1], axis=0)
                            ).then_inc(s_g[par], 16)
                gather(0, 0, 0)
                gather(1, 1, 0)
                with pool.Fori(1, UNITS // 2) as pair:
                    gather(pair * 2, 0, pair)
                    gather(pair * 2 + 1, 1, pair)

            @block.vector
            def _(dve):
                def unit(u, par, pair):
                    if not at(u, 0):
                        dve.wait_ge(s_acc, u * TOPK)
                    dve.tensor_copy(fw[:], WT[:, bass.ds(u * TPU, TPU), :]).then_inc(s_fw, 1)
                    dve.wait_ge(s_fw, u + 1)
                    dve.wait_ge(s_g[par], 16 * NL * (pair + 1))
                    for k in range(TOPK):
                        if k:
                            dve.wait_ge(s_acc, u * TOPK + k)
                        for j in range(TPU):
                            sh = SH[:, bass.ds(u * TPU + j, 1), :].rearrange("p j d -> p (j d)")
                            t = dve.scalar_tensor_tensor(out=acc[:, j, :], in0=rows[par][:, j, k, :],
                                                         scalar=fw[:, j, k:k + 1], in1=acc[:, j, :] if k else sh,
                                                         op0=ALU.mult, op1=ALU.add)
                        t.then_inc(s_acc, 1)
                    dve.wait_ge(s_acc, u * TOPK + TOPK)
                    pause(dve, scratch, 10)
                    for j in range(TPU):
                        t = dve.bn_stats(fst[:, j, :], acc[:, j, :])
                    t.then_inc(s_fst, 1)
                    dve.wait_ge(s_fst, u + 1)
                    pause(dve, scratch, 11)
                    for j in range(TPU):
                        t = dve.bn_aggr(fmv[:, j, :], fst[:, j, :])
                    t.then_inc(s_fmv, 1)
                    dve.wait_ge(s_frs, u + 1)
                    if not at(pair, 0):
                        dve.wait_ge(s_out[par], 16 * pair)
                    for j in range(TPU):
                        t = dve.tensor_scalar(fo[par][:, j, :], acc[:, j, :], fmv[:, j, 0:1], frs[:, j:j + 1],
                                              ALU.subtract, ALU.mult)
                    t.then_inc(s_fn, 1)
                    dve.wait_ge(s_fn, u + 1)
                    dve.tensor_tensor(fo[par][:], fo[par][:], X2[:, bass.ds(u * TPU, TPU), :], ALU.add).then_inc(s_fo, 1)
                unit(0, 0, 0)
                unit(1, 1, 0)
                with dve.Fori(1, UNITS // 2) as pair:
                    unit(pair * 2, 0, pair)
                    unit(pair * 2 + 1, 1, pair)

            @block.scalar
            def _(act):
                with act.Fori(0, UNITS) as u:
                    act.preload_act_table_set(EXP_LN)
                    act.wait_ge(s_fmv, u + 1)
                    act.activation(fln[:], fmv[:, :, 1], ACT.Ln, bias=eps[:]).then_inc(s_fln, 1)
                    act.wait_ge(s_fln, u + 1)
                    act.activation(frs[:], fln[:], ACT.Exp, scale=-0.5).then_inc(s_frs, 1)

            @block.sync
            def _(sp):
                with sp.Fori(0, UNITS // 2) as pair:
                    for par in range(2):
                        sp.wait_ge(s_fo, pair * 2 + par + 1)
                        sp.dma_start(unit_rows(out, pair * 2 + par), fo[par][:]).then_inc(s_out[par], 16)
                for par in range(2):
                    sp.wait_ge(s_out[par], 16 * (UNITS // 2))


def kernel(**inputs):
    import concourse.bacc as _bacc
    from concourse.bass_utils import run_bass_kernel_spmd as _run

    a = {k.removeprefix("L0_attn_").removeprefix("L0_ffn_"): np.asarray(v) for k, v in inputs.items()}
    layout = {
        "x": a["x"].reshape(TOK, DM),
        "W_inT": a["W_in"].T,
        "w_convT": a["w_conv"].T,
        "b_conv": a["b_conv"].reshape(NH, P).T,
        "W_x": a["W_x"],
        "W_xT": a["W_x"].T,
        "W_dtT": a["W_dt"].T,
        "b_dt": a["b_dt"].reshape(NH, P).T,
        "A_log": a["A_log"],
        "Dv": a["D"].reshape(NH, P).T,
        "W_outT": a["W_out"].T,
        "routerT": a["router_w"].T,
        "router_bias": a["router_bias"],
        "gate_upT": np.stack([a["gate_w"], a["up_w"]], 1).transpose(3, 0, 1, 2).reshape(DM, NE, 2 * P),
        "downT": a["down_w"].transpose(2, 0, 1),
        "sgateT": a["sgate_w"].T,
        "supT": a["sup_w"].T,
        "sdownT": a["sdown_w"].T,
        "sel": np.repeat(np.tile(np.eye(2 * NS, dtype=np.float32), (3, 1)), P, axis=1),
        "ident": np.eye(P, dtype=np.float32),
        "upper": np.triu(np.ones((P, P), np.float32), 1),
    }
    nc = _bacc.Bacc("TRN2", target_bir_lowering=False, num_devices=1)
    arrays, args = {}, []
    for name, v in layout.items():
        v = np.ascontiguousarray(v)
        arrays[f"in_{name}"] = v
        args.append(nc.dram_tensor(f"in_{name}", v.shape, mybir.dt.from_np(v.dtype), kind="ExternalInput").ap())
    args.append(nc.dram_tensor("out_0", (TOK, DM), F32, kind="ExternalOutput").ap())
    mamba_moe_kernel(nc, *args)
    r = _run(nc, [arrays], core_ids=[0])
    return r.results[0]["out_0"].reshape(BATCH, SEQ, DM)
```

```python
import numpy as np
import concourse.bass as bass
from concourse import mybir
from contextlib import ExitStack

F32 = mybir.dt.float32
BF16 = mybir.dt.bfloat16
U32 = mybir.dt.uint32
I32 = mybir.dt.int32
ALU = mybir.AluOpType
ACT = mybir.ActivationFunctionType
AX = mybir.AxisListType

P = 128
BATCH, SEQ = 32, 256
DM = 128
DI = 256
NS = 16
KC = 4
NH = DI // P
TOK = BATCH * SEQ
UB = 2
UT = UB * SEQ
UNITS = TOK // UT
TPU = UT // P
TILES = TOK // P
SG = 4
NSG = NS // SG
NCH = NSG * NH
NE, TOPK = 32, 4
HS = P * TOPK
HST = HS // P
HALF_TILES = TOK // 2 * TOPK // P + NE
SLOT_TILES = 2 * HALF_TILES
GT = 4
HG = HALF_TILES // GT
HU = UNITS // 2
EPS = 1e-5
EXP_LN = "natural_log_exp_and_others"
A_RING, H_RING = 2, 4
B, C = 0, 1
ARENA_COLS = (A_RING + H_RING + 4) * SG * UT
POOL_CMUL = (3, 7)


def at(u, n):
    return isinstance(u, int) and u == n


def has(u):
    return not isinstance(u, int) or 0 <= u < UNITS


def pause(eng, scratch, place):
    eng.tensor_tensor(scratch[:, place:place + 1], scratch[:, 0:1], scratch[:, 0:1], ALU.mult)


def mamba_moe_kernel(nc, x, W_inT, w_convT, b_conv, W_x, W_xT, W_dtT, b_dt, A_log, Dv, W_outT,
                     routerT, router_bias, gate_upT, downT, sgateT, supT, sdownT,
                     sel, ident, from_on, out):
    xs_dram = [nc.dram_tensor(f"xs_scratch{q}", (HALF_TILES * P, DM), F32, kind="Internal").ap() for q in range(2)]
    ys_dram = [nc.dram_tensor(f"ys_scratch{q}", (HALF_TILES * P, DM), F32, kind="Internal").ap() for q in range(2)]
    xn2_dram = nc.dram_tensor("xn2_scratch", (TOK, DM), F32, kind="Internal").ap()
    xn2T_dram = nc.dram_tensor("xn2T_scratch", (UNITS * P, UT), F32, kind="Internal").ap()

    def unit_rows(dram, u):
        return dram[bass.ds(u * UT, UT), :].rearrange("(j p) d -> p j d", p=P)

    with ExitStack() as ctx:
        def sb(name, shape, dt=F32):
            return ctx.enter_context(nc.sbuf_tensor(name, shape, dt))

        def sem(name):
            return ctx.enter_context(nc.semaphore(name))

        X2 = sb("X2", [P, TILES, DM])
        LG = sb("LG", [P, TILES, NE])
        V8 = sb("V8", [P, TILES, 8])
        I8 = sb("I8", [P, TILES, 8], U32)
        IDX = sb("IDX", [P, TILES * TOPK], U32)
        WT = sb("WT", [P, TILES, TOPK])

        idf = sb("idf", [P, P])
        eps = sb("eps", [P, 1])
        s_eps = sem("s_eps")
        scratch = sb("scratch", [P, 16])
        ARENA = sb("ARENA", [P, ARENA_COLS])

        with ExitStack() as m:
            def msb(name, shape, dt=F32):
                return m.enter_context(nc.sbuf_tensor(name, shape, dt))

            def msem(name):
                return m.enter_context(nc.semaphore(name))

            CW = SG * UT

            def ring(base, n):
                return [ARENA[:, base + i * CW:base + (i + 1) * CW].rearrange("p (s t) -> p s t", s=SG)
                        for i in range(n)]

            decay = ring(0, A_RING)
            state = ring(A_RING * CW, H_RING)
            Bbc = ring((A_RING + H_RING) * CW, 2)
            Cbc = ring((A_RING + H_RING + 2) * CW, 2)
            setup = ARENA[:, (A_RING + H_RING) * CW:(A_RING + H_RING + 4) * CW]
            self32 = setup[0:3 * 2 * NS, 0:2 * NS * P]
            o = 2 * NS * P
            winx = setup[:, o:o + DI]
            wcv = setup[:, o + DI:o + DI + KC * DI]
            o += DI + KC * DI
            wxd = setup[:, o:o + NH * DI].rearrange("p (h c) -> p h c", h=NH)
            o += NH * DI
            wdt = setup[:, o:o + NH * DI].rearrange("p (h c) -> p h c", h=NH)
            winz = msb("winz", [P, DI])
            wcomb = msb("wcomb", [P, KC, DI])
            bcv = msb("bcv", [P, NH])
            bdt = msb("bdt", [P, NH])
            wbc = msb("wbc", [P, NH, 3, 2 * NS])
            wdelta = msb("wdelta", [P, NH, DI])
            Apos = msb("Apos", [P, NH, NS])
            Aneg = msb("Aneg", [P, NH, NS])
            Dsb = msb("Dsb", [P, NH])
            wout = msb("wout", [P, NH, DM])
            wr = msb("wr", [P, NE])
            rbias = msb("rbias", [P, NE])
            selb = msb("selb", [3 * 2 * NS, 2 * NS, P], BF16)
            zrow = msb("zrow", [P, 1024])

            xst = msb("xst", [P, TPU, 6])
            xmv = msb("xmv", [P, TPU, 2])
            xln = msb("xln", [P, TPU])
            xrs = msb("xrs", [P, TPU])
            xn = msb("xn", [P, TPU, DM])
            xnT = msb("xnT", [P, UB, KC - 1 + SEQ])
            xc = msb("xc", [P, 2, NH, UT])
            sz = msb("sz", [P, 2, NH, UT])
            dl = msb("dl", [P, 2, NH, UB, SEQ])
            dtmp = msb("dtmp", [P, NH, UT])
            bcs = msb("bcs", [96, 2, UT], BF16)
            r1 = msb("r1", [96, UT])
            r2 = msb("r2", [96, UT])
            yg = msb("yg", [P, NH, UT])
            mst = msb("mst", [P, TPU, 6])
            mmv = msb("mmv", [P, TPU, 2])
            mln = msb("mln", [P, TPU])
            mrs = msb("mrs", [P, TPU])
            mo = msb("mo", [P, TPU, DM])
            nst = msb("nst", [P, TPU, 6])
            nmv = msb("nmv", [P, TPU, 2])
            nln = msb("nln", [P, TPU])
            nrs = msb("nrs", [P, TPU])
            xn2 = msb("xn2", [P, TPU, DM])
            xn2T = msb("xn2T", [P, UT])
            lgs = msb("lgs", [P, TPU, NE])
            v8s = msb("v8s", [P, TPU, 8])
            i8s = msb("i8s", [P, TPU, 8], U32)

            Y = [m.enter_context(nc.psum_tensor(f"Y{h}", [P, UT], F32)) for h in range(NH)]
            BCP = [m.enter_context(nc.psum_tensor(f"BCP{i}", [P, UT], F32)) for i in range(3)]
            BCP_OF, BCP_AGO = (0, 1, 2, 1), (4, 2, 4, 2)
            PJ = [m.enter_context(nc.psum_tensor(f"PJ{i}", [P, UT], F32)) for i in range(2)]
            PK = m.enter_context(nc.psum_tensor("PK", [P, UT], F32))

            s_w, s_sel = msem("s_w"), msem("s_sel")
            s_x0, s_x1, s_xr = msem("s_x0"), msem("s_x1"), msem("s_xr")
            s_set = msem("s_set")
            s_wc = msem("s_wc")
            s_wdm, s_wdc = msem("s_wdm"), msem("s_wdc")
            s_ap, s_an = msem("s_ap"), msem("s_an")
            s_zero = msem("s_zero")
            s_xst, s_xmv, s_xln, s_xrs, s_xn = (msem(n) for n in ("s_xst", "s_xmv", "s_xln", "s_xrs", "s_xn"))
            s_T, s_xnT = msem("s_T"), msem("s_xnT")
            s_pc = [msem(f"s_pc{h}") for h in range(NH)]
            s_xc = [msem(f"s_xc{h}") for h in range(NH)]
            s_pz = [msem(f"s_pz{h}") for h in range(NH)]
            s_sz = [msem(f"s_sz{h}") for h in range(NH)]
            s_pbc, s_hi, s_r1 = msem("s_pbc"), msem("s_hi"), msem("s_r1")
            s_mid, s_r2, s_bcs = msem("s_mid"), msem("s_r2"), msem("s_bcs")
            s_pd = [msem(f"s_pd{h}") for h in range(NH)]
            s_dm = [msem(f"s_dm{h}") for h in range(NH)]
            s_de = [msem(f"s_de{h}") for h in range(NH)]
            s_dn = [msem(f"s_dn{h}") for h in range(NH)]
            s_dl = [msem(f"s_dl{h}") for h in range(NH)]
            s_bp, s_bcp = msem("s_bp"), msem("s_bcp")
            s_exp, s_bx, s_scan = msem("s_exp"), msem("s_bx"), msem("s_scan")
            s_cmv, s_cmp = msem("s_cmv"), msem("s_cmp")
            s_sum = msem("s_sum")
            s_yd, s_yg, s_po = msem("s_yd"), msem("s_yg"), msem("s_po")
            s_mst, s_mmv, s_mln, s_mrs, s_mo = (msem(n) for n in ("s_mst", "s_mmv", "s_mln", "s_mrs", "s_mo"))
            s_res, s_nst, s_nmv, s_nln, s_nrs = (msem(n) for n in ("s_res", "s_nst", "s_nmv", "s_nln", "s_nrs"))
            s_xn2, s_T2, s_xn2T = msem("s_xn2"), msem("s_T2"), msem("s_xn2T")
            s_pl, s_lg, s_v8, s_i8, s_keep = (msem(n) for n in ("s_pl", "s_lg", "s_v8", "s_i8", "s_keep"))
            s_stx, s_stT = msem("s_stx"), msem("s_stT")

            NWD = 19

            def nvec(u, c):
                p = sum(k < c for k in POOL_CMUL)
                return u * (NCH - len(POOL_CMUL)) + c - p

            def npool(u, c):
                return u * len(POOL_CMUL) + sum(k < c for k in POOL_CMUL)

            block = m.enter_context(nc.Block())

            @block.sync
            def _(sp):
                sp.dma_start(X2[:, 0:TPU, :], unit_rows(x, 0)).then_inc(s_x0, 16)
                loads = [
                    (winx, W_inT[:, 0:DI]), (winz[:], W_inT[:, DI:2 * DI]),
                    (wcv, w_convT.rearrange("k c -> (k c)").partition_broadcast(P)),
                    (bcv[:], b_conv),
                    (bdt[:], b_dt),
                    (wxd, W_x[0:DI, :].rearrange("(h p) c -> p h c", p=P)),
                    (wdt, W_dtT.rearrange("(h p) c -> p h c", p=P)),
                    (Apos[:], A_log.rearrange("(h p) s -> p h s", p=P)),
                    (Dsb[:], Dv),
                    (wout[:], W_outT.rearrange("(h p) c -> p h c", p=P)),
                    (wr[:], routerT), (rbias[:], router_bias.partition_broadcast(P)),
                    (idf[:], ident),
                ] + [(wbc[:, h, r, :], W_xT[h * P:(h + 1) * P, DI:DI + 2 * NS]) for h in range(NH) for r in range(3)]
                assert len(loads) == NWD
                for dst, src in loads:
                    sp.dma_start(dst, src).then_inc(s_w, 16)
                sp.dma_start(self32, sel).then_inc(s_sel, 16)
                sp.dma_start(X2[:, TPU:2 * TPU, :], unit_rows(x, 1)).then_inc(s_x1, 16)
                sp.dma_start(X2[:, 2 * TPU:TILES, :],
                             x[2 * UT:TOK, :].rearrange("(j p) d -> p j d", p=P)).then_inc(s_xr, 16)
                sp.wait_ge(s_set, 1)
                for q in range(2):
                    for z in range(HALF_TILES // 8):
                        sp.dma_start(xs_dram[q][z * 8 * P:(z + 1) * 8 * P, :].rearrange("(p r) d -> p (r d)", p=P),
                                     zrow[:]).then_inc(s_zero, 16)

                def store(u):
                    sp.wait_ge(s_xn2, u + 1)
                    sp.dma_start(unit_rows(xn2_dram, u), xn2[:]).then_inc(s_stx, 16)
                    sp.wait_ge(s_xn2T, u + 1)
                    sp.dma_start(xn2T_dram[bass.ds(u * P, P), :], xn2T[:]).then_inc(s_stT, 16)
                with sp.Fori(0, UNITS) as u:
                    store(u)
                sp.wait_ge(s_stx, 16 * UNITS)
                sp.wait_ge(s_stT, 16 * UNITS)
                sp.wait_ge(s_zero, 16 * (SLOT_TILES // 8))

            @block.tensor
            def _(pe):
                pe.wait_ge(s_w, 16 * NWD)
                for kc in range(NH):
                    for mm in range(NH):
                        last = pe.matmul(BCP[kc][:, 0:DI], wxd[:, mm, kc * P:(kc + 1) * P], wdt[:, mm, :],
                                         start=mm == 0, stop=mm == NH - 1)
                    last.then_inc(s_wdm, 1)

                def transposed(f):
                    if not has(f):
                        return
                    pe.wait_ge(s_xn, f + 1)
                    if not at(f, 0):
                        pe.wait_ge(s_dl[0], f)
                    for j in range(TPU):
                        t = pe.transpose(PJ[1][:, j * P:(j + 1) * P], xn[:, j, :], idf[:])
                    t.then_inc(s_T, 1)

                def project_x(f, h):
                    if not has(f):
                        return
                    if h == 0:
                        pe.wait_ge(s_xnT, f + 1)
                        if at(f, 0):
                            pe.wait_ge(s_wc, KC)
                        else:
                            pe.wait_ge(s_dl[1], f)
                    for k in range(KC):
                        t = pe.matmul(PJ[h][:].rearrange("p (b t) -> p b t", b=UB),
                                      wcomb[:, k, h * P:(h + 1) * P],
                                      xnT[:, :, k:k + SEQ], start=k == 0, stop=k == KC - 1)
                    t.then_inc(s_pc[h], 1)

                def project_z(f, h):
                    if not has(f):
                        return
                    pe.wait_ge(s_xc[h], f + 1)
                    pe.matmul(PJ[h][:].rearrange("p (b t) -> p b t", b=UB), winz[:, h * P:(h + 1) * P],
                              xnT[:, :, KC - 1:KC - 1 + SEQ], start=True, stop=True).then_inc(s_pz[h], 1)

                def project_bc(f, par):
                    if not has(f):
                        return
                    if at(f, 0):
                        pe.wait_ge(s_wdc, NH)
                    pe.wait_ge(s_sz[0], f + 1)
                    for h in range(NH):
                        t = pe.matmul(PJ[0][0:96, :], wbc[:, h, :, :].rearrange("p r n -> p (r n)"),
                                      xc[:, par, h, :], start=h == 0, stop=h == NH - 1)
                    t.then_inc(s_pbc, 1)

                def project_delta(f, par, o):
                    if not has(f):
                        return
                    if o == 0:
                        pe.wait_ge(s_sz[1], f + 1)
                    else:
                        pe.wait_ge(s_r1, f + 1)
                    for h in range(NH):
                        t = pe.matmul(PJ[1 - o][:], wdelta[:, h, o * P:(o + 1) * P], xc[:, par, h, :],
                                      start=h == 0, stop=h == NH - 1)
                    t.then_inc(s_pd[o], 1)

                def broadcast(u, par, sg, which, *rows):
                    if not has(u):
                        return
                    for i in rows:
                        if which == B and sg == 0 and i == 0:
                            pe.wait_ge(s_bcs, u + 1)
                        k = (sg * 2 + which) * SG + i
                        if not (at(u, 0) and k < BCP_AGO[i]):
                            pe.wait_ge(s_bcp, u * (2 * NS) + k - BCP_AGO[i] + 1)
                        pe.matmul(BCP[BCP_OF[i]][:], selb[:, which * NS + sg * SG + i, :], bcs[:, par, :],
                                  start=True, stop=True).then_inc(s_bp, 1)

                def sum_states(u, c):
                    if not has(u):
                        return
                    sg, h = c // NH, c % NH
                    if c in POOL_CMUL:
                        pe.wait_ge(s_cmp, npool(u, c) + 1)
                    else:
                        pe.wait_ge(s_cmv, nvec(u, c) + 1)
                    if sg == 0 and not at(u, 0):
                        pe.wait_ge(s_yd, u * NH - 1 + h)
                    for s in range(SG):
                        t = pe.matmul(Y[h][:], idf[:], state[c % H_RING][:, s, :],
                                      start=sg == 0 and s == 0, stop=sg == NSG - 1 and s == SG - 1)
                    t.then_inc(s_sum, 1)

                def out_proj(b):
                    if not has(b):
                        return
                    pe.wait_ge(s_yg, b + 1)
                    if not at(b, 0):
                        pe.wait_ge(s_lg, b)
                    for j in range(TPU):
                        for h in range(NH):
                            t = pe.matmul(PK[:, j * P:(j + 1) * P], yg[:, h, j * P:(j + 1) * P], wout[:, h, :],
                                          start=h == 0, stop=h == NH - 1)
                    t.then_inc(s_po, 1)

                def transposed2(b):
                    if not has(b):
                        return
                    pe.wait_ge(s_xn2, b + 1)
                    for j in range(TPU):
                        t = pe.transpose(PK[:, j * P:(j + 1) * P], xn2[:, j, :], idf[:])
                    t.then_inc(s_T2, 1)

                def logits(b):
                    if not has(b):
                        return
                    pe.wait_ge(s_xn2T, b + 1)
                    for j in range(TPU):
                        t = pe.matmul(PK[:, j * NE:(j + 1) * NE], xn2T[:, j * P:(j + 1) * P], wr[:],
                                      start=True, stop=True)
                    t.then_inc(s_pl, 1)

                def body(u, par):
                    broadcast(u, par, 1, B, 0)
                    transposed(u + 1)
                    broadcast(u, par, 1, B, 1, 2)
                    sum_states(u - 1, 6)
                    broadcast(u, par, 1, B, 3)
                    broadcast(u, par, 1, C, 0)
                    project_x(u + 1, 0)
                    broadcast(u, par, 1, C, 1, 2)
                    sum_states(u - 1, 7)
                    broadcast(u, par, 1, C, 3)
                    broadcast(u, par, 2, B, 0)
                    project_x(u + 1, 1)
                    broadcast(u, par, 2, B, 1)
                    logits(u - 2)
                    broadcast(u, par, 2, B, 2)
                    sum_states(u, 0)
                    broadcast(u, par, 2, B, 3)
                    project_z(u + 1, 0)
                    broadcast(u, par, 2, C, 0)
                    project_z(u + 1, 1)
                    broadcast(u, par, 2, C, 1, 2)
                    sum_states(u, 1)
                    broadcast(u, par, 2, C, 3)
                    broadcast(u, par, 3, B, 0)
                    out_proj(u - 1)
                    broadcast(u, par, 3, B, 1)
                    project_bc(u + 1, 1 - par)
                    broadcast(u, par, 3, B, 2)
                    sum_states(u, 2)
                    broadcast(u, par, 3, B, 3)
                    project_delta(u + 1, 1 - par, 0)
                    broadcast(u, par, 3, C, 0, 1, 2)
                    sum_states(u, 3)
                    broadcast(u, par, 3, C, 3)
                    broadcast(u + 1, 1 - par, 0, B, 0)
                    project_delta(u + 1, 1 - par, 1)
                    broadcast(u + 1, 1 - par, 0, B, 1, 2)
                    sum_states(u, 4)
                    broadcast(u + 1, 1 - par, 0, B, 3)
                    transposed2(u - 1)
                    broadcast(u + 1, 1 - par, 0, C, 0, 1, 2)
                    sum_states(u, 5)
                    broadcast(u + 1, 1 - par, 0, C, 3)

                for n in range(-2, 3):
                    body(n, n % 2)
                with pe.Fori(1, UNITS // 2 - 2) as pair:
                    u = pair * 2 + 1
                    body(u, 1)
                    body(u + 1, 0)
                for n in range(UNITS - 3, UNITS + 2):
                    body(n, n % 2)

            @block.scalar
            def _(act):
                act.preload_act_table_set(EXP_LN)

                def rstd(var, ln, rs, s_mv, s_ln, s_rs, u):
                    if not has(u):
                        return
                    act.wait_ge(s_mv, u + 1)
                    act.activation(ln[:], var[:, :, 1], ACT.Ln, bias=eps[:]).then_inc(s_ln, 1)
                    act.wait_ge(s_ln, u + 1)
                    act.activation(rs[:], ln[:], ACT.Exp, scale=-0.5).then_inc(s_rs, 1)

                def copy_xnT(f):
                    if not has(f):
                        return
                    act.wait_ge(s_T, f + 1)
                    if not at(f, 0):
                        for h in range(NH):
                            act.wait_ge(s_pz[h], f)
                    act.activation(xnT[:, :, KC - 1:KC - 1 + SEQ], PJ[1][:].rearrange("p (b t) -> p b t", b=UB),
                                   ACT.Copy).then_inc(s_xnT, 1)

                def silu_x(f, par, h):
                    if not has(f):
                        return
                    if h == 0 and not (at(f, 0) or at(f, 1)):
                        act.wait_ge(s_yg, f - 1)
                    act.wait_ge(s_pc[h], f + 1)
                    act.activation(xc[:, par, h, :], PJ[h][:], ACT.Silu, bias=bcv[:, h:h + 1]).then_inc(s_xc[h], 1)

                def silu_z(f, par, h):
                    if not has(f):
                        return
                    act.wait_ge(s_pz[h], f + 1)
                    act.activation(sz[:, par, h, :], PJ[h][:], ACT.Silu).then_inc(s_sz[h], 1)
                    if h == NH - 1:
                        act.preload_act_table_set(EXP_LN)

                def exp_delta(f, h):
                    if not has(f):
                        return
                    act.wait_ge(s_dm[h], f + 1)
                    act.activation(dtmp[:, h, :], dtmp[:, h, :], ACT.Exp).then_inc(s_de[h], 1)

                def ln_delta(f, h):
                    if not has(f):
                        return
                    act.wait_ge(s_de[h], f + 1)
                    act.activation(dtmp[:, h, :], dtmp[:, h, :], ACT.Ln, bias=1.0).then_inc(s_dn[h], 1)

                def copies(u, sg, which, *rows):
                    if not has(u):
                        return
                    for i in rows:
                        k = (sg * 2 + which) * SG + i
                        if at(u, 0) and k == 0:
                            act.wait_ge(s_sel, 17)
                        act.wait_ge(s_bp, u * (2 * NS) + k + 1)
                        if i == 0 and not (at(u, 0) and sg < 2):
                            v, c = (u, (sg - 1) * NH) if sg else (u - 1, NCH - NH)
                            if which == B:
                                act.wait_ge(s_bx, v * NCH + c)
                            else:
                                act.wait_ge(s_cmv, nvec(v, c))
                                if not at(npool(v, c), 0):
                                    act.wait_ge(s_cmp, npool(v, c))
                        act.activation((Bbc, Cbc)[which][sg % 2][:, i, :], BCP[BCP_OF[i]][:],
                                       ACT.Copy).then_inc(s_bcp, 1)

                def decays(u, par, c):
                    if not has(u):
                        return
                    sg, h = c // NH, c % NH
                    if sg == 0:
                        act.wait_ge(s_dl[h], u + 1)
                    if not (at(u, 0) and c < A_RING):
                        act.wait_ge(s_scan, u * NCH + c - A_RING + 1)
                    a = decay[c % A_RING].rearrange("p s (b t) -> p s b t", b=UB)
                    for s in range(SG):
                        t = act.activation(a[:, s, :, 1:SEQ], dl[:, par, h, :, 1:SEQ], ACT.Exp,
                                           scale=Aneg[:, h, sg * SG + s:sg * SG + s + 1])
                    t.then_inc(s_exp, 1)

                def copy_xn2T(b):
                    if not has(b):
                        return
                    act.wait_ge(s_T2, b + 1)
                    if not at(b, 0):
                        act.wait_ge(s_stT, 16 * b)
                        act.wait_ge(s_pl, b)
                    act.activation(xn2T[:], PK[:], ACT.Copy).then_inc(s_xn2T, 1)

                def body(u, par):
                    copy_xnT(u + 1)
                    copies(u, 1, B, 0, 1)
                    decays(u, par, 1)
                    copies(u, 1, B, 2, 3)
                    decays(u, par, 2)
                    copies(u, 1, C, 0, 1)
                    copy_xn2T(u - 2)
                    copies(u, 1, C, 2)
                    rstd(xmv, xln, xrs, s_xmv, s_xln, s_xrs, u + 2)
                    copies(u, 1, C, 3)
                    copies(u, 2, B, 0)
                    decays(u, par, 3)
                    copies(u, 2, B, 1)
                    silu_x(u + 1, 1 - par, 0)
                    silu_x(u + 1, 1 - par, 1)
                    copies(u, 2, B, 2, 3)
                    copies(u, 2, C, 0)
                    silu_z(u + 1, 1 - par, 0)
                    copies(u, 2, C, 1, 2)
                    silu_z(u + 1, 1 - par, 1)
                    copies(u, 2, C, 3)
                    decays(u, par, 4)
                    copies(u, 3, B, 0)
                    rstd(mmv, mln, mrs, s_mmv, s_mln, s_mrs, u - 1)
                    copies(u, 3, B, 1)
                    decays(u, par, 5)
                    copies(u, 3, B, 2, 3)
                    copies(u, 3, C, 0, 1)
                    decays(u, par, 6)
                    exp_delta(u + 1, 0)
                    copies(u, 3, C, 2)
                    rstd(nmv, nln, nrs, s_nmv, s_nln, s_nrs, u - 1)
                    copies(u, 3, C, 3)
                    copies(u + 1, 0, B, 0, 1)
                    decays(u, par, 7)
                    copies(u + 1, 0, B, 2)
                    ln_delta(u + 1, 0)
                    copies(u + 1, 0, B, 3)
                    exp_delta(u + 1, 1)
                    ln_delta(u + 1, 1)
                    copies(u + 1, 0, C, 0, 1, 2, 3)
                    decays(u + 1, 1 - par, 0)

                act.wait_ge(s_eps, 2)
                body(-2, 0)
                act.wait_ge(s_w, 16 * NWD)
                act.activation(Apos[:], Apos[:], ACT.Exp).then_inc(s_ap, 1)
                for kc in range(NH):
                    act.wait_ge(s_wdm, kc + 1)
                    act.activation(wdelta[:, kc, :], BCP[kc][:, 0:DI], ACT.Copy).then_inc(s_wdc, 1)
                act.wait_ge(s_set, 4)
                act.wait_ge(s_an, 1)
                for n in range(-1, 3):
                    body(n, n % 2)
                with act.Fori(1, UNITS // 2 - 2) as pair:
                    u = pair * 2 + 1
                    act.preload_act_table_set(EXP_LN)
                    body(u, 1)
                    body(u + 1, 0)
                for n in range(UNITS - 3, UNITS + 2):
                    body(n, n % 2)

            @block.gpsimd
            def _(pool):
                zero = scratch[:, 0:1].to_broadcast([P, UT])

                def parts(f, par):
                    if not has(f):
                        return
                    if not at(f, 0):
                        pool.wait_ge(s_bx, (f - 1) * NCH + 6)
                        pool.wait_ge(s_cmp, npool(f - 1, 5))
                    pool.wait_ge(s_r1, f + 1)
                    pool.tensor_tensor(bcs[32:64, par, :], r1[32:64, :], zero[32:64], ALU.add).then_inc(s_mid, 1)
                    pool.wait_ge(s_mid, 2 * f + 1)
                    pool.tensor_tensor(bcs[64:96, par, :], r1[64:96, :], zero[64:96], ALU.add).then_inc(s_mid, 1)
                    pool.wait_ge(s_mid, 2 * f + 2)
                    pool.tensor_tensor(r2[64:96, :], r1[64:96, :], bcs[64:96, par, :], ALU.subtract).then_inc(s_r2, 1)
                    pool.wait_ge(s_r2, f + 1)
                    pool.tensor_tensor(bcs[64:96, par, :], r2[64:96, :], zero[64:96], ALU.add).then_inc(s_bcs, 1)
                    pool.wait_ge(s_bcs, f + 1)

                def times_b(u, par, c):
                    if not has(u):
                        return
                    sg, h = c // NH, c % NH
                    n = u * NCH + c
                    if sg == 0:
                        pool.wait_ge(s_xc[h], u + 1)
                    pool.wait_ge(s_bcp, u * (2 * NS) + (sg * 2 + 1) * SG)
                    if not (at(u, 0) and c < H_RING):
                        pool.wait_ge(s_sum, n - H_RING + 1)
                    pool.tensor_tensor(state[c % H_RING], Bbc[sg % 2],
                                       xc[:, par, h, :].unsqueeze(1).to_broadcast([P, SG, UT]),
                                       ALU.mult).then_inc(s_bx, 1)

                def times_c(u, c):
                    if not has(u):
                        return
                    sg = c // NH
                    pool.wait_ge(s_scan, u * NCH + c + 1)
                    pool.wait_ge(s_bcp, u * (2 * NS) + (sg * 2 + 2) * SG)
                    pool.tensor_tensor(state[c % H_RING], state[c % H_RING], Cbc[sg % 2], ALU.mult).then_inc(s_cmp, 1)

                def body(u, par):
                    times_b(u, par, 0)
                    times_c(u - 1, 7)
                    times_b(u, par, 1)
                    times_b(u, par, 2)
                    times_b(u, par, 3)
                    times_b(u, par, 4)
                    times_c(u, 3)
                    times_b(u, par, 5)
                    parts(u + 1, 1 - par)
                    times_b(u, par, 6)
                    times_b(u, par, 7)

                pool.wait_ge(s_sel, 16)
                pool.tensor_copy(selb[:], self32.rearrange("p (s m) -> p s m", s=2 * NS)).then_inc(s_sel, 1)
                pool.wait_ge(s_sel, 17)
                pool.wait_ge(s_eps, 2)
                for n in range(-2, 3):
                    body(n, n % 2)
                with pool.Fori(1, UNITS // 2 - 2) as pair:
                    u = pair * 2 + 1
                    body(u, 1)
                    body(u + 1, 0)
                for n in range(UNITS - 3, UNITS + 2):
                    body(n, n % 2)

            @block.vector
            def _(dve):
                def x2_tile(u, j):
                    return X2[:, bass.ds(u * TPU + j, 1), :].rearrange("p j d -> p (j d)")

                def moments(src, st, mv, s_st, s_mv, u):
                    for j in range(TPU):
                        t = dve.bn_stats(st[:, j, :], src(j))
                    t.then_inc(s_st, 1)
                    dve.wait_ge(s_st, u + 1)
                    pause(dve, scratch, 1)
                    for j in range(TPU):
                        t = dve.bn_aggr(mv[:, j, :], st[:, j, :])
                    t.then_inc(s_mv, 1)

                def normalise(dst, src, mv, rs, s_rs, s_done, u):
                    dve.wait_ge(s_rs, u + 1)
                    for j in range(TPU):
                        t = dve.tensor_scalar(dst(j), src(j), mv[:, j, 0:1], rs[:, j:j + 1], ALU.subtract, ALU.mult)
                    t.then_inc(s_done, 1)

                def x_moments(f):
                    if not has(f):
                        return
                    if at(f, 0):
                        dve.wait_ge(s_x0, 16)
                    elif at(f, 1):
                        dve.wait_ge(s_x1, 16)
                    else:
                        dve.wait_ge(s_xr, 16)
                    moments(lambda j: x2_tile(f, j), xst, xmv, s_xst, s_xmv, f)

                def x_norm(f):
                    if not has(f):
                        return
                    if not at(f, 0):
                        dve.wait_ge(s_T, f)
                    normalise(lambda j: xn[:, j, :], lambda j: x2_tile(f, j), xmv, xrs, s_xrs, s_xn, f)

                def high_parts(f, par):
                    if not has(f):
                        return
                    dve.wait_ge(s_pbc, f + 1)
                    if not at(f, 0):
                        dve.wait_ge(s_bcs, f)
                    dve.tensor_copy(bcs[:, par, :], PJ[0][0:96, :]).then_inc(s_hi, 1)
                    dve.wait_ge(s_hi, f + 1)
                    dve.tensor_tensor(r1[:], PJ[0][0:96, :], bcs[:, par, :], ALU.subtract).then_inc(s_r1, 1)

                def delta_min(f, h):
                    if not has(f):
                        return
                    dve.wait_ge(s_pd[h], f + 1)
                    dve.tensor_scalar(dtmp[:, h, :], PJ[1 - h][:], bdt[:, h:h + 1], 40.0,
                                      ALU.add, ALU.min).then_inc(s_dm[h], 1)

                def delta_max(f, par, h):
                    if not has(f):
                        return
                    dve.wait_ge(s_dn[h], f + 1)
                    dve.scalar_tensor_tensor(out=dl[:, par, h, :, :].rearrange("p b t -> p (b t)"),
                                             in0=PJ[1 - h][:], scalar=bdt[:, h:h + 1], in1=dtmp[:, h, :],
                                             op0=ALU.add, op1=ALU.max).then_inc(s_dl[h], 1)

                def scan(u, c):
                    if not has(u):
                        return
                    n = u * NCH + c
                    dve.wait_ge(s_bx, n + 1)
                    dve.wait_ge(s_exp, n + 1)
                    st = state[c % H_RING].rearrange("p s t -> p (s t)")
                    dve.tensor_tensor_scan(st, decay[c % A_RING].rearrange("p s t -> p (s t)"), st,
                                           0.0, ALU.mult, ALU.add).then_inc(s_scan, 1)

                def times_c(u, c):
                    if not has(u):
                        return
                    sg = c // NH
                    dve.wait_ge(s_scan, u * NCH + c + 1)
                    dve.wait_ge(s_bcp, u * (2 * NS) + (sg * 2 + 2) * SG)
                    dve.tensor_tensor(state[c % H_RING], state[c % H_RING], Cbc[sg % 2], ALU.mult).then_inc(s_cmv, 1)

                def add_d(b, par, h):
                    if not has(b):
                        return
                    dve.wait_ge(s_sum, b * NCH + NCH - 1 + h)
                    if not at(b, 0):
                        dve.wait_ge(s_po, b)
                    dve.scalar_tensor_tensor(out=yg[:, h, :], in0=xc[:, par, h, :], scalar=Dsb[:, h:h + 1],
                                             in1=Y[h][:], op0=ALU.mult, op1=ALU.add).then_inc(s_yd, 1)

                def gate(b, par):
                    if not has(b):
                        return
                    dve.wait_ge(s_yd, (b + 1) * NH)
                    dve.tensor_tensor(yg[:], yg[:], sz[:, par, :, :], ALU.mult).then_inc(s_yg, 1)

                def out_moments(b):
                    if not has(b):
                        return
                    dve.wait_ge(s_po, b + 1)
                    pause(dve, scratch, 2)
                    moments(lambda j: PK[:, j * P:(j + 1) * P], mst, mmv, s_mst, s_mmv, b)

                def out_norm(b):
                    if not has(b):
                        return
                    normalise(lambda j: mo[:, j, :], lambda j: PK[:, j * P:(j + 1) * P], mmv, mrs, s_mrs, s_mo, b)

                def residual(b):
                    if not has(b):
                        return
                    dve.wait_ge(s_mo, b + 1)
                    rows = X2[:, bass.ds(b * TPU, TPU), :]
                    dve.tensor_tensor(rows, rows, mo[:], ALU.add).then_inc(s_res, 1)
                    dve.wait_ge(s_res, b + 1)
                    pause(dve, scratch, 3)
                    moments(lambda j: x2_tile(b, j), nst, nmv, s_nst, s_nmv, b)

                def norm2(b):
                    if not has(b):
                        return
                    if not at(b, 0):
                        dve.wait_ge(s_stx, 16 * b)
                        dve.wait_ge(s_T2, b)
                    normalise(lambda j: xn2[:, j, :], lambda j: x2_tile(b, j), nmv, nrs, s_nrs, s_xn2, b)

                def pick(b):
                    if not has(b):
                        return
                    dve.wait_ge(s_pl, b + 1)
                    if not at(b, 0):
                        dve.wait_ge(s_keep, b)
                    dve.tensor_tensor(lgs[:], PK[:, 0:TPU * NE].rearrange("p (j e) -> p j e", j=TPU),
                                      rbias[:].unsqueeze(1).to_broadcast([P, TPU, NE]), ALU.add).then_inc(s_lg, 1)
                    dve.wait_ge(s_lg, b + 1)
                    pause(dve, scratch, 4)
                    for j in range(TPU):
                        t = dve.max(v8s[:, j, :], lgs[:, j, :])
                    t.then_inc(s_v8, 1)
                    dve.wait_ge(s_v8, b + 1)
                    pause(dve, scratch, 5)
                    for j in range(TPU):
                        t = dve.max_index(i8s[:, j, :], v8s[:, j, :], lgs[:, j, :])
                    t.then_inc(s_i8, 1)
                    dve.tensor_copy(LG[:, bass.ds(b * TPU, TPU), :], lgs[:])
                    dve.tensor_copy(V8[:, bass.ds(b * TPU, TPU), :], v8s[:])
                    dve.wait_ge(s_i8, b + 1)
                    dve.tensor_copy(I8[:, bass.ds(b * TPU, TPU), :], i8s[:]).then_inc(s_keep, 1)

                def body(u, par):
                    x_moments(u + 2)
                    scan(u, 0)
                    scan(u, 1)
                    x_norm(u + 2)
                    add_d(u - 1, 1 - par, 0)
                    times_c(u, 0)
                    add_d(u - 1, 1 - par, 1)
                    gate(u - 1, 1 - par)
                    scan(u, 2)
                    times_c(u, 1)
                    scan(u, 3)
                    pick(u - 2)
                    times_c(u, 2)
                    out_moments(u - 1)
                    high_parts(u + 1, 1 - par)
                    scan(u, 4)
                    out_norm(u - 1)
                    scan(u, 5)
                    delta_min(u + 1, 0)
                    residual(u - 1)
                    times_c(u, 4)
                    norm2(u - 1)
                    scan(u, 6)
                    times_c(u, 5)
                    delta_min(u + 1, 1)
                    scan(u, 7)
                    delta_max(u + 1, 1 - par, 0)
                    times_c(u, 6)
                    delta_max(u + 1, 1 - par, 1)

                dve.memset(eps[:], EPS).then_inc(s_eps, 1)
                dve.memset(scratch[:], 0.0).then_inc(s_eps, 1)
                dve.memset(zrow[:], 0.0).then_inc(s_set, 1)
                dve.memset(xnT[:], 0.0).then_inc(s_set, 1)
                for a in decay:
                    dve.memset(a, 0.0).then_inc(s_set, 1)
                body(-2, 0)
                dve.wait_ge(s_w, 16 * NWD)
                for k in range(KC):
                    dve.tensor_tensor(wcomb[:, k, :], winx, wcv[:, k * DI:(k + 1) * DI], ALU.mult).then_inc(s_wc, 1)
                dve.wait_ge(s_ap, 1)
                dve.tensor_scalar(Aneg[:], Apos[:], -1.0, None, ALU.mult).then_inc(s_an, 1)
                for n in range(-1, 3):
                    body(n, n % 2)
                with dve.Fori(1, UNITS // 2 - 2) as pair:
                    u = pair * 2 + 1
                    body(u, 1)
                    body(u + 1, 0)
                for n in range(UNITS - 3, UNITS + 2):
                    body(n, n % 2)



        NL = UT * TOPK // P

        class Move:
            pass

        def scatter_buffers(rsb, rsem):
            S = Move()
            S.stage = [rsb(f"stage{i}", [P, TPU, DM]) for i in range(2)]
            S.idx = [rsb(f"stidx{i}", [P, NL], U32) for i in range(2)]
            S.s_st = [rsem(f"s_st{i}") for i in range(2)]
            S.s_ix = rsem("s_ix")
            S.s_sc = [rsem(f"s_sc{i}") for i in range(2)]
            return S

        def scatter_half(pool, half, S):
            def scatter(u, par, pair):
                if not at(pair, 0):
                    pool.wait_ge(S.s_sc[par], 16 * NL * pair)
                pause(pool, scratch, 6)
                pool.tensor_copy(S.idx[par][:], IDX[:, bass.ds(u * NL, NL)]).then_inc(S.s_ix, 1)
                pool.wait_ge(S.s_ix, u + 1)
                pool.wait_ge(S.s_st[par], 16 * (pair + 1))
                pause(pool, scratch, 7)
                for j in range(TPU):
                    for k in range(TOPK):
                        pool.indirect_dma_start(
                            xs_dram[half], bass.IndirectOffsetOnAxis(ap=S.idx[par][:, j * TOPK + k:j * TOPK + k + 1], axis=0),
                            S.stage[par][:, j, :], None).then_inc(S.s_sc[par], 16)
            first = half * HU // 2
            scatter(first * 2, 0, first)
            scatter(first * 2 + 1, 1, first)
            with pool.Fori(first + 1, first + HU // 2) as pair:
                scatter(pair * 2, 0, pair)
                scatter(pair * 2 + 1, 1, pair)
            for par in range(2):
                pool.wait_ge(S.s_sc[par], 16 * NL * (first + HU // 2))

        def load_stage(eng, u, par, pair, S):
            if not at(pair, 0):
                eng.wait_ge(S.s_sc[par], 16 * NL * pair)
            eng.dma_start(S.stage[par][:], unit_rows(xn2_dram, u)).then_inc(S.s_st[par], 16)

        NX = 4
        xg = [sb(f"xg{i}", [P, GT, DM]) for i in range(NX)]
        s_xg = [sem(f"s_xg{i}") for i in range(NX)]

        def slot_rows(dram, g):
            return dram[bass.ds(g * GT * P, GT * P), :].rearrange("(j p) d -> p j d", p=P)

        def load_group(eng, half, g, i):
            eng.dma_start(xg[i][:], slot_rows(xs_dram[half], g)).then_inc(s_xg[i], 16)

        sgw, suw, sdw = sb("sgw", [P, HS]), sb("suw", [P, HS]), sb("sdw", [P, HST, DM])
        s_sw = sem("s_sw")

        scattering = ExitStack()
        S = scatter_buffers(lambda name, shape, dt=F32: scattering.enter_context(nc.sbuf_tensor(name, shape, dt)),
                            lambda name: scattering.enter_context(nc.semaphore(name)))

        te_dram = nc.dram_tensor("te_scratch", (4 * P,), I32, kind="Internal").ap()
        with ExitStack() as r:
            def rsem(name):
                return r.enter_context(nc.semaphore(name))

            W = TILES * NE
            TC = -(-SLOT_TILES // P)

            def area(i, n=1):
                return ARENA[:, i * W:(i + n) * W]

            def by_tile(ap):
                return ap.rearrange("p (j e) -> p j e", e=NE)

            pick = [by_tile(area(k)) for k in range(TOPK)]
            oh = area(4)
            both = by_tile(area(5))
            tot = area(6)
            incl = area(7)
            scanm = area(8)
            pos = by_tile(area(9))

            def rsb(name, shape, dt=F32):
                return r.enter_context(nc.sbuf_tensor(name, shape, dt))

            from_on_sb, from_on16, ones16 = rsb("from_on_sb", [P, P]), rsb("from_on16", [P, P], BF16), rsb("ones16", [P, P], BF16)
            oh16 = rsb("oh16", [P, W], BF16)
            iei, ief = rsb("iei", [P, NE], I32), rsb("ief", [P, NE])
            i8f = rsb("i8f", [P, TILES, TOPK])
            cnti, cnts = rsb("cnti", [P, 2, NE], I32), rsb("cnts", [P, 2, NE], I32)
            ntf, nti, base = rsb("ntf", [P, 2, NE]), rsb("nti", [P, 2, NE]), rsb("base", [P, 2, NE])
            halves = rsb("halves", [P, 2, NE])
            gi, gf, late = rsb("gi", [P, TC], I32), rsb("gf", [P, TC]), rsb("late", [P, TC])
            cmp_ = rsb("cmp_", [P, TC, 2 * NE])
            tef, tei = rsb("tef", [P, TC]), rsb("tei", [P, TC], I32)
            idxf = rsb("idxf", [P, TILES, TOPK])
            PR = [r.enter_context(nc.psum_tensor(f"PR{i}", [P, W // 4], F32)) for i in range(4)]
            PT = [r.enter_context(nc.psum_tensor(f"PT{i}", [P, W // 4], F32)) for i in range(4)]

            s_c = rsem("s_c")
            s_iota = rsem("s_iota")
            s_v = rsem("s_v")
            s_oh, s_pr, s_pt = rsem("s_oh"), rsem("s_pr"), rsem("s_pt")
            s_p01, s_sm = rsem("s_p01"), rsem("s_sm")
            s_ps, s_pm = rsem("s_ps"), rsem("s_pm")
            s_tc, s_te, s_teo = rsem("s_tc"), rsem("s_te"), rsem("s_teo")
            block = r.enter_context(nc.Block())

            @block.sync
            def _(sp):
                sp.dma_start(from_on_sb[:], from_on).then_inc(s_c, 16)
                for u in range(2):
                    load_stage(sp, u, u, 0, S)
                for dst, src in ((sgw[:], sgateT), (suw[:], supT), (sdw[:], sdownT.rearrange("(m p) d -> p m d", p=P))):
                    sp.dma_start(dst, src).then_inc(s_sw, 16)
                sp.wait_ge(s_te, 1)
                with nc.allow_non_contiguous_dma(reason="a few hundred integers"):
                    sp.dma_start(te_dram[0:TC * P].rearrange("(c p) -> p c", p=P), tei[:]).then_inc(s_teo, 16)
                sp.wait_ge(s_teo, 16)

            @block.gpsimd
            def _(pool):
                pool.iota(iei[:], pattern=[[1, NE]], base=0, channel_multiplier=0).then_inc(s_iota, 1)
                pool.iota(gi[:], pattern=[[P, TC]], base=0, channel_multiplier=1).then_inc(s_iota, 1)
                pool.memset(scanm, 1.0).then_inc(s_sm, 1)
                pool.wait_ge(s_v, 3)
                pool.tensor_tensor(by_tile(oh), pick[0], pick[1], ALU.add).then_inc(s_p01, 1)
                pool.wait_ge(s_ps, 4)
                for k in (3, 2):
                    pool.tensor_tensor(pick[k], pick[k], pos, ALU.mult).then_inc(s_pm, 1)

            @block.tensor
            def _(pe):
                pe.wait_ge(s_oh, 1)
                for i in range(4):
                    pe.matmul(PT[i][:], ones16[:], oh16[:, i * (W // 4):(i + 1) * (W // 4)],
                              start=True, stop=True).then_inc(s_pt, 1)
                for i in range(4):
                    pe.matmul(PR[i][:], from_on16[:], oh16[:, i * (W // 4):(i + 1) * (W // 4)],
                              start=True, stop=True).then_inc(s_pr, 1)

            @block.scalar
            def _(act):
                for i in range(4):
                    act.wait_ge(s_pt, i + 1)
                    act.activation(tot.rearrange("p (e j) -> p j e", j=TILES)[:, i * TILES // 4:(i + 1) * TILES // 4, :],
                                   PT[i][:].rearrange("p (j e) -> p j e", e=NE), ACT.Copy).then_inc(s_tc, 1)

            @block.vector
            def _(dve):
                steps = [0]

                def step(ins):
                    steps[0] += 1
                    ins.then_inc(s_v, 1)
                    dve.wait_ge(s_v, steps[0])

                dve.wait_ge(s_iota, 2)
                dve.tensor_copy(i8f[:], I8[:, :, 0:TOPK])
                dve.tensor_copy(gf[:], gi[:])
                dve.memset(ones16[:], 1.0)
                dve.wait_ge(s_c, 16)
                dve.tensor_copy(from_on16[:], from_on_sb[:])
                step(dve.tensor_copy(ief[:], iei[:]))
                for k in range(TOPK):
                    step(dve.tensor_tensor(pick[k], ief[:].unsqueeze(1).to_broadcast([P, TILES, NE]),
                                           i8f[:, :, k:k + 1].to_broadcast([P, TILES, NE]), ALU.is_equal))
                step(dve.tensor_tensor(both, pick[2], pick[3], ALU.add))
                dve.wait_ge(s_p01, 1)
                dve.tensor_tensor(by_tile(oh16[:]), by_tile(oh), both, ALU.add).then_inc(s_oh, 1)
                dve.wait_ge(s_sm, 1)
                step(dve.memset(scanm.rearrange("p (e j) -> p e j", j=TILES // 2)[:, :, 0:1], 0.0))
                step(dve.memset(halves[:], 1.0))
                step(dve.memset(halves[:, 1, 0:1], 0.0))
                dve.wait_ge(s_tc, 4)
                step(dve.tensor_tensor_scan(incl, scanm, tot, 0.0, ALU.mult, ALU.add))
                step(dve.tensor_scalar(cnti[:], incl.rearrange("p (e q j) -> p q e j", q=2, j=TILES // 2)[:, :, :, TILES // 2 - 1],
                                       float(P - 1), None, ALU.add))
                step(dve.tensor_scalar(cnts[:], cnti[:], 7, None, ALU.arith_shift_right))
                step(dve.tensor_copy(ntf[:], cnts[:]))
                step(dve.tensor_tensor_scan(nti[:].rearrange("p q e -> p (q e)"), halves[:].rearrange("p q e -> p (q e)"),
                                            ntf[:].rearrange("p q e -> p (q e)"), 0.0, ALU.mult, ALU.add))
                step(dve.tensor_tensor(base[:], nti[:], ntf[:], ALU.subtract))
                step(dve.tensor_scalar(base[:], base[:], float(P), None, ALU.mult))
                step(dve.tensor_scalar(nti[:, 1, :], nti[:, 1, :], float(HALF_TILES), None, ALU.add))
                step(dve.tensor_tensor(cmp_[:], nti[:].rearrange("p q e -> p (q e)").unsqueeze(1).to_broadcast([P, TC, 2 * NE]),
                                       gf[:].unsqueeze(2).to_broadcast([P, TC, 2 * NE]), ALU.is_le))
                step(dve.tensor_scalar(late[:], gf[:], float(HALF_TILES), float(NE), ALU.is_ge, ALU.mult))
                step(dve.tensor_reduce(tef[:], cmp_[:], AX.X, ALU.add))
                step(dve.tensor_tensor(tef[:], tef[:], late[:], ALU.subtract))
                dve.tensor_scalar(tei[:], tef[:], float(NE - 1), None, ALU.min).then_inc(s_te, 1)
                for q in range(2):
                    mine = slice(q * TILES // 2, (q + 1) * TILES // 2)
                    step(dve.tensor_tensor(pos[:, mine, :], incl.rearrange("p (e j) -> p j e", j=TILES)[:, mine, :],
                                           base[:, q:q + 1, :].to_broadcast([P, TILES // 2, NE]), ALU.add))
                for i in range(4):
                    part = pos[:, i * TILES // 4:(i + 1) * TILES // 4, :]
                    dve.wait_ge(s_pr, i + 1)
                    dve.tensor_tensor(part, part, PR[i][:].rearrange("p (j e) -> p j e", e=NE), ALU.add).then_inc(s_ps, 1)
                dve.wait_ge(s_ps, 4)
                for k in (0, 1, 3, 2):
                    if k < 2:
                        step(dve.tensor_tensor(pick[k], pick[k], pos, ALU.mult))
                    else:
                        dve.wait_ge(s_pm, TOPK - k)
                    step(dve.tensor_reduce(idxf[:, :, k], pick[k], AX.X, ALU.add))
                step(dve.tensor_copy(IDX[:], idxf[:].rearrange("p j k -> p (j k)")))

        WGU = ARENA[:, 0:NE * 2 * P].rearrange("p (e c) -> p e c", e=NE)
        WD = ARENA[:, NE * 2 * P:NE * 3 * P].rearrange("p (e c) -> p e c", e=NE)
        SH = ARENA[:, NE * 3 * P:NE * 3 * P + TILES * DM].rearrange("p (j d) -> p j d", d=DM)
        SHARED_LATE = 2

        def gather_half(pool, half, F):
            def gather(u, par, pair):
                if not at(pair, 0):
                    pool.wait_ge(F.s_g[par], 16 * NL * pair)
                pause(pool, scratch, 8)
                pool.tensor_copy(F.gidx[par][:], IDX[:, bass.ds(u * NL, NL)]).then_inc(F.s_gi, 1)
                pool.wait_ge(F.s_gi, u + 1)
                if not at(pair, 0):
                    pool.wait_ge(F.s_acc, (u - 1) * TOPK)
                pause(pool, scratch, 9)
                for j in range(TPU):
                    for k in range(TOPK):
                        pool.indirect_dma_start(
                            F.rows[par][:, j, k, :], None, ys_dram[half],
                            bass.IndirectOffsetOnAxis(ap=F.gidx[par][:, j * TOPK + k:j * TOPK + k + 1], axis=0)
                        ).then_inc(F.s_g[par], 16)
            first = half * HU // 2
            gather(first * 2, 0, first)
            gather(first * 2 + 1, 1, first)
            with pool.Fori(first + 1, first + HU // 2) as pair:
                gather(pair * 2, 0, pair)
                gather(pair * 2 + 1, 1, pair)

        s_ew = sem("s_ew")
        s_xT = [sem(f"s_xT{i}") for i in range(2)]
        s_pg, s_pu, s_gs, s_hs = sem("s_pg"), sem("s_pu"), sem("s_gs"), sem("s_hs")
        s_pd2, s_sh = sem("s_pd2"), sem("s_sh")
        s_wt, s_ex = sem("s_wt"), sem("s_ex")

        def end_stage(half, S, F):
            first, end = (0, UNITS - SHARED_LATE) if half == 0 else (UNITS - SHARED_LATE, UNITS)
            with ExitStack() as r:
                def rsb(name, shape, dt=F32):
                    return r.enter_context(nc.sbuf_tensor(f"{name}_e{half}", shape, dt))

                xT = [rsb(f"xT{i}", [P, UT]) for i in range(2)]
                gs = rsb("gs", [P, 2, UT])
                hsb = rsb("hsb", [P, 2, HST, UT])
                PG = [r.enter_context(nc.psum_tensor(f"PG{i}_e{half}", [P, UT], F32)) for i in range(2)]
                PU = [r.enter_context(nc.psum_tensor(f"PU{i}_e{half}", [P, UT], F32)) for i in range(2)]
                PD = [r.enter_context(nc.psum_tensor(f"PD{i}_e{half}", [P, UT], F32)) for i in range(2)]
                if half == 0:
                    ssum, srec = rsb("ssum", [P, TILES]), rsb("srec", [P, TILES])
                    v4 = rsb("v4", [P, TILES, TOPK])
                    wsum, wrec = rsb("wsum", [P, TILES]), rsb("wrec", [P, TILES])
                block = r.enter_context(nc.Block())

                @block.sync
                def _(sp):
                    if half == 0:
                        with sp.Fori(1, HU // 2) as pair:
                            load_stage(sp, pair * 2, 0, pair, S)
                            load_stage(sp, pair * 2 + 1, 1, pair, S)
                        for par in range(2):
                            sp.wait_ge(S.s_sc[par], 16 * NL * (HU // 2))
                        for i in range(NX):
                            load_group(sp, 0, i, i)
                        sp.wait_ge(s_ew, 32)
                    else:
                        store_all(sp, F)

                @block.gpsimd
                def _(pool):
                    if half == 0:
                        scatter_half(pool, 0, S)
                    else:
                        gather_half(pool, 1, F)

                @block.tensor
                def _(pe):
                    pe.wait_ge(s_sw, 48)

                    def hidden(v, par, pair, back):
                        pe.wait_ge(s_xT[par], 16 * (pair + 1))
                        for mm in range(HST):
                            n = v * HST + mm
                            if back or mm >= 2:
                                pe.wait_ge(s_hs, n - 1)
                            pe.matmul(PG[mm % 2][:], sgw[:, mm * P:(mm + 1) * P], xT[par][:],
                                      start=True, stop=True).then_inc(s_pg, 1)
                            pe.matmul(PU[mm % 2][:], suw[:, mm * P:(mm + 1) * P], xT[par][:],
                                      start=True, stop=True).then_inc(s_pu, 1)

                    def down(v, par, back):
                        pe.wait_ge(s_hs, HST * (v + 1))
                        if back:
                            pe.wait_ge(s_sh, v - 1)
                        for j in range(TPU):
                            for mm in range(HST):
                                t = pe.matmul(PD[par][:, j * P:(j + 1) * P], hsb[:, par, mm, j * P:(j + 1) * P], sdw[:, mm, :],
                                              start=mm == 0, stop=mm == HST - 1)
                        t.then_inc(s_pd2, 1)
                    hidden(first, 0, first // 2, half == 1)
                    hidden(first + 1, 1, first // 2, True)
                    down(first, 0, half == 1)
                    if half == 0:
                        hidden(2, 0, 1, True)
                        down(1, 1, False)
                        hidden(3, 1, 1, True)
                        down(2, 0, True)
                        with pe.Fori(2, end // 2) as pair:
                            hidden(pair * 2, 0, pair, True)
                            down(pair * 2 - 1, 1, True)
                            hidden(pair * 2 + 1, 1, pair, True)
                            down(pair * 2, 0, True)
                    down(end - 1, 1, True)

                @block.scalar
                def _(act):
                    def load(v, par):
                        act.dma_start(xT[par][:], xn2T_dram[bass.ds(v * P, P), :]).then_inc(s_xT[par], 16)

                    def output(v, par):
                        act.wait_ge(s_pd2, v + 1)
                        act.activation(SH[:, bass.ds(v * TPU, TPU), :],
                                       PD[par][:].rearrange("p (j d) -> p j d", d=DM), ACT.Copy).then_inc(s_sh, 1)

                    def unit(v, par, back, more):
                        for mm in range(HST):
                            n = v * HST + mm
                            act.wait_ge(s_pg, n + 1)
                            if mm == 0 and back and more:
                                load(v + 1, 1 - par)
                            if back or mm >= 2:
                                act.wait_ge(s_hs, n - 1)
                            act.activation(gs[:, mm % 2, :], PG[mm % 2][:], ACT.Silu).then_inc(s_gs, 1)
                        if back:
                            output(v - 1, 1 - par)
                    load(first, 0)
                    load(first + 1, 1)
                    if half == 0:
                        act.dma_start(WGU, gate_upT).then_inc(s_ew, 16)
                        act.dma_start(WD, downT).then_inc(s_ew, 16)
                        act.wait_ge(s_wt, 2)
                        act.activation(LG[:], LG[:], ACT.Exp).then_inc(s_ex, 1)
                        act.activation(v4[:], v4[:], ACT.Exp).then_inc(s_ex, 1)
                    else:
                        finish_rstd(act, 0, HU, 1, F)
                    unit(first, 0, False, False)
                    if half == 0:
                        unit(1, 1, True, True)
                        with act.Fori(1, end // 2 - 1) as pair:
                            unit(pair * 2, 0, True, True)
                            unit(pair * 2 + 1, 1, True, True)
                        unit(end - 2, 0, True, True)
                    unit(end - 1, 1, True, False)
                    output(end - 1, 1)
                    if half == 1:
                        act.preload_act_table_set(EXP_LN)
                        with act.Fori(0, HU) as i:
                            finish_rstd(act, HU + i, 1, i + 2, F)

                @block.vector
                def _(dve):
                    def unit(v, par, back):
                        if back:
                            dve.wait_ge(s_pd2, v - 1)
                        for mm in range(HST):
                            n = v * HST + mm
                            dve.wait_ge(s_gs, n + 1)
                            dve.wait_ge(s_pu, n + 1)
                            dve.tensor_tensor(hsb[:, par, mm, :], gs[:, mm % 2, :], PU[mm % 2][:],
                                              ALU.mult).then_inc(s_hs, 1)

                    def finish(u, par, pair):
                        for k in range(TOPK):
                            finish_add(dve, u, par, pair, k, F)
                        finish_moments(dve, u, F)
                    if half == 1:
                        finish(HU - 1, 1, HU // 2 - 1)
                    else:
                        dve.tensor_tensor(v4[:], V8[:, :, 0:TOPK], V8[:, :, 0:1].to_broadcast([P, TILES, TOPK]),
                                          ALU.subtract).then_inc(s_wt, 1)
                        dve.tensor_tensor(LG[:], LG[:], V8[:, :, 0:1].to_broadcast([P, TILES, NE]),
                                          ALU.subtract).then_inc(s_wt, 1)
                    unit(first, 0, False)
                    unit(first + 1, 1, False)
                    if half == 0:
                        with dve.Fori(1, end // 2) as pair:
                            unit(pair * 2, 0, True)
                            unit(pair * 2 + 1, 1, True)
                    if half == 0:
                        dve.wait_ge(s_ex, 2)
                        dve.tensor_reduce(ssum[:], LG[:], AX.X, ALU.add).then_inc(s_wt, 1)
                        dve.wait_ge(s_wt, 3)
                        dve.reciprocal(srec[:], ssum[:]).then_inc(s_wt, 1)
                        dve.wait_ge(s_wt, 4)
                        dve.tensor_tensor(v4[:], v4[:], srec[:].unsqueeze(2).to_broadcast([P, TILES, TOPK]),
                                          ALU.mult).then_inc(s_wt, 1)
                        dve.wait_ge(s_wt, 5)
                        dve.tensor_reduce(wsum[:], v4[:], AX.X, ALU.add).then_inc(s_wt, 1)
                        dve.wait_ge(s_wt, 6)
                        dve.tensor_scalar(wsum[:], wsum[:], 1e-12, None, ALU.max).then_inc(s_wt, 1)
                        dve.wait_ge(s_wt, 7)
                        dve.reciprocal(wrec[:], wsum[:]).then_inc(s_wt, 1)
                        dve.wait_ge(s_wt, 8)
                        dve.tensor_tensor(WT[:], v4[:], wrec[:].unsqueeze(2).to_broadcast([P, TILES, TOPK]), ALU.mult)
                    else:
                        dve.wait_ge(s_sh, UNITS)

                        def both(i, par, pair):
                            finish_norm(dve, i, i, 0, F)
                            finish(HU + i, par, pair + HU // 2)
                            finish_norm(dve, HU + i, i, 1, F)
                        both(0, 0, 0)
                        both(1, 1, 0)
                        with dve.Fori(1, HU // 2) as pair:
                            both(pair * 2, 0, pair)
                            both(pair * 2 + 1, 1, pair)

        def finish_buffers(rsb, rsem):
            F = Move()
            F.gidx = [rsb(f"gidx{i}", [P, NL], U32) for i in range(2)]
            F.rows = [rsb(f"rows{i}", [P, TPU, TOPK, DM]) for i in range(2)]
            F.st, F.mv = rsb("fst", [P, TPU, 6]), rsb("fmv", [P, TPU, 2])
            F.w = rsb("fw", [P, TPU, TOPK])
            F.moments = rsb("fmoments", [P, TILES, 2])
            F.ln, F.rstd = rsb("fln", [P, TILES]), rsb("frstd", [P, TILES])
            F.mean1, F.rstd1 = rsb("fmean1", [P, TPU]), rsb("frstd1", [P, TPU])
            F.out = [rsb(f"fo{i}", [P, TPU, DM]) for i in range(2)]
            F.s_gi, F.s_fw, F.s_acc = rsem("s_gi"), rsem("s_fw"), rsem("s_acc")
            F.s_g = [rsem(f"s_g{i}") for i in range(2)]
            F.s_st, F.s_mv, F.s_kept = rsem("s_fst"), rsem("s_fmv"), rsem("s_kept")
            F.s_ln, F.s_rs, F.s_one, F.s_n, F.s_fo = (rsem(n) for n in ("s_fln", "s_frs", "s_one", "s_fn", "s_fo"))
            F.s_out = [rsem(f"s_out{i}") for i in range(2)]
            return F

        def finish_add(dve, u, par, pair, k, F):
            if k == 0:
                if not at(u, 0):
                    dve.wait_ge(F.s_acc, u * TOPK)
                dve.tensor_copy(F.w[:], WT[:, bass.ds(u * TPU, TPU), :]).then_inc(F.s_fw, 1)
                dve.wait_ge(F.s_fw, u + 1)
                dve.wait_ge(F.s_g[par], 16 * NL * (pair + 1))
            else:
                dve.wait_ge(F.s_acc, u * TOPK + k)
            for j in range(TPU):
                total = SH[:, bass.ds(u * TPU + j, 1), :].rearrange("p j d -> p (j d)")
                t = dve.scalar_tensor_tensor(out=total, in0=F.rows[par][:, j, k, :], scalar=F.w[:, j, k:k + 1],
                                             in1=total, op0=ALU.mult, op1=ALU.add)
            t.then_inc(F.s_acc, 1)

        def finish_moments(dve, u, F):
            dve.wait_ge(F.s_acc, u * TOPK + TOPK)
            pause(dve, scratch, 10)
            for j in range(TPU):
                t = dve.bn_stats(F.st[:, j, :], SH[:, bass.ds(u * TPU + j, 1), :].rearrange("p j d -> p (j d)"))
            t.then_inc(F.s_st, 1)
            dve.wait_ge(F.s_st, u + 1)
            pause(dve, scratch, 11)
            for j in range(TPU):
                t = dve.bn_aggr(F.mv[:, j, :], F.st[:, j, :])
            t.then_inc(F.s_mv, 1)
            dve.wait_ge(F.s_mv, u + 1)
            pause(dve, scratch, 12)
            dve.tensor_copy(F.moments[:, bass.ds(u * TPU, TPU), :], F.mv[:]).then_inc(F.s_kept, 1)

        def finish_rstd(act, first, units, done, F):
            tiles = bass.ds(first * TPU, units * TPU)
            act.wait_ge(F.s_kept, first + units)
            act.activation(F.ln[:, tiles], F.moments[:, tiles, 1], ACT.Ln, bias=eps[:]).then_inc(F.s_ln, 1)
            act.wait_ge(F.s_ln, done)
            act.activation(F.rstd[:, tiles], F.ln[:, tiles], ACT.Exp, scale=-0.5).then_inc(F.s_rs, 1)

        def finish_norm(dve, u, i, late, F):
            n = 2 * i + late
            dve.wait_ge(F.s_rs, i + 2 if late else 1)
            if not (at(i, 0) and not late):
                dve.wait_ge(F.s_n, n)
            pause(dve, scratch, 13)
            dve.tensor_copy(F.mean1[:], F.moments[:, bass.ds(u * TPU, TPU), 0])
            dve.tensor_copy(F.rstd1[:], F.rstd[:, bass.ds(u * TPU, TPU)]).then_inc(F.s_one, 1)
            dve.wait_ge(F.s_one, n + 1)
            if not at(i, 0):
                dve.wait_ge(F.s_out[late], 16 * i)
            for j in range(TPU):
                t = dve.tensor_scalar(F.out[late][:, j, :], SH[:, bass.ds(u * TPU + j, 1), :].rearrange("p j d -> p (j d)"),
                                      F.mean1[:, j:j + 1], F.rstd1[:, j:j + 1], ALU.subtract, ALU.mult)
            t.then_inc(F.s_n, 1)
            dve.wait_ge(F.s_n, n + 1)
            dve.tensor_tensor(F.out[late][:], F.out[late][:], X2[:, bass.ds(u * TPU, TPU), :], ALU.add).then_inc(F.s_fo, 1)

        def store_all(eng, F):
            with eng.Fori(0, HU) as i:
                for late in range(2):
                    eng.wait_ge(F.s_fo, i * 2 + late + 1)
                    eng.dma_start(unit_rows(out, i + late * HU), F.out[late][:]).then_inc(F.s_out[late], 16)
            for late in range(2):
                eng.wait_ge(F.s_out[late], 16 * HU)

        def middle_stage(half, S, F):
            with ExitStack() as r:
                def rsb(name, shape, dt=F32):
                    return r.enter_context(nc.sbuf_tensor(f"{name}_m{half}", shape, dt))

                def rsem(name):
                    return r.enter_context(nc.semaphore(f"{name}_m{half}"))

                TL = 8
                SPU = HG // HU
                xgT = [rsb(f"xgT{i}", [P, GT * P]) for i in range(2)]
                sg = [rsb(f"sg{i}", [P, GT, P]) for i in range(2)]
                hg = [rsb(f"hg{i}", [P, GT, P]) for i in range(2)]
                hgT = [rsb(f"hgT{i}", [P, GT * P]) for i in range(2)]
                yo = [rsb(f"yo{i}", [P, GT, DM]) for i in range(2)]
                PXT = r.enter_context(nc.psum_tensor(f"PXT_m{half}", [P, GT * P], F32))
                PHT = r.enter_context(nc.psum_tensor(f"PHT_m{half}", [P, GT * P], F32))
                PGU = [r.enter_context(nc.psum_tensor(f"PGU{i}_m{half}", [P, 2, 2, P], F32)) for i in range(4)]
                PY = [r.enter_context(nc.psum_tensor(f"PY{i}_m{half}", [P, GT * DM], F32)) for i in range(2)]
                s_xt, s_xtc = rsem("s_xt"), rsem("s_xtc")
                s_gu, s_sg, s_hg = rsem("s_gu"), rsem("s_sg"), rsem("s_hg")
                s_ht, s_htc, s_y, s_yo = rsem("s_ht"), rsem("s_htc"), rsem("s_y"), rsem("s_yo")
                s_ys = [rsem(f"s_ys{i}") for i in range(2)]
                block = r.enter_context(nc.Block())

                @block.sync
                def _(sp):
                    def load(g, i):
                        sp.wait_ge(s_xt, g - NX + 1)
                        load_group(sp, half, g, i)

                    def store(g, par):
                        sp.wait_ge(s_yo, g + 1)
                        sp.dma_start(slot_rows(ys_dram[half], g), yo[par][:]).then_inc(s_ys[par], 16)
                    for g in range(NX):
                        load(NX + g, g)
                        if g >= 2:
                            store(g - 2, g % 2)
                    with sp.Fori(1, HG // NX - 1) as turn:
                        for i in range(NX):
                            load(turn * NX + NX + i, i)
                            store(turn * NX + i - 2, i % 2)
                    for g in range(HG - NX - 2, HG - 2):
                        store(g, g % 2)
                    if half == 0:
                        for par in range(2):
                            sp.wait_ge(S.s_sc[par], 16 * NL * HU)
                        for i in range(NX):
                            sp.wait_ge(s_xt, HG - NX + i + 1)
                            load_group(sp, 1, i, i)
                    for g in range(HG - 2, HG):
                        store(g, g % 2)
                    for par in range(2):
                        sp.wait_ge(s_ys[par], 16 * (HG // 2))

                @block.gpsimd
                def _(pool):
                    if half == 0:
                        scatter_half(pool, 1, S)
                    else:
                        gather_half(pool, 0, F)

                @block.tensor
                def _(pe):
                    def experts(at_group, n):
                        return nc.values_load_multi_w_load_instructions(
                            te_dram[bass.ds(at_group * GT + half * HALF_TILES, n)].unsqueeze(0),
                            engines=[mybir.EngineType.PE], min_val=0,
                            max_val=NE - 1, skip_runtime_bounds_check_because="it is a minimum with NE - 1")[1]

                    def tokens_T(g, i, loads):
                        pe.wait_ge(s_xg[i], 16 * (loads + half * (HG // NX)))
                        if not at(g, 0):
                            pe.wait_ge(s_xtc, g)
                        for j in range(GT):
                            t = pe.transpose(PXT[:, j * P:(j + 1) * P], xg[i][:, j, :], idf[:])
                        t.then_inc(s_xt, 1)

                    def gate_up(g, par, es, back):
                        pe.wait_ge(s_xtc, g + 1)
                        if back:
                            pe.wait_ge(s_hg, 2 * g - 2)
                        for j in range(GT):
                            t = pe.matmul(PGU[2 * par + j // 2][:, j % 2, :, :].rearrange("p a c -> p (a c)"),
                                          xgT[par][:, j * P:(j + 1) * P],
                                          WGU[:, bass.ds(es[j], 1), :].rearrange("p e c -> p (e c)"),
                                          start=True, stop=True)
                            if j % 2:
                                t.then_inc(s_gu, 1)

                    def hidden_T(g, par):
                        pe.wait_ge(s_hg, 2 * g + 2)
                        if not at(g, 0):
                            pe.wait_ge(s_htc, g)
                        for j in range(GT):
                            t = pe.transpose(PHT[:, j * P:(j + 1) * P], hg[par][:, j, :], idf[:])
                        t.then_inc(s_ht, 1)

                    def down(g, par, es, back):
                        pe.wait_ge(s_htc, g + 1)
                        if back:
                            pe.wait_ge(s_yo, g - 1)
                        for j in range(GT):
                            t = pe.matmul(PY[par][:, j * DM:(j + 1) * DM], hgT[par][:, j * P:(j + 1) * P],
                                          WD[:, bass.ds(es[j], 1), :].rearrange("p e c -> p (e c)"),
                                          start=True, stop=True)
                        t.then_inc(s_y, 1)

                    def body(g, par, i, turn, es, peeled, more):
                        gate_up(g, par, es[2 * GT:3 * GT], not peeled or g >= 2)
                        if more:
                            tokens_T(g + 1, (i + 1) % NX, turn * (TL // NX) + (i + 1) // NX + 1)
                        if not peeled or g >= 1:
                            hidden_T(g - 1, 1 - par)
                        if not peeled or g >= 2:
                            down(g - 2, par, es[0:GT], not peeled or g >= 4)

                    def turn_of_groups(turn, last):
                        es = list(experts(turn * TL - 2, 2 * GT)) + list(experts(turn * TL, TL * GT))
                        for i in range(TL):
                            body(turn * TL + i, i % 2, i, turn, es[i * GT:], False, not last or i < TL - 1)
                        return es

                    tokens_T(0, 0, 1)
                    es = [None] * (2 * GT) + list(experts(0, TL * GT))
                    for g in range(TL):
                        body(g, g % 2, g, 0, es[g * GT:], True, True)
                    with pe.Fori(1, HG // TL - 1) as turn:
                        turn_of_groups(turn, False)
                    es = turn_of_groups(HG // TL - 1, True)
                    hidden_T(HG - 1, 1)
                    down(HG - 2, 0, es[TL * GT:], True)
                    down(HG - 1, 1, es[(TL + 1) * GT:], True)

                @block.scalar
                def _(act):
                    def tokens(g, par):
                        act.wait_ge(s_xt, g + 1)
                        if not (at(g, 0) or at(g, 1)):
                            act.wait_ge(s_gu, 2 * g - 2)
                        act.activation(xgT[par][:], PXT[:], ACT.Copy).then_inc(s_xtc, 1)

                    def gates(g, par):
                        for q in range(2):
                            act.wait_ge(s_gu, 2 * g + q + 1)
                            if not (at(g, 0) or at(g, 1)):
                                act.wait_ge(s_hg, 2 * g - 3 + q)
                            act.activation(sg[par][:, 2 * q:2 * q + 2, :], PGU[2 * par + q][:, :, 0, :],
                                           ACT.Silu).then_inc(s_sg, 1)

                    def hidden_T(g, par):
                        act.wait_ge(s_ht, g + 1)
                        if not (at(g, 0) or at(g, 1)):
                            act.wait_ge(s_y, g - 1)
                        act.activation(hgT[par][:], PHT[:], ACT.Copy).then_inc(s_htc, 1)

                    def step(t, par, pair):
                        for i in range(SPU):
                            g, p = t * SPU + i, (par * SPU + i) % 2
                            gates(g, p)
                            if not (at(t, HU - 1) and i == SPU - 1):
                                tokens(g + 1, 1 - p)
                            if not at(g, 0):
                                hidden_T(g - 1, 1 - p)
                            if half == 0 and pair is not None and not at(t, HU - 1) and i == 1:
                                load_stage(act, HU + t + 1, 1 - par, HU // 2 + pair + 1, S)
                    if half == 0:
                        load_stage(act, HU, 0, HU // 2, S)
                        load_stage(act, HU + 1, 1, HU // 2, S)
                    tokens(0, 0)
                    step(0, 0, None)
                    step(1, 1, 0)
                    step(2, 0, 0)
                    with act.Fori(1, HU // 2 - 1) as pair:
                        step(pair * 2 + 1, 1, pair)
                        step(pair * 2 + 2, 0, pair)
                    step(HU - 1, 1, HU // 2 - 1)
                    hidden_T(HG - 1, 1)

                @block.vector
                def _(dve):
                    def hidden(g, par):
                        if not (at(g, 0) or at(g, 1)):
                            dve.wait_ge(s_ht, g - 1)
                        for q in range(2):
                            dve.wait_ge(s_sg, 2 * g + q + 1)
                            dve.tensor_tensor(hg[par][:, 2 * q:2 * q + 2, :], sg[par][:, 2 * q:2 * q + 2, :],
                                              PGU[2 * par + q][:, :, 1, :], ALU.mult).then_inc(s_hg, 1)

                    def output(g, par):
                        dve.wait_ge(s_y, g + 1)
                        if not (at(g, 0) or at(g, 1)):
                            dve.wait_ge(s_ys[par], 8 * (g - par))
                        dve.tensor_copy(yo[par][:].rearrange("p j d -> p (j d)"), PY[par][:]).then_inc(s_yo, 1)

                    def step(t, par, pair):
                        finish = half == 1 and pair is not None
                        for i in range(SPU):
                            g, p = t * SPU + i, (par * SPU + i) % 2
                            if not (at(t, HU - 1) and i == SPU - 1):
                                hidden(g + 1, 1 - p)
                            if finish and i < TOPK:
                                finish_add(dve, t - 1, 1 - par, pair, i, F)
                            if finish and i == TOPK - 1:
                                finish_moments(dve, t - 1, F)
                            if not at(g, 0):
                                output(g - 1, 1 - p)
                    hidden(0, 0)
                    step(0, 0, None)
                    step(1, 1, 0)
                    step(2, 0, 0)
                    with dve.Fori(1, HU // 2 - 1) as pair:
                        step(pair * 2 + 1, 1, pair)
                        step(pair * 2 + 2, 0, pair)
                    step(HU - 1, 1, HU // 2 - 1)
                    output(HG - 1, 1)

        end_stage(0, S, None)
        middle_stage(0, S, None)
        scattering.close()
        with ExitStack() as f:
            F = finish_buffers(lambda name, shape, dt=F32: f.enter_context(nc.sbuf_tensor(name, shape, dt)),
                               lambda name: f.enter_context(nc.semaphore(name)))
            middle_stage(1, None, F)
            end_stage(1, None, F)


def kernel(**inputs):
    import concourse.bacc as _bacc
    from concourse.bass_utils import run_bass_kernel_spmd as _run

    a = {k.removeprefix("L0_attn_").removeprefix("L0_ffn_"): np.asarray(v) for k, v in inputs.items()}
    layout = {
        "x": a["x"].reshape(TOK, DM),
        "W_inT": a["W_in"].T,
        "w_convT": a["w_conv"].T,
        "b_conv": a["b_conv"].reshape(NH, P).T,
        "W_x": a["W_x"],
        "W_xT": a["W_x"].T,
        "W_dtT": a["W_dt"].T,
        "b_dt": a["b_dt"].reshape(NH, P).T,
        "A_log": a["A_log"],
        "Dv": a["D"].reshape(NH, P).T,
        "W_outT": a["W_out"].T,
        "routerT": a["router_w"].T,
        "router_bias": a["router_bias"],
        "gate_upT": np.stack([a["gate_w"], a["up_w"]], 1).transpose(3, 0, 1, 2).reshape(DM, NE, 2 * P),
        "downT": a["down_w"].transpose(2, 0, 1),
        "sgateT": a["sgate_w"].T,
        "supT": a["sup_w"].T,
        "sdownT": a["sdown_w"].T,
        "sel": np.repeat(np.tile(np.eye(2 * NS, dtype=np.float32), (3, 1)), P, axis=1),
        "ident": np.eye(P, dtype=np.float32),
        "from_on": -np.tril(np.ones((P, P), np.float32)),
    }
    nc = _bacc.Bacc("TRN2", target_bir_lowering=False, num_devices=1)
    arrays, args = {}, []
    for name, v in layout.items():
        v = np.ascontiguousarray(v)
        arrays[f"in_{name}"] = v
        args.append(nc.dram_tensor(f"in_{name}", v.shape, mybir.dt.from_np(v.dtype), kind="ExternalInput").ap())
    args.append(nc.dram_tensor("out_0", (TOK, DM), F32, kind="ExternalOutput").ap())
    mamba_moe_kernel(nc, *args)
    r = _run(nc, [arrays], core_ids=[0])
    return r.results[0]["out_0"].reshape(BATCH, SEQ, DM)
```
